# Optimizing a Trainium2 kernel written in Bass

```python
import numpy as np
import jax
import jax.numpy as jnp

def _softmax(x, axis=-1):
    return jax.nn.softmax(x, axis=axis)

def _gelu(x):
    return jax.nn.gelu(x, approximate=True)

def _silu(x):
    return jax.nn.silu(x)

def _sigmoid(x):
    return jax.nn.sigmoid(x)

def _layernorm(x, axis=-1, eps=1e-05):
    m = jnp.mean(x, axis=axis, keepdims=True)
    v = jnp.var(x, axis=axis, keepdims=True)
    return (x - m) / jnp.sqrt(v + eps)

def _scatter_add(tgt, idx, src, axis=0):
    return tgt.at[idx].add(src)

def _segment_sum(src, seg, n):
    return jax.ops.segment_sum(src, seg, n)
kernel_name = 'mk_seq_postln_d2_jaxref_r4_91d23d'

def setup_inputs(seed: int=0):
    np.random.seed(seed)
    _w = jnp.asarray

    def _L0_attn_setup():
        import jax, jax.numpy as jnp
        import numpy as np
        D_MODEL = 256
        D_INNER = 512
        N_STATES = 16
        DT_RANK = 64
        K = 4
        B_SZ = 2
        L = 512

        def _causal_conv(x, w):
            xt = jnp.transpose(x, (0, 2, 1))
            y = jax.lax.conv_general_dilated(xt, w, window_strides=(1,), padding=[(K - 1, 0)], feature_group_count=D_INNER, dimension_numbers=('NCH', 'OIH', 'NCH'))
            return jnp.transpose(y, (0, 2, 1))

        def _selective_scan(delta, A, Bmat, C, x):
            dA = jnp.exp(delta[..., None] * A[None, None])
            dBx = (delta * x)[..., None] * Bmat[:, :, None, :]

            def step(h, inputs):
                dA_t, dBx_t = inputs
                h = dA_t * h + dBx_t
                y = jnp.einsum('bdn,dn->bd', h, C)
                return (h, y)
            h0 = jnp.zeros((x.shape[0], D_INNER, N_STATES), x.dtype)
            _, ys = jax.lax.scan(step, h0, (jnp.moveaxis(dA, 1, 0), jnp.moveaxis(dBx, 1, 0)))
            return jnp.moveaxis(ys, 0, 1)
        key = jax.random.key(seed)
        ks = jax.random.split(key, 10)
        inp = {}
        inp['input'] = jax.random.normal(ks[0], (B_SZ, L, D_MODEL), jnp.float32)
        out_dim = 2 * D_INNER + N_STATES + DT_RANK
        inp['Win'] = jax.random.normal(ks[1], (out_dim, D_MODEL), jnp.float32) * 0.02
        inp['b_in'] = jnp.zeros((out_dim,), jnp.float32)
        inp['A_log'] = jnp.log(jnp.tile(jnp.arange(1, N_STATES + 1, dtype=jnp.float32), (D_INNER, 1)))
        inp['B_param'] = jax.random.normal(ks[2], (N_STATES,), jnp.float32) / N_STATES ** 0.5
        inp['C_param'] = jax.random.normal(ks[3], (D_INNER, N_STATES), jnp.float32) / N_STATES ** 0.5
        inp['Wdt'] = jax.random.normal(ks[4], (D_INNER, DT_RANK), jnp.float32) * 0.02
        dt_vals = jnp.exp(jax.random.uniform(ks[5], (D_INNER,), jnp.float32) * (np.log(0.1) - np.log(0.001)) + np.log(0.001))
        inp['b_dt'] = jnp.log(jnp.expm1(dt_vals))
        inp['Wconv'] = jax.random.normal(ks[6], (D_INNER, 1, K), jnp.float32) * (1.0 / np.sqrt(K))
        inp['Wout'] = jax.random.normal(ks[7], (D_MODEL, D_INNER), jnp.float32) * 0.02
        inp['b_out'] = jnp.zeros((D_MODEL,), jnp.float32)
        return inp
    _L0_attn_in = _L0_attn_setup()

    def _L0_ffn_setup():
        import math
        import jax, jax.numpy as jnp
        import numpy as np
        NUM_EXPERTS = 8
        CAPACITY_FACTOR = 1.5
        key = jax.random.key(seed)
        ks = jax.random.split(key, 4)
        B, T, D, F, E = (4, 512, 256, 1024, NUM_EXPERTS)
        scale = 0.02
        return {'x': jax.random.normal(ks[0], (B, T, D), dtype=jnp.float32), 'router_w': jax.random.normal(ks[1], (E, D), dtype=jnp.float32) * scale, 'w1': jax.random.normal(ks[2], (E, D, F), dtype=jnp.float32) * scale, 'b1': jnp.zeros((E, F), dtype=jnp.float32), 'w2': jax.random.normal(ks[3], (E, F, D), dtype=jnp.float32) * scale, 'b2': jnp.zeros((E, D), dtype=jnp.float32)}
    _L0_ffn_in = _L0_ffn_setup()

    def _L1_attn_setup():
        import jax, jax.numpy as jnp
        import numpy as np
        D_MODEL, HD_DIM, NUM_HEADS = (256, 512, 16)
        HEAD_DIM = HD_DIM // NUM_HEADS
        B, T = (4, 512)
        key = jax.random.key(seed)
        ks = jax.random.split(key, 10)
        s = 0.02
        x = jax.random.normal(ks[0], (B, T, D_MODEL), dtype=jnp.float32)
        conv_w = jax.random.normal(ks[1], (D_MODEL, 1, 4), dtype=jnp.float32) * s
        conv_b = jax.random.normal(ks[2], (D_MODEL,), dtype=jnp.float32) * s
        qk_w = jax.random.normal(ks[3], (HD_DIM, D_MODEL), dtype=jnp.float32) * s
        v_w = jnp.eye(HD_DIM, D_MODEL, dtype=jnp.float32)
        g_w = jax.random.normal(ks[4], (HD_DIM, D_MODEL), dtype=jnp.float32) * s
        g_b = jnp.full((HD_DIM,), 2.0, dtype=jnp.float32)
        o_w = jax.random.normal(ks[5], (D_MODEL, HD_DIM), dtype=jnp.float32) * s
        ln_g = jnp.ones((D_MODEL,), dtype=jnp.float32)
        ln_b = jnp.zeros((D_MODEL,), dtype=jnp.float32)
        idx = jnp.linspace(0.0, 1.0, HEAD_DIM)
        h = jnp.arange(NUM_HEADS, dtype=jnp.float32)[:, None]
        freqs = jnp.where(h > 0, (10.0 ** idx)[None, :] * h, 0.0).astype(jnp.float32)
        gamma = jnp.full((NUM_HEADS, 1, 1), 0.999, dtype=jnp.float32).at[0].set(1.0)
        return {'x': x, 'conv_w': conv_w, 'conv_b': conv_b, 'qk_w': qk_w, 'v_w': v_w, 'g_w': g_w, 'g_b': g_b, 'o_w': o_w, 'ln_g': ln_g, 'ln_b': ln_b, 'freqs': freqs, 'gamma': gamma}
    _L1_attn_in = _L1_attn_setup()

    def _L1_ffn_setup():
        import jax, jax.numpy as jnp
        import numpy as np
        EMBED_DIM = 256
        NUM_EXPERTS = 8
        B, S = (2, 512)
        key = jax.random.key(seed)
        ks = jax.random.split(key, 5)
        scale = 1.0 / np.sqrt(EMBED_DIM)
        x = jax.random.normal(ks[0], (B, S, EMBED_DIM), dtype=jnp.float32)
        router_w = jax.random.normal(ks[1], (NUM_EXPERTS, EMBED_DIM), dtype=jnp.float32) * scale
        router_b = jnp.zeros((NUM_EXPERTS,), dtype=jnp.float32)
        expert_w = jax.random.normal(ks[2], (NUM_EXPERTS, EMBED_DIM, EMBED_DIM), dtype=jnp.float32) * scale
        expert_b = jnp.zeros((NUM_EXPERTS, EMBED_DIM), dtype=jnp.float32)
        return {'x': x, 'router_w': router_w, 'router_b': router_b, 'expert_w': expert_w, 'expert_b': expert_b}
    _L1_ffn_in = _L1_ffn_setup()
    _d = {'L0_attn_input': _L0_attn_in['input'], 'L0_attn_Win': _L0_attn_in['Win'], 'L0_attn_b_in': _L0_attn_in['b_in'], 'L0_attn_A_log': _L0_attn_in['A_log'], 'L0_attn_B_param': _L0_attn_in['B_param'], 'L0_attn_C_param': _L0_attn_in['C_param'], 'L0_attn_Wdt': _L0_attn_in['Wdt'], 'L0_attn_b_dt': _L0_attn_in['b_dt'], 'L0_attn_Wconv': _L0_attn_in['Wconv'], 'L0_attn_Wout': _L0_attn_in['Wout'], 'L0_attn_b_out': _L0_attn_in['b_out'], 'L0_ffn_router_w': _L0_ffn_in['router_w'], 'L0_ffn_w1': _L0_ffn_in['w1'], 'L0_ffn_b1': _L0_ffn_in['b1'], 'L0_ffn_w2': _L0_ffn_in['w2'], 'L0_ffn_b2': _L0_ffn_in['b2'], 'L1_attn_conv_w': _L1_attn_in['conv_w'], 'L1_attn_conv_b': _L1_attn_in['conv_b'], 'L1_attn_qk_w': _L1_attn_in['qk_w'], 'L1_attn_v_w': _L1_attn_in['v_w'], 'L1_attn_g_w': _L1_attn_in['g_w'], 'L1_attn_g_b': _L1_attn_in['g_b'], 'L1_attn_o_w': _L1_attn_in['o_w'], 'L1_attn_ln_g': _L1_attn_in['ln_g'], 'L1_attn_ln_b': _L1_attn_in['ln_b'], 'L1_attn_freqs': _L1_attn_in['freqs'], 'L1_attn_gamma': _L1_attn_in['gamma'], 'L1_ffn_router_w': _L1_ffn_in['router_w'], 'L1_ffn_router_b': _L1_ffn_in['router_b'], 'L1_ffn_expert_w': _L1_ffn_in['expert_w'], 'L1_ffn_expert_b': _L1_ffn_in['expert_b']}
    _x0 = _d['L0_attn_input']
    _d['L0_attn_input'] = jax.random.normal(jax.random.fold_in(jax.random.key(seed), 1), (2, 2048, 256), dtype=_x0.dtype)
    del _x0
    return _d

def reference(L0_attn_input, L0_attn_Win, L0_attn_b_in, L0_attn_A_log, L0_attn_B_param, L0_attn_C_param, L0_attn_Wdt, L0_attn_b_dt, L0_attn_Wconv, L0_attn_Wout, L0_attn_b_out, L0_ffn_router_w, L0_ffn_w1, L0_ffn_b1, L0_ffn_w2, L0_ffn_b2, L1_attn_conv_w, L1_attn_conv_b, L1_attn_qk_w, L1_attn_v_w, L1_attn_g_w, L1_attn_g_b, L1_attn_o_w, L1_attn_ln_g, L1_attn_ln_b, L1_attn_freqs, L1_attn_gamma, L1_ffn_router_w, L1_ffn_router_b, L1_ffn_expert_w, L1_ffn_expert_b):

    def _L0_attn_ref(input, Win, b_in, A_log, B_param, C_param, Wdt, b_dt, Wconv, Wout, b_out):
        import jax, jax.numpy as jnp
        import numpy as np
        D_MODEL = 256
        D_INNER = 512
        N_STATES = 16
        DT_RANK = 64
        K = 4
        B_SZ = 2
        L = 512

        def _causal_conv(x, w):
            xt = jnp.transpose(x, (0, 2, 1))
            y = jax.lax.conv_general_dilated(xt, w, window_strides=(1,), padding=[(K - 1, 0)], feature_group_count=D_INNER, dimension_numbers=('NCH', 'OIH', 'NCH'))
            return jnp.transpose(y, (0, 2, 1))

        def _selective_scan(delta, A, Bmat, C, x):
            dA = jnp.exp(delta[..., None] * A[None, None])
            dBx = (delta * x)[..., None] * Bmat[:, :, None, :]

            def step(h, inputs):
                dA_t, dBx_t = inputs
                h = dA_t * h + dBx_t
                y = jnp.einsum('bdn,dn->bd', h, C)
                return (h, y)
            h0 = jnp.zeros((x.shape[0], D_INNER, N_STATES), x.dtype)
            _, ys = jax.lax.scan(step, h0, (jnp.moveaxis(dA, 1, 0), jnp.moveaxis(dBx, 1, 0)))
            return jnp.moveaxis(ys, 0, 1)
        xp = input @ Win.T + b_in
        v, x, Bproj, dr = jnp.split(xp, [D_INNER, 2 * D_INNER, 2 * D_INNER + N_STATES], axis=-1)
        x = jax.nn.silu(_causal_conv(x, Wconv))
        delta = jax.nn.softplus(dr @ Wdt.T + b_dt)
        A = -jnp.exp(A_log)
        Bmat = Bproj + B_param[None, None, :]
        y = _selective_scan(delta, A, Bmat, C_param, x)
        out = y * jax.nn.silu(v)
        return out @ Wout.T + b_out

    def _L0_ffn_ref(x, router_w, w1, b1, w2, b2):
        import math
        import jax, jax.numpy as jnp
        import numpy as np
        NUM_EXPERTS = 8
        CAPACITY_FACTOR = 1.5
        B, T, D = x.shape
        E = router_w.shape[0]
        N = B * T
        C = max(math.ceil(CAPACITY_FACTOR * N / E), 1)
        x_flat = x.reshape(N, D)
        logits = x_flat @ router_w.T
        probs = jax.nn.softmax(logits, axis=-1)
        chosen_e = jnp.argmax(probs, axis=-1)
        chosen_p = jnp.max(probs, axis=-1)
        onehot = jax.nn.one_hot(chosen_e, E, dtype=jnp.float32)
        pos = jnp.take_along_axis(jnp.cumsum(onehot, axis=0), chosen_e[:, None], axis=1)[:, 0] - 1.0
        pos = pos.astype(jnp.int32)
        kept = pos < C
        pos_c = jnp.clip(pos, 0, C - 1)
        buf = jnp.zeros((E, C, D), dtype=x.dtype).at[chosen_e, pos_c].add(x_flat * kept[:, None].astype(x.dtype))
        h = jax.nn.gelu(jnp.einsum('ecd,edf->ecf', buf, w1) + b1[:, None, :], approximate=False)
        eo = jnp.einsum('ecf,efd->ecd', h, w2) + b2[:, None, :]
        y = eo[chosen_e, pos_c] * (chosen_p * kept.astype(x.dtype))[:, None]
        return y.reshape(B, T, D)

    def _L1_attn_ref(x, conv_w, conv_b, qk_w, v_w, g_w, g_b, o_w, ln_g, ln_b, freqs, gamma):
        import jax, jax.numpy as jnp
        import numpy as np
        D_MODEL, HD_DIM, NUM_HEADS = (256, 512, 16)
        HEAD_DIM = HD_DIM // NUM_HEADS
        B, T = (4, 512)
        Bsz, Tlen, C = x.shape
        H, D = freqs.shape
        xc = jax.lax.conv_general_dilated(x.transpose(0, 2, 1), conv_w, window_strides=(1,), padding=[(3, 0)], feature_group_count=C, dimension_numbers=('NCH', 'OIH', 'NCH'))
        xc = (xc + conv_b[None, :, None]).transpose(0, 2, 1)
        qk = jnp.einsum('btc,ec->bte', xc, qk_w).reshape(Bsz, Tlen, H, D)
        nrm = jnp.maximum(jnp.sqrt(jnp.sum(qk * qk, axis=-1, keepdims=True)), 1e-12)
        q = qk / nrm
        k = q
        v = jnp.einsum('btc,ec->bte', xc, v_w).reshape(Bsz, Tlen, H, D)
        g = jax.nn.sigmoid(jnp.einsum('btc,ec->bte', xc, g_w) + g_b).reshape(Bsz, Tlen, H, D)
        t = jnp.arange(Tlen, dtype=x.dtype)[None, :, None, None]
        angles = t * freqs[None, None]
        k_sh = jnp.concatenate([jnp.zeros_like(k[:, :1]), k[:, :-1]], axis=1)
        state_r = (v * jnp.cos(angles) + v * k_sh) * g
        decay = jnp.power(gamma.reshape(1, 1, H, 1), t)
        mem_r = jnp.cumsum(state_r * decay, axis=1) / (decay + 1e-06)
        out = (mem_r * q).reshape(Bsz, Tlen, H * D)
        out = jnp.einsum('bte,ce->btc', out, o_w)
        mu = jnp.mean(out, axis=-1, keepdims=True)
        var = jnp.mean((out - mu) ** 2, axis=-1, keepdims=True)
        return (out - mu) / jnp.sqrt(var + 1e-05) * ln_g + ln_b

    def _L1_ffn_ref(x, router_w, router_b, expert_w, expert_b):
        import jax, jax.numpy as jnp
        import numpy as np
        EMBED_DIM = 256
        NUM_EXPERTS = 8
        B, S = (2, 512)
        Bb, Ss, D = x.shape
        xt = x.reshape(-1, D)
        logits = xt @ router_w.T + router_b
        probs = jax.nn.softmax(logits, axis=-1)
        idx = jnp.argmax(logits, axis=-1)
        w = jnp.take_along_axis(probs, idx[:, None], axis=1)[:, 0]
        y_all = jnp.einsum('td,efd->tef', xt, expert_w) + expert_b
        y = jnp.take_along_axis(y_all, idx[:, None, None], axis=1)[:, 0]
        out = (y * w[:, None]).reshape(Bb, Ss, D)
        return out
    x = L0_attn_input
    x = _layernorm(x + _L0_attn_ref(x, L0_attn_Win, L0_attn_b_in, L0_attn_A_log, L0_attn_B_param, L0_attn_C_param, L0_attn_Wdt, L0_attn_b_dt, L0_attn_Wconv, L0_attn_Wout, L0_attn_b_out), axis=-1)
    x = _layernorm(x + _L0_ffn_ref(x, L0_ffn_router_w, L0_ffn_w1, L0_ffn_b1, L0_ffn_w2, L0_ffn_b2), axis=-1)
    x = _layernorm(x + _L1_attn_ref(x, L1_attn_conv_w, L1_attn_conv_b, L1_attn_qk_w, L1_attn_v_w, L1_attn_g_w, L1_attn_g_b, L1_attn_o_w, L1_attn_ln_g, L1_attn_ln_b, L1_attn_freqs, L1_attn_gamma), axis=-1)
    x = _layernorm(x + _L1_ffn_ref(x, L1_ffn_router_w, L1_ffn_router_b, L1_ffn_expert_w, L1_ffn_expert_b), axis=-1)
    return x

_drawn_inputs = setup_inputs


def setup_inputs(seed=0):
    import zlib

    import numpy as np

    out = dict(_drawn_inputs(seed))
    spreads = {'L0_attn_b_in': (0.0, 0.8),
     'L0_attn_b_out': (0.0, 0.1),
     'L0_ffn_b1': (0.0, 0.287),
     'L0_ffn_b2': (0.0, 0.1),
     'L1_attn_g_b': (2.0, 0.2),
     'L1_attn_ln_g': (1.0, 0.2),
     'L1_attn_ln_b': (0.0, 0.1),
     'L1_ffn_router_b': (0.0, 0.1),
     'L1_ffn_expert_b': (0.0, 0.1)}
    factors = {'L0_attn_Win': 7.465,
     'L0_attn_A_log': 8.0,
     'L0_attn_B_param': 8.0,
     'L0_attn_C_param': 7.741,
     'L0_attn_Wdt': 8.0,
     'L0_attn_b_dt': 8.0,
     'L0_attn_Wconv': 6.6,
     'L0_attn_Wout': 7.354,
     'L1_attn_g_w': 20.2}
    for name, (base, spread) in spreads.items():
        noise = np.random.default_rng([zlib.crc32(name.encode()), seed]).standard_normal(out[name].shape)
        drawn = base * np.exp(spread * noise) if base else spread * noise
        out[name] = jnp.asarray(drawn.astype(out[name].dtype))
    for name, factor in factors.items():
        out[name] = (out[name] * factor).astype(out[name].dtype)
    return out
```

```python
from contextlib import ExitStack

import concourse.bass as bass
from concourse import mybir

F32 = mybir.dt.float32
BF16 = mybir.dt.bfloat16
I32 = mybir.dt.int32
U32 = mybir.dt.uint32
ALU = mybir.AluOpType
ACT = mybir.ActivationFunctionType
AX = mybir.AxisListType

P = 128
B, T, D = 2, 2048, 256
N = B * T
KD = D // P
EPS = 1e-5
BANK = 512


class Scope:

    def __init__(self, nc, stack, prefix):
        self.nc, self.stack, self.prefix, self.sems = nc, stack, prefix, []
        stack.callback(self.clear)

    def sbuf(self, name, shape, dtype=F32):
        return self.stack.enter_context(self.nc.sbuf_tensor(f"{self.prefix}_{name}", shape, dtype))

    def psum(self, name, shape, dtype=F32):
        return self.stack.enter_context(self.nc.psum_tensor(f"{self.prefix}_{name}", shape, dtype))

    def sem(self, name):
        self.sems.append(self.nc.alloc_semaphore(f"{self.prefix}_{name}"))
        return self.sems[-1]

    def clear(self):
        if self.sems:
            self.nc.clear_and_free_semaphores(self.sems)
            self.nc.all_engine_barrier()

    def dram(self, name, shape, dtype=F32):
        return self.nc.dram_tensor(f"{self.prefix}_{name}", shape, dtype)


def make_identity(nc, s, ident, engine, zeroed, made):
    nc.gpsimd.memset(ident[:], 0.0).then_inc(zeroed, 1)
    engine.wait_ge(zeroed, 1)
    nc.gpsimd.affine_select(out=ident[:], in_=ident[:], compare_op=ALU.not_equal, fill=1.0, base=0,
                            pattern=[[-1, P]], channel_multiplier=1).then_inc(made, 1)


EXPERTS = 8
TOKEN_TILES = N // P
SLOT_TILES = TOKEN_TILES + EXPERTS


def layernorm_tiles(nc, dve, rows, stats, mv, rstd, spare, tiles, k, stat_step, var_ready, std_ready,
                    rstd_ready, normed, dst=None):
    dst = rows if dst is None else dst
    for j in range(tiles):
        ins = nc.vector.bn_stats(stats[:, j, :], rows[:, j, :])
    ins.then_inc(stat_step, 1)
    dve.wait_ge(stat_step, k)
    nc.vector.memset(spare[:], 0.0)
    for j in range(tiles):
        ins = nc.vector.bn_aggr(mv[:, j, :], stats[:, j, :])
    ins.then_inc(var_ready, 1)
    dve.wait_ge(std_ready, k)
    nc.vector.reciprocal(rstd[:], rstd[:]).then_inc(rstd_ready, 1)
    dve.wait_ge(rstd_ready, k)
    for j in range(tiles):
        ins = nc.vector.tensor_scalar(dst[:, j, :], rows[:, j, :], mv[:, j, 0:1], rstd[:, j:j + 1], ALU.subtract, ALU.mult)
    ins.then_inc(normed, 1)


def state_space_layer(nc, x_tok, x_feat, win, b_in, a_log, b_param, c_param, wdt, b_dt, wconv, wout,
                      b_out, x1):
    DI, NS, RANK, TAPS = 512, 16, 64, 4
    M = DI // P
    CH = 1024
    CHUNKS = N // CH
    HALVES = CH // BANK
    STEPS = M * NS
    TILES = CH // P
    TG = 4
    A_RING, DBX_RING, H_RING = 2, 2, 4
    PROJ_USES = 1 + 3 * M + TILES // TG
    COLS = DI * 2 + RANK + NS

    with ExitStack() as stack:
        s = Scope(nc, stack, "ssm")
        win_sb = s.sbuf("win", [P, KD, COLS])
        wout_sb = s.sbuf("wout", [P, M, D])
        wdt_sb = s.sbuf("wdt", [RANK + 1, DI])
        conv_sb = s.sbuf("conv", [P, M, TAPS])
        bv_sb = s.sbuf("bv", [P, M])
        bx_sb = s.sbuf("bx", [P, M])
        brb_sb = s.sbuf("brb", [RANK + NS, 1])
        bparam_sb = s.sbuf("bparam", [RANK + NS, 1])
        alog_sb = s.sbuf("alog", [P, M, NS])
        a_sb = s.sbuf("a", [P, M, NS])
        c_sb = s.sbuf("c", [P, M, NS])
        bout_sb = s.sbuf("bout", [P, D])
        ident = s.sbuf("ident", [P, P])
        diag_c = s.sbuf("diag_c", [P, M * NS, P])
        keep = s.sbuf("keep", [P, CHUNKS])
        eps_sb = s.sbuf("eps", [P, 1])
        xf = s.sbuf("xf", [P, KD, CH])
        rank = s.sbuf("rank", [RANK + 1, CH])
        b_all = s.sbuf("b_all", [P, NS, CH])
        xpad = s.sbuf("xpad", [P, TAPS - 1 + CH])
        hist = s.sbuf("hist", [P, M, TAPS - 1])
        xs = s.sbuf("xs", [P, M, CH])
        delta = s.sbuf("delta", [P, 2, CH])
        gate = s.sbuf("gate", [P, M, CH])
        soft_tmp = s.sbuf("soft_tmp", [P, 3, CH])
        sp_e, sp_u, sp_l = (soft_tmp[:, k, :] for k in range(3))
        xt = soft_tmp[:, 0:TILES * D // CH, :].rearrange("p a (b d) -> p (a b) d", d=D)
        b_rows = xs[:, M - 1, :]
        dbx = s.sbuf("dbx", [P, DBX_RING, CH])
        h = s.sbuf("h", [P, H_RING, CH])
        carry = s.sbuf("carry", [P, STEPS])
        stats = s.sbuf("stats", [P, TG, 6])
        mv = s.sbuf("mv", [P, TG, 2])
        rstd = s.sbuf("rstd", [P, TG])
        spare = s.sbuf("spare", [P, 1])

        decay = s.psum("decay", [P, A_RING, CH])
        y_ps = s.psum("y", [P, CH])
        proj = s.psum("proj", [P, CH])

        b_dram = s.dram("b", [NS, N])

        consts_in = s.sem("consts_in")
        zeroed = s.sem("zeroed")
        ident_ready = s.sem("ident_ready")
        pool_consts = s.sem("pool_consts")
        neg_a = s.sem("neg_a")
        a_ready = s.sem("a_ready")
        brb_ready = s.sem("brb_ready")
        diag_ready = s.sem("diag_ready")
        carry_zero = s.sem("carry_zero")
        xf_in = s.sem("xf_in")
        xt_in = s.sem("xt_in")
        proj_full = s.sem("proj_full")
        b_ready = s.sem("b_ready")
        b_stored = s.sem("b_stored")
        b_in_all = [s.sem(f"b_in_all{n}") for n in range(NS)]
        xpad_ready = s.sem("xpad_ready")
        xpad_free = s.sem("xpad_free")
        conv_step = s.sem("conv_step")
        conv_ready = s.sem("conv_ready")
        silu_ready = s.sem("silu_ready")
        gate_ready = s.sem("gate_ready")
        soft_abs = s.sem("soft_abs")
        soft_exp = s.sem("soft_exp")
        soft_add = s.sem("soft_add")
        soft_ready = s.sem("soft_ready")
        soft_step = s.sem("soft_step")
        delta_ready = s.sem("delta_ready")
        dx_ready = s.sem("dx_ready")
        decay_ready = s.sem("decay_ready")
        dbx_ready = s.sem("dbx_ready")
        scan_done = s.sem("scan_done")
        carried = s.sem("carried")
        h_used = s.sem("h_used")
        gated = s.sem("gated")
        xt_biased = s.sem("xt_biased")
        res_ready = s.sem("res_ready")
        stat_step = s.sem("stat_step")
        var_ready = s.sem("var_ready")
        std_ready = s.sem("std_ready")
        rstd_ready = s.sem("rstd_ready")
        normed = s.sem("normed")
        stored = s.sem("stored")

        b_lo, b_hi = RANK, RANK + NS

        loads = [
            (win_sb[:, :, 0:2 * DI], win.rearrange("(k p) c -> p k c", p=P)[:, :, 0:2 * DI]),
            (win_sb[:, :, 2 * DI:2 * DI + RANK], win.rearrange("(k p) c -> p k c", p=P)[:, :, 2 * DI + NS:COLS]),
            (win_sb[:, :, 2 * DI + RANK:COLS], win.rearrange("(k p) c -> p k c", p=P)[:, :, 2 * DI:2 * DI + NS]),
            (wout_sb[:], wout.rearrange("(m p) c -> p m c", p=P)),
            (wdt_sb[0:RANK, :], wdt),
            (wdt_sb[RANK:RANK + 1, :], b_dt.rearrange("(a d) -> a d", a=1)),
            (conv_sb[:], wconv.rearrange("(m p) a k -> p m (a k)", p=P)),
            (bv_sb[:], b_in[0:DI].rearrange("(m p) -> p m", p=P)),
            (bx_sb[:], b_in[DI:2 * DI].rearrange("(m p) -> p m", p=P)),
            (brb_sb[0:RANK, :], b_in[2 * DI + NS:COLS].rearrange("(p a) -> p a", a=1)),
            (brb_sb[b_lo:b_hi, :], b_in[2 * DI:2 * DI + NS].rearrange("(p a) -> p a", a=1)),
            (bparam_sb[b_lo:b_hi, :], b_param.rearrange("(p a) -> p a", a=1)),
            (alog_sb[:], a_log.rearrange("(m p) n -> p m n", p=P)),
            (c_sb[:], c_param.rearrange("(m p) n -> p m n", p=P)),
            (bout_sb[:], b_out.rearrange("(a d) -> a d", a=1).partition_broadcast(P)),
        ]
        ALL_IN = 16 * len(loads)
        POOL_FILLS = 4 + CHUNKS

        block = stack.enter_context(nc.Block())

        @block.sync
        def _(sp):
            for dst, src in loads:
                sp.dma_start(dst, src, allow_slow_non_contiguous=True).then_inc(consts_in, 16)

            def load_xf(c):
                sp.dma_start(xf[:], x_feat.rearrange("(k p) t -> p k t", p=P)[:, :, bass.ds(c * CH, CH)]).then_inc(xf_in, 16)

            def load_xt(c):
                sp.wait_ge(delta_ready, M * c + M + 1)
                sp.dma_start(xt, x_tok.rearrange("(i p) d -> p i d", p=P)[:, bass.ds(c * TILES, TILES), :]).then_inc(xt_in, 16)

            def spread_b(c):
                sp.wait_ge(b_ready, 2 * c + 2)
                sp.dma_start(b_dram[:, bass.ds(c * CH, CH)], b_rows[b_lo:b_hi, :]).then_inc(b_stored, 16)
                sp.wait_ge(b_stored, 16 * c + 16)
                for n in range(NS):
                    sp.dma_start(b_all[:, n, :], b_dram[n, bass.ds(c * CH, CH)].partition_broadcast(P)).then_inc(b_in_all[n], 16)

            load_xf(0)
            spread_b(0)
            load_xt(0)
            with sp.Fori(1, CHUNKS) as c:
                sp.wait_ge(proj_full, c * PROJ_USES - TILES // TG - 1)
                load_xf(c)
                sp.wait_ge(dbx_ready, c * STEPS)
                spread_b(c)
                load_xt(c)

        @block.gpsimd
        def _(pool):
            fills = [(eps_sb[:], EPS), (hist[:], 0.0), (rank[RANK:RANK + 1, :], 1.0), (carry[:], 0.0)]
            fills += [(keep[:, c:c + 1], 0.0 if (c + 1) * CH % T == 0 else 1.0) for c in range(CHUNKS)]
            for k, (dst, value) in enumerate(fills):
                nc.gpsimd.memset(dst, value).then_inc(pool_consts, 1)
                pool.wait_ge(pool_consts, k + 1)
            make_identity(nc, s, ident, pool, zeroed, ident_ready)
            with pool.Fori(0, CHUNKS) as c:
                base = pool.snap(c * STEPS)
                dmas = pool.snap((c + 1) * 16)
                for m in range(M):
                    pool.wait_ge(dx_ready, pool.snap(c * M + m + 1))
                    for n in range(NS):
                        i = m * NS + n
                        if m == 0:
                            pool.wait_ge(b_in_all[n], dmas)
                        pool.wait_ge(scan_done, base + (i + 1))
                        nc.gpsimd.tensor_tensor(dbx[:, i % DBX_RING, :], xs[:, m, :], b_all[:, n, :], ALU.mult).then_inc(dbx_ready, 1)
                pool.wait_ge(xt_in, dmas)
                nc.gpsimd.tensor_tensor(xt, xt, bout_sb[:].unsqueeze(1).broadcast_to([P, TILES, D]), ALU.add).then_inc(xt_biased, 1)

        @block.scalar
        def _(act):
            act.wait_ge(consts_in, ALL_IN)
            nc.scalar.activation(a_sb[:], alog_sb[:], ACT.Exp).then_inc(neg_a, 1)
            act.wait_ge(pool_consts, POOL_FILLS)
            act.wait_ge(brb_ready, 1)
            act.wait_ge(a_ready, 1)
            with act.Fori(0, CHUNKS) as c:
                base = act.snap(c * STEPS)
                uses = act.snap(c * PROJ_USES)
                groups = act.snap(c * (TILES // TG))
                blocks = act.snap(c * M)

                act.wait_ge(proj_full, uses + 1)
                nc.scalar.activation(rank[0:RANK, :], proj[0:RANK, :], ACT.Identity, bias=brb_sb[0:RANK, :]).then_inc(b_ready, 1)
                nc.scalar.activation(b_rows[b_lo:b_hi, :], proj[b_lo:b_hi, :], ACT.Identity, bias=brb_sb[b_lo:b_hi, :]).then_inc(b_ready, 1)

                def take_x(m):
                    act.wait_ge(proj_full, uses + (2 + 3 * m))
                    act.wait_ge(xpad_free, blocks + (m + 1))
                    nc.scalar.activation(xpad[:, TAPS - 1:], proj[:], ACT.Identity, bias=bx_sb[:, m:m + 1]).then_inc(xpad_ready, 1)

                def silus(m):
                    act.wait_ge(conv_ready, blocks + (m + 1))
                    nc.scalar.activation(xs[:, m, :], xs[:, m, :], ACT.Silu).then_inc(silu_ready, 1)
                    act.wait_ge(proj_full, uses + (3 + 3 * m))
                    nc.scalar.activation(gate[:, m, :], proj[:], ACT.Silu, bias=bv_sb[:, m:m + 1]).then_inc(gate_ready, 1)

                def soft(m):
                    act.wait_ge(proj_full, uses + (4 + 3 * m))
                    act.wait_ge(delta_ready, blocks + (m + 1))
                    if m == 0:
                        act.wait_ge(stored, 16 * c + 16)
                    nc.scalar.activation(sp_e, proj[:], ACT.Abs).then_inc(soft_abs, 1)
                    act.wait_ge(soft_abs, blocks + (m + 1))
                    nc.scalar.activation(sp_e, sp_e, ACT.Exp, scale=-1.0).then_inc(soft_exp, 1)
                    act.wait_ge(soft_exp, blocks + (m + 1))
                    nc.scalar.activation(sp_u, sp_e, ACT.Identity, bias=1.0).then_inc(soft_add, 1)
                    act.wait_ge(soft_add, blocks + (m + 1))
                    nc.scalar.activation(sp_l, sp_u, ACT.Ln).then_inc(soft_ready, 1)

                def decays(m, n):
                    i = m * NS + n
                    act.wait_ge(scan_done, base + (i + 1))
                    nc.scalar.activation(decay[:, i % A_RING, :], delta[:, m % 2, :], ACT.Exp, scale=a_sb[:, m, n:n + 1]).then_inc(decay_ready, 1)

                take_x(0)
                silus(0)
                soft(0)
                for m in range(M):
                    act.wait_ge(delta_ready, blocks + (m + 2))
                    for n in range(NS):
                        decays(m, n)
                        if m + 1 < M:
                            if n == 1:
                                take_x(m + 1)
                            if n == 5:
                                silus(m + 1)
                            if n == 8:
                                soft(m + 1)

                for g in range(TILES // TG):
                    act.wait_ge(var_ready, groups + (g + 1))
                    nc.scalar.activation(rstd[:], mv[:, :, 1], ACT.Sqrt, bias=eps_sb[:]).then_inc(std_ready, 1)
                act.wait_ge(normed, groups + TILES // TG)
                act.dma_start(x1.rearrange("(i p) d -> p i d", p=P)[:, bass.ds(c * TILES, TILES), :], xt).then_inc(stored, 16)
            act.wait_ge(stored, 16 * CHUNKS + 16)

        @block.vector
        def _(dve):
            dve.wait_ge(consts_in, ALL_IN)
            dve.wait_ge(pool_consts, POOL_FILLS)
            dve.sem_inc(res_ready, 1)
            dve.sem_inc(xpad_free, 1)
            dve.sem_inc(delta_ready, 1)
            dve.sem_inc(scan_done, A_RING)
            dve.sem_inc(h_used, H_RING)
            dve.sem_inc(gated, 1)
            dve.sem_inc(carried, 1)
            dve.sem_inc(stored, 16)
            nc.vector.tensor_tensor(brb_sb[b_lo:b_hi, :], brb_sb[b_lo:b_hi, :], bparam_sb[b_lo:b_hi, :], ALU.add).then_inc(brb_ready, 1)
            dve.wait_ge(neg_a, 1)
            nc.vector.tensor_scalar(a_sb[:], a_sb[:], -1.0, None, ALU.mult).then_inc(a_ready, 1)
            dve.wait_ge(ident_ready, 1)
            for m in range(M):
                for n in range(NS):
                    last = nc.vector.tensor_scalar(diag_c[:, m * NS + n, :], ident[:], c_sb[:, m, n:n + 1], None, ALU.mult)
            last.then_inc(diag_ready, 1)
            with dve.Fori(0, CHUNKS) as c:
                base = dve.snap(c * STEPS)
                uses = dve.snap(c * PROJ_USES)
                blocks = dve.snap(c * M)
                convs = dve.snap(c * (M * TAPS))
                softs = dve.snap(c * (M * 2))
                groups = dve.snap(c * (TILES // TG))

                def conv(m):
                    dve.wait_ge(xpad_free, blocks + (m + 1))
                    nc.vector.tensor_copy(xpad[:, 0:TAPS - 1], hist[:, m, :]).then_inc(conv_step, 1)
                    dve.wait_ge(conv_step, convs + (m * TAPS + 1))
                    dve.wait_ge(xpad_ready, blocks + (m + 1))
                    if m == M - 1:
                        dve.wait_ge(b_stored, 16 * c + 16)
                    nc.vector.tensor_scalar(xs[:, m, :], xpad[:, 0:CH], conv_sb[:, m, 0:1], None, ALU.mult).then_inc(conv_step, 1)
                    for k in range(1, TAPS):
                        dve.wait_ge(conv_step, convs + (m * TAPS + 1 + k))
                        ins = nc.vector.scalar_tensor_tensor(out=xs[:, m, :], in0=xpad[:, k:k + CH], scalar=conv_sb[:, m, k:k + 1],
                                                             in1=xs[:, m, :], op0=ALU.mult, op1=ALU.add)
                        ins.then_inc(conv_ready if k == TAPS - 1 else conv_step, 1)
                    nc.vector.tensor_scalar(hist[:, m, :], xpad[:, CH:CH + TAPS - 1], keep[:, bass.ds(c, 1)], None, ALU.mult).then_inc(xpad_free, 1)

                def soft(m):
                    dve.wait_ge(soft_ready, blocks + (m + 1))
                    nc.vector.scalar_tensor_tensor(out=sp_u, in0=sp_u, scalar=-1.0, in1=sp_e, op0=ALU.add, op1=ALU.subtract).then_inc(soft_step, 1)
                    nc.vector.scalar_tensor_tensor(out=sp_l, in0=proj[:], scalar=0.0, in1=sp_l, op0=ALU.max, op1=ALU.add).then_inc(soft_step, 1)
                    dve.wait_ge(soft_step, softs + (2 * m + 2))
                    nc.vector.tensor_tensor(delta[:, m % 2, :], sp_l, sp_u, ALU.subtract).then_inc(delta_ready, 1)
                    dve.wait_ge(delta_ready, blocks + (m + 2))
                    dve.wait_ge(silu_ready, blocks + (m + 1))
                    nc.vector.tensor_tensor(xs[:, m, :], xs[:, m, :], delta[:, m % 2, :], ALU.mult).then_inc(dx_ready, 1)

                def scan(i):
                    dve.wait_ge(decay_ready, base + (i + 1))
                    dve.wait_ge(dbx_ready, base + (i + 1))
                    dve.wait_ge(h_used, base + (i + 1))
                    nc.vector.tensor_tensor_scan(h[:, i % H_RING, :], decay[:, i % A_RING, :], dbx[:, i % DBX_RING, :],
                                                 carry[:, i:i + 1], ALU.mult, ALU.add).then_inc(scan_done, 1)

                def save(i):
                    dve.wait_ge(scan_done, base + (i + 3))
                    nc.vector.tensor_scalar(carry[:, i:i + 1], h[:, i % H_RING, CH - 1:CH], keep[:, bass.ds(c, 1)], None, ALU.mult).then_inc(carried, 1)

                def gate_y(m):
                    dve.wait_ge(h_used, base + ((m + 1) * NS + H_RING))
                    dve.wait_ge(gate_ready, blocks + (m + 1))
                    nc.vector.tensor_tensor(gate[:, m, :], y_ps[:], gate[:, m, :], ALU.mult).then_inc(gated, 1)

                conv(0)
                soft(0)
                for m in range(M):
                    for n in range(NS):
                        i = m * NS + n
                        if i == 0:
                            dve.wait_ge(carried, base + 1)
                        scan(i)
                        if i:
                            save(i - 1)
                        if n == 1 and m:
                            gate_y(m - 1)
                        if m + 1 < M:
                            if n == 3:
                                conv(m + 1)
                            if n == 11:
                                soft(m + 1)
                save(STEPS - 1)
                gate_y(M - 1)
                dve.wait_ge(xt_biased, dve.snap(c + 1))
                for g in range(TILES // TG):
                    rows = xt[:, g * TG:(g + 1) * TG, :]
                    dve.wait_ge(proj_full, uses + (2 + 3 * M + g))
                    nc.vector.tensor_tensor(rows, proj[:].rearrange("p (i d) -> p i d", d=D), rows, ALU.add).then_inc(res_ready, 1)
                    dve.wait_ge(res_ready, groups + (g + 2))
                    layernorm_tiles(nc, dve, rows, stats, mv, rstd, spare, TG, groups + (g + 1), stat_step, var_ready,
                                    std_ready, rstd_ready, normed)
                    dve.wait_ge(normed, groups + (g + 1))

        @block.tensor
        def _(pe):
            pe.wait_ge(consts_in, ALL_IN)
            pe.wait_ge(diag_ready, 1)
            pe.wait_ge(pool_consts, POOL_FILLS)
            with pe.Fori(0, CHUNKS) as c:
                base = pe.snap(c * STEPS)
                groups = pe.snap(c * (TILES // TG))
                blocks = pe.snap(c * M)

                def project(rows, lhs, rhs):
                    for half in range(HALVES):
                        cols = slice(half * BANK, (half + 1) * BANK)
                        for j in range(len(lhs)):
                            ins = nc.tensor.matmul(proj[0:rows, cols], lhs[j], rhs[j][:, cols], start=(j == 0), stop=(j == len(lhs) - 1))
                    return ins

                xf_k = [xf[:, k, :] for k in range(KD)]

                def project_x(m):
                    if m == 0:
                        pe.wait_ge(b_ready, 2 * c + 2)
                    else:
                        pe.wait_ge(delta_ready, blocks + (m + 1))
                    project(P, [win_sb[:, k, DI + m * P:DI + (m + 1) * P] for k in range(KD)], xf_k).then_inc(proj_full, 1)

                def project_v(m):
                    pe.wait_ge(xpad_ready, blocks + (m + 1))
                    project(P, [win_sb[:, k, m * P:(m + 1) * P] for k in range(KD)], xf_k).then_inc(proj_full, 1)

                def project_dt(m):
                    pe.wait_ge(gate_ready, blocks + (m + 1))
                    project(P, [wdt_sb[:, m * P:(m + 1) * P]], [rank]).then_inc(proj_full, 1)

                pe.wait_ge(xf_in, pe.snap((c + 1) * 16))
                pe.wait_ge(res_ready, groups + 1)
                project(RANK + NS, [win_sb[:, k, 2 * DI:COLS] for k in range(KD)], xf_k).then_inc(proj_full, 1)
                project_x(0)
                project_v(0)
                project_dt(0)
                for m in range(M):
                    for n in range(NS):
                        i = m * NS + n
                        if n == 0:
                            pe.wait_ge(gated, blocks + (m + 1))
                        pe.wait_ge(scan_done, base + (i + 3))
                        for half in range(HALVES):
                            cols = slice(half * BANK, (half + 1) * BANK)
                            ins = nc.tensor.matmul(y_ps[:, cols], diag_c[:, i, :], h[:, i % H_RING, cols], start=(n == 0), stop=(n == NS - 1))
                        ins.then_inc(h_used, 1)
                        if m + 1 < M:
                            if n == 0:
                                project_x(m + 1)
                            if n == 3:
                                project_v(m + 1)
                            if n == 6:
                                project_dt(m + 1)
                pe.wait_ge(gated, blocks + (M + 1))
                for g in range(TILES // TG):
                    if g:
                        pe.wait_ge(res_ready, groups + (g + 1))
                    else:
                        pe.wait_ge(delta_ready, blocks + (M + 1))
                    for j in range(TG):
                        t = (g * TG + j) * P
                        for m in range(M):
                            ins = nc.tensor.matmul(proj[:, j * D:(j + 1) * D], gate[:, m, t:t + P], wout_sb[:, m, :],
                                                   start=(m == 0), stop=(m == M - 1))
                    ins.then_inc(proj_full, 1)


def route(nc, prefix, x1, router, router_b, slot_table, slots, weight, capacity, tile_expert=None):
    E, NT = EXPERTS, TOKEN_TILES
    G = 4
    GROUPS = NT // G
    SLOTS = E * capacity if capacity else P * SLOT_TILES
    with ExitStack() as stack:
        s = Scope(nc, stack, prefix)
        router_sb = s.sbuf("router", [P, KD, E])
        bias_sb = s.sbuf("bias", [P, E])
        ident = s.sbuf("ident", [P, P])
        xt = s.sbuf("xt", [P, 2, G, D])
        xT = s.sbuf("xT", [P, 2, G, D])
        logits = s.sbuf("logits", [P, NT, E])
        ex = s.sbuf("ex", [P, NT, E])
        row = s.sbuf("row", [P, 6, NT])
        big, total, p, best, pos, slot = (row[:, k, :] for k in range(6))
        hot = s.sbuf("hot", [P, NT, E])
        hot_b = s.sbuf("hot_b", [P, NT, E], BF16)
        rev = s.sbuf("rev", [P, E])
        base = s.sbuf("base", [P, E])
        token = s.sbuf("token", [P, NT], I32)
        token_f = s.sbuf("token_f", [P, NT])
        iota_i = s.sbuf("iota_i", [P, 2 * E], I32)
        zeros = s.sbuf("zeros", [P, SLOTS // P], I32)
        ones_row = s.sbuf("ones_row", [P, NT])
        upper = s.sbuf("upper", [P, P], BF16)
        ones = s.sbuf("ones", [P, P], BF16)
        before = s.sbuf("before", [P, NT, E])
        small = s.sbuf("small", [P, 4, E])
        small_i = s.sbuf("small_i", [P, E], I32)
        tile_no = s.sbuf("tile_no", [P, SLOT_TILES, E])
        tile_no_i = s.sbuf("tile_no_i", [P, SLOT_TILES, E], I32)
        tile_f = s.sbuf("tile_f", [P, SLOT_TILES])
        low = s.sbuf("low", [P, NT], I32)
        t_ps = s.psum("t", [P, 2, G * D])
        l_ps = s.psum("l", [P, 2, BANK])
        c_ps = s.psum("c", [P, 2, NT, E])

        router_in = s.sem("router_in")
        zeroed = s.sem("zeroed")
        ident_ready = s.sem("ident_ready")
        consts = s.sem("consts")
        x_in = [s.sem(f"x_in{u}") for u in range(2)]
        turned = s.sem("turned")
        xT_ready = s.sem("xT_ready")
        logit_ps = s.sem("logit_ps")
        logit_ready = s.sem("logit_ready")
        step = s.sem("step")
        ex_ready = s.sem("ex_ready")
        hot_ready = s.sem("hot_ready")
        counted = s.sem("counted")
        slots_ready = s.sem("slots_ready")
        table_zero = s.sem("table_zero")
        scattered = s.sem("scattered")
        CONSTS = 8
        ROUTER_IN = 16 if router_b is None else 32

        block = stack.enter_context(nc.Block())

        @block.sync
        def _(sp):
            sp.dma_start(router_sb[:], router.rearrange("(k p) e -> p k e", p=P)).then_inc(router_in, 16)
            if router_b is not None:
                sp.dma_start(bias_sb[:], router_b.rearrange("(a e) -> a e", a=1).partition_broadcast(P)).then_inc(router_in, 16)
            x_v = x1.rearrange("(i p) d -> p i d", p=P)
            for g in range(2):
                sp.dma_start(xt[:, g, :, :], x_v[:, g * G:(g + 1) * G, :]).then_inc(x_in[g], 16)
            sp.wait_ge(consts, CONSTS)
            sp.dma_start(slot_table[0:SLOTS, :].rearrange("(p a) b -> p (a b)", p=P), zeros[:]).then_inc(table_zero, 16)
            with sp.Fori(1, GROUPS // 2) as i:
                for u in range(2):
                    sp.wait_ge(turned, 2 * i + (u - 1))
                    sp.dma_start(xt[:, u, :, :], x_v[:, bass.ds((2 * i + u) * G, G), :]).then_inc(x_in[u], 16)

        @block.gpsimd
        def _(pool):
            nc.gpsimd.memset(ident[:], 0.0).then_inc(zeroed, 1)
            nc.gpsimd.memset(upper[:], 1.0).then_inc(zeroed, 1)
            pool.wait_ge(zeroed, 2)
            nc.gpsimd.affine_select(out=ident[:], in_=ident[:], compare_op=ALU.not_equal, fill=1.0, base=0,
                                    pattern=[[-1, P]], channel_multiplier=1).then_inc(ident_ready, 1)
            nc.gpsimd.affine_select(out=upper[:], in_=upper[:], compare_op=ALU.is_ge, fill=0.0, base=0,
                                    pattern=[[1, P]], channel_multiplier=-1).then_inc(consts, 1)
            nc.gpsimd.memset(ones[:], 1.0).then_inc(consts, 1)
            nc.gpsimd.memset(ones_row[:], 1.0).then_inc(consts, 1)
            nc.gpsimd.memset(zeros[:], 0).then_inc(consts, 1)
            nc.gpsimd.iota(token[:], pattern=[[P, NT]], base=0, channel_multiplier=1).then_inc(zeroed, 1)
            nc.gpsimd.iota(iota_i[:, 0:E], pattern=[[-1, E]], base=E, channel_multiplier=0).then_inc(zeroed, 1)
            nc.gpsimd.iota(iota_i[:, E:2 * E], pattern=[[capacity or 0, E]], base=0, channel_multiplier=0).then_inc(zeroed, 1)
            nc.gpsimd.iota(tile_no_i[:], pattern=[[1, SLOT_TILES], [0, E]], base=0, channel_multiplier=0).then_inc(zeroed, 1)
            pool.wait_ge(zeroed, 6)
            pool.wait_ge(consts, 4)
            nc.gpsimd.tensor_copy(token_f[:], token[:]).then_inc(consts, 1)
            nc.gpsimd.tensor_copy(tile_no[:], tile_no_i[:]).then_inc(consts, 1)
            nc.gpsimd.tensor_copy(rev[:], iota_i[:, 0:E]).then_inc(consts, 1)
            nc.gpsimd.tensor_copy(base[:], iota_i[:, E:2 * E]).then_inc(consts, 1)
            pool.wait_ge(consts, CONSTS)
            pool.wait_ge(slots_ready, 1)
            pool.wait_ge(table_zero, 16)
            for t in range(NT):
                nc.gpsimd.indirect_dma_start(slot_table[:], bass.IndirectOffsetOnAxis(ap=slots[:, t:t + 1], axis=0),
                                             token[:, t:t + 1], None).then_inc(scattered, 16)
            pool.wait_ge(scattered, 16 * NT)

        @block.scalar
        def _(act):
            with act.Fori(0, GROUPS // 2) as i:
                for u in range(2):
                    act.wait_ge(turned, 2 * i + (u + 1))
                    act.wait_ge(logit_ps, 2 * i + (u + 1))
                    nc.scalar.activation(xT[:, u, :, :], t_ps[:, u, :].rearrange("p (g d) -> p g d", d=D), ACT.Copy).then_inc(xT_ready, 1)
            act.wait_ge(step, 2 if router_b is None else 3)
            nc.scalar.activation(ex[:], ex[:], ACT.Exp).then_inc(ex_ready, 1)

        @block.tensor
        def _(pe):
            pe.wait_ge(router_in, ROUTER_IN)
            pe.wait_ge(ident_ready, 1)
            with pe.Fori(0, GROUPS // 2) as i:
                for u in range(2):
                    pe.wait_ge(x_in[u], 16 * i + 16)
                    pe.wait_ge(xT_ready, 2 * i + (u + 1))
                    for j in range(G):
                        for k in range(KD):
                            ins = nc.tensor.transpose(t_ps[:, u, j * D + k * P:j * D + (k + 1) * P], xt[:, u, j, k * P:(k + 1) * P], ident[:])
                    ins.then_inc(turned, 1)
                for u in range(2):
                    pe.wait_ge(xT_ready, 2 * i + (u + 3))
                    pe.wait_ge(logit_ready, 2 * i + (u + 1))
                    for j in range(G):
                        for k in range(KD):
                            ins = nc.tensor.matmul(l_ps[:, u, j * E:(j + 1) * E], xT[:, u, j, k * P:(k + 1) * P], router_sb[:, k, :],
                                                   start=(k == 0), stop=(k == KD - 1))
                    ins.then_inc(logit_ps, 1)
            pe.wait_ge(consts, CONSTS)
            pe.wait_ge(hot_ready, 1)
            nc.tensor.matmul(c_ps[:, 0, :, :], upper[:], hot_b[:], start=True, stop=True)
            nc.tensor.matmul(c_ps[:, 1, :, :], ones[:], hot_b[:], start=True, stop=True).then_inc(counted, 1)

        @block.vector
        def _(dve):
            dve.sem_inc(xT_ready, 2)
            dve.sem_inc(logit_ready, 2)
            dve.sem_inc(logit_ps, 2)
            with dve.Fori(0, GROUPS // 2) as i:
                for u in range(2):
                    dve.wait_ge(logit_ps, 2 * i + (u + 3))
                    nc.vector.tensor_copy(logits[:, bass.ds((2 * i + u) * G, G), :],
                                          l_ps[:, u, 0:G * E].rearrange("p (g e) -> p g e", e=E)).then_inc(logit_ready, 1)
            dve.wait_ge(logit_ready, GROUPS + 2)
            dve.wait_ge(consts, CONSTS)
            done = [0]

            def after(ins):
                ins.then_inc(step, 1)
                done[0] += 1
                dve.wait_ge(step, done[0])

            def per_expert(x):
                return x.unsqueeze(1).broadcast_to([P, NT, E])

            def per_token(x):
                return x.unsqueeze(2).broadcast_to([P, NT, E])

            v = nc.vector
            if router_b is not None:
                dve.wait_ge(router_in, ROUTER_IN)
                after(v.tensor_tensor(logits[:], logits[:], per_expert(bias_sb[:]), ALU.add))
            after(v.tensor_reduce(big, logits[:], AX.X, ALU.max))
            after(v.tensor_tensor(ex[:], logits[:], per_token(big), ALU.subtract))
            dve.wait_ge(ex_ready, 1)
            after(v.tensor_reduce(total, ex[:], AX.X, ALU.add))
            after(v.reciprocal(p, total))
            scores = ex if capacity else logits
            after(v.tensor_reduce(big, scores[:], AX.X, ALU.max))
            after(v.tensor_tensor(hot[:], scores[:], per_token(big), ALU.is_ge))
            after(v.tensor_tensor(hot[:], hot[:], per_expert(rev[:]), ALU.mult))
            after(v.tensor_reduce(best, hot[:], AX.X, ALU.max))
            after(v.tensor_tensor(hot[:], per_expert(rev[:]), per_token(best), ALU.is_equal))
            v.tensor_copy(hot_b[:], hot[:]).then_inc(hot_ready, 1)
            dve.wait_ge(counted, 1)
            after(v.tensor_copy(ex[:], c_ps[:, 1, :, :]))
            for e in range(E):
                ins = v.tensor_tensor_scan(before[:, :, e], ones_row[:], ex[:, :, e], 0.0, ALU.mult, ALU.add)
            after(ins)
            if not capacity:
                counts, tiles, ends, starts = (small[:, k, :] for k in range(4))
                after(v.tensor_scalar(counts, before[:, NT - 1, :], P / 2 - 0.5, 1.0 / P, ALU.add, ALU.mult))
                after(v.tensor_copy(small_i[:], counts))
                after(v.tensor_copy(tiles, small_i[:]))
                after(v.tensor_tensor_scan(ends, ones_row[:, 0:E], tiles, 0.0, ALU.mult, ALU.add))
                after(v.tensor_tensor(starts, ends, tiles, ALU.subtract))
                after(v.tensor_scalar(base[:], starts, float(P), None, ALU.mult))
                after(v.tensor_tensor(tile_no[:], tile_no[:], ends.unsqueeze(1).broadcast_to([P, SLOT_TILES, E]), ALU.is_ge))
                after(v.tensor_reduce(tile_f[:], tile_no[:], AX.X, ALU.add))
                after(v.tensor_scalar(tile_f[:], tile_f[:], float(E - 1), None, ALU.min))
                after(v.tensor_copy(tile_expert[:], tile_f[0:1, :]))
            after(v.tensor_tensor(before[:], before[:], ex[:], ALU.subtract))
            after(v.tensor_tensor(before[:], before[:], c_ps[:, 0, :, :], ALU.add))
            after(v.tensor_tensor(ex[:], before[:], hot[:], ALU.mult))
            after(v.tensor_reduce(pos, ex[:], AX.X, ALU.add))
            after(v.tensor_tensor(ex[:], per_expert(base[:]), hot[:], ALU.mult))
            after(v.tensor_reduce(slot, ex[:], AX.X, ALU.add))
            after(v.scalar_tensor_tensor(out=slot, in0=slot, scalar=-1.0, in1=pos, op0=ALU.add, op1=ALU.add))
            if not capacity:
                after(v.tensor_copy(weight[:], p))
                after(v.tensor_copy(slots[:], slot))
                after(v.tensor_scalar(low[:], slots[:], P - 1, None, ALU.bitwise_and))
                after(v.tensor_scalar(slots[:], slots[:], P.bit_length() - 1, None, ALU.logical_shift_right))
                after(v.tensor_copy(pos, low[:]))
                after(v.tensor_copy(slot, slots[:]))
                after(v.scalar_tensor_tensor(out=slot, in0=pos, scalar=float(SLOT_TILES), in1=slot, op0=ALU.mult, op1=ALU.add))
                v.tensor_copy(slots[:], slot).then_inc(slots_ready, 1)
                return
            after(v.tensor_scalar(pos, pos, float(capacity), None, ALU.is_le))
            after(v.tensor_tensor(weight[:], p, pos, ALU.mult))
            after(v.tensor_scalar(token_f[:], token_f[:], float(SLOTS), None, ALU.add))
            after(v.tensor_tensor(slot, slot, token_f[:], ALU.subtract))
            after(v.tensor_tensor(slot, slot, pos, ALU.mult))
            after(v.tensor_tensor(slot, slot, token_f[:], ALU.add))
            v.tensor_copy(slots[:], slot).then_inc(slots_ready, 1)


def capacity_experts(nc, x1, slot_table, w1, b1, w2, b2, eo, capacity):
    E, F = EXPERTS, w1.shape[2]
    FB = F // P
    J = capacity // P
    HALF = capacity // 2
    H_BANKS, O_BANKS = 4, 2
    with ExitStack() as stack:
        s = Scope(nc, stack, "ffn")
        ident = s.sbuf("ident", [P, P])
        w1_sb = s.sbuf("w1", [P, 2, KD, F])
        w2_sb = s.sbuf("w2", [P, 2, FB, D])
        b1_rows = s.sbuf("b1_rows", [E * FB, P])
        b1_sb = s.sbuf("b1", [P, E * FB])
        b2_sb = s.sbuf("b2", [P, E, D])
        ids = s.sbuf("ids", [P, E, J], I32)
        ids_now = s.sbuf("ids_now", [P, 2, J], I32)
        b1_now = s.sbuf("b1_now", [P, 2, FB])
        spare = s.sbuf("spare", [P, 1])
        xg = s.sbuf("xg", [P, 2, J, D])
        xT = s.sbuf("xT", [P, 2, KD, capacity])
        hT = s.sbuf("hT", [P, 2, FB, capacity])
        out_sb = s.sbuf("out", [P, 2, J, D])
        t_ps = s.psum("t", [P, 2, BANK])
        h_ps = s.psum("h", [P, H_BANKS, BANK])
        o_ps = s.psum("o", [P, O_BANKS, BANK])

        zeroed = s.sem("zeroed")
        ident_ready = s.sem("ident_ready")
        ids_in = s.sem("ids_in")
        b1_in = s.sem("b1_in")
        b2_in = s.sem("b2_in")
        b1_turned = s.sem("b1_turned")
        b1_ready = s.sem("b1_ready")
        w1_in = [s.sem(f"w1_in{u}") for u in range(2)]
        w2_in = [s.sem(f"w2_in{u}") for u in range(2)]
        ids_ready = s.sem("ids_ready")
        gathered = [s.sem(f"gathered{u}") for u in range(2)]
        turned = s.sem("turned")
        xT_ready = s.sem("xT_ready")
        h_full = s.sem("h_full")
        h_ready = s.sem("h_ready")
        o_full = s.sem("o_full")
        o_ready = s.sem("o_ready")
        stored = [s.sem(f"stored{u}") for u in range(2)]
        TG = J // 2
        HG = 2 * FB

        block = stack.enter_context(nc.Block())

        @block.sync
        def _(sp):
            sp.dma_start(ids[:], slot_table[0:E * capacity, :].rearrange("(e p j) a -> p e (j a)", p=P, e=E)).then_inc(ids_in, 16)
            sp.dma_start(b1_rows[:], b1.rearrange("e (f p) -> (e f) p", p=P)).then_inc(b1_in, 16)

            def load(e, u):
                sp.dma_start(w1_sb[:, u, :, :], w1[bass.ds(e, 1), :, :].rearrange("a (k p) f -> p (a k) f", p=P)).then_inc(w1_in[u], 16)
                sp.dma_start(w2_sb[:, u, :, :], w2[bass.ds(e, 1), :, :].rearrange("a (f p) d -> p (a f) d", p=P)).then_inc(w2_in[u], 16)

            load(0, 0)
            load(1, 1)
            sp.dma_start(b2_sb[:], b2.partition_broadcast(P)).then_inc(b2_in, 16)

            def store(e, u):
                sp.wait_ge(o_ready, (e + 1) * J + O_BANKS)
                sp.dma_start(eo.rearrange("(e p j) d -> p e (j d)", e=E, p=P)[:, bass.ds(e, 1), :].rearrange("p a b -> p (a b)"),
                             out_sb[:, u, :, :].rearrange("p j d -> p (j d)")).then_inc(stored[u], 16)

            with sp.Fori(0, E // 2 - 1) as i:
                for u in range(2):
                    store(2 * i + u, u)
                    sp.wait_ge(o_full, (2 * i + (u + 3)) * J)
                    load(2 * i + (u + 2), u)
            store(E - 2, 0)
            store(E - 1, 1)
            for u in range(2):
                sp.wait_ge(stored[u], 8 * E + 16)

        @block.gpsimd
        def _(pool):
            make_identity(nc, s, ident, pool, zeroed, ident_ready)
            pool.wait_ge(ids_in, 16)
            pool.wait_ge(ident_ready, 1)
            with pool.Fori(0, E // 2) as i:
                for u in range(2):
                    pool.wait_ge(turned, (2 * i + (u + 1)) * TG)
                    nc.gpsimd.tensor_copy(ids_now[:, u, :], ids[:, bass.ds(2 * i + u, 1), :].rearrange("p a j -> p (a j)")).then_inc(ids_ready, 1)
                    pool.wait_ge(ids_ready, 2 * i + (u + 1))
                    nc.gpsimd.tensor_tensor(spare[:], ident[:, 0:1], ident[:, 0:1], ALU.add)
                    for j in range(J):
                        nc.gpsimd.indirect_dma_start(xg[:, u, j, :], None, x1[:],
                                                     bass.IndirectOffsetOnAxis(ap=ids_now[:, u, j:j + 1], axis=0)).then_inc(gathered[u], 16)

        @block.scalar
        def _(act):
            act.wait_ge(b1_turned, 1)
            nc.scalar.activation(b1_sb[:], t_ps[:, 0, 0:E * FB], ACT.Copy).then_inc(b1_ready, 1)
            act.wait_ge(b1_ready, 1)
            with act.Fori(0, E // 2) as i:
                for u in range(2):
                    groups = act.snap((2 * i + u) * HG)
                    act.wait_ge(o_full, (2 * i + (u + 1)) * J)
                    nc.scalar.activation(b1_now[:, u, :], b1_sb[:, bass.ds((2 * i + u) * FB, FB)], ACT.Copy).then_inc(b1_ready, 1)
                    act.wait_ge(b1_ready, 2 * i + (u + 2))
                    for f in range(FB):
                        for half in range(2):
                            k = 2 * f + half
                            act.wait_ge(h_full, groups + (k + 1))
                            nc.scalar.activation(hT[:, u, f, half * HALF:(half + 1) * HALF], h_ps[:, (u * HG + k) % H_BANKS, 0:HALF],
                                                 ACT.Gelu, bias=b1_now[:, u, f:f + 1]).then_inc(h_ready, 1)

        @block.tensor
        def _(pe):
            pe.wait_ge(ident_ready, 1)
            pe.wait_ge(b1_in, 16)
            nc.tensor.transpose(t_ps[:, 0, 0:E * FB], b1_rows[:], ident[0:E * FB, 0:E * FB]).then_inc(b1_turned, 1)
            pe.wait_ge(b1_ready, 1)
            with pe.Fori(0, E // 2) as i:
                for u in range(2):
                    e = 2 * i + u
                    tgroups = pe.snap(e * TG)
                    hgroups = pe.snap(e * HG)
                    ogroups = pe.snap(e * J)
                    pe.wait_ge(gathered[u], (16 * J) * i + 16 * J)
                    for g in range(TG):
                        b = (u * TG + g) % 2
                        pe.wait_ge(xT_ready, tgroups + (g + 1))
                        for jj in range(2):
                            for k in range(KD):
                                ins = nc.tensor.transpose(t_ps[:, b, (2 * jj + k) * P:(2 * jj + k + 1) * P], xg[:, u, 2 * g + jj, k * P:(k + 1) * P], ident[:])
                        ins.then_inc(turned, 1)
                    pe.wait_ge(xT_ready, tgroups + (TG + 2))
                    pe.wait_ge(w1_in[u], 16 * i + 16)
                    for f in range(FB):
                        for half in range(2):
                            n = 2 * f + half
                            pe.wait_ge(h_ready, hgroups + (n + 1))
                            for k in range(KD):
                                ins = nc.tensor.matmul(h_ps[:, (u * HG + n) % H_BANKS, 0:HALF], w1_sb[:, u, k, f * P:(f + 1) * P],
                                                       xT[:, u, k, half * HALF:(half + 1) * HALF], start=(k == 0), stop=(k == KD - 1))
                            ins.then_inc(h_full, 1)
                    pe.wait_ge(h_ready, hgroups + (HG + H_BANKS))
                    pe.wait_ge(w2_in[u], 16 * i + 16)
                    for j in range(J):
                        pe.wait_ge(o_ready, ogroups + (j + 1))
                        for f in range(FB):
                            ins = nc.tensor.matmul(o_ps[:, j % O_BANKS, 0:D], hT[:, u, f, j * P:(j + 1) * P], w2_sb[:, u, f, :],
                                                   start=(f == 0), stop=(f == FB - 1))
                        ins.then_inc(o_full, 1)

        @block.vector
        def _(dve):
            dve.sem_inc(xT_ready, 2)
            dve.sem_inc(h_ready, H_BANKS)
            dve.sem_inc(o_ready, O_BANKS)
            dve.sem_inc(turned, 2 * TG)
            dve.sem_inc(o_full, 2 * J)
            dve.sem_inc(stored[0], 16)
            dve.sem_inc(stored[1], 16)
            dve.wait_ge(b2_in, 16)
            with dve.Fori(0, E // 2) as i:
                for u in range(2):
                    e = 2 * i + u
                    tgroups = dve.snap(e * TG)
                    ogroups = dve.snap(e * J)
                    for g in range(TG):
                        b = (u * TG + g) % 2
                        dve.wait_ge(turned, tgroups + (2 * TG + g + 1))
                        nc.vector.tensor_copy(xT[:, u, :, 2 * g * P:(2 * g + 2) * P].rearrange("p k (j t) -> p j k t", t=P),
                                              t_ps[:, b, :].rearrange("p (j k t) -> p j k t", k=KD, t=P)).then_inc(xT_ready, 1)
                    dve.wait_ge(stored[u], 16 * i + 16)
                    for j in range(J):
                        dve.wait_ge(o_full, ogroups + (2 * J + j + 1))
                        nc.vector.tensor_tensor(out_sb[:, u, j, :], o_ps[:, j % O_BANKS, 0:D], b2_sb[:, bass.ds(e, 1), :].rearrange("p a d -> p (a d)"), ALU.add).then_inc(o_ready, 1)


def combine(nc, prefix, x1, eo, slots, weight, x2, last_slot):
    NT = TOKEN_TILES
    G = 4
    GROUPS = NT // G
    with ExitStack() as stack:
        s = Scope(nc, stack, prefix)
        xt = s.sbuf("xt", [P, 2, G, D])
        y = s.sbuf("y", [P, 2, G, D])
        inside = s.sbuf("inside", [P, NT], I32)
        inside_now = s.sbuf("inside_now", [P, 2, G], I32)
        spare_p = s.sbuf("spare_p", [P, 1])
        stats = s.sbuf("stats", [P, G, 6])
        mv = s.sbuf("mv", [P, G, 2])
        rstd = s.sbuf("rstd", [P, G])
        spare = s.sbuf("spare", [P, 1])
        eps_sb = s.sbuf("eps", [P, 1])

        eps_ready = s.sem("eps_ready")
        inside_ready = s.sem("inside_ready")
        now_ready = s.sem("now_ready")
        gathered = [s.sem(f"gathered{u}") for u in range(2)]
        x_in = [s.sem(f"x_in{u}") for u in range(2)]
        summed = s.sem("summed")
        stat_step = s.sem("stat_step")
        var_ready = s.sem("var_ready")
        std_ready = s.sem("std_ready")
        rstd_ready = s.sem("rstd_ready")
        normed = s.sem("normed")
        stored = [s.sem(f"stored{u}") for u in range(2)]

        block = stack.enter_context(nc.Block())

        @block.sync
        def _(sp):
            x_v = x1.rearrange("(i p) d -> p i d", p=P)
            for g in range(2):
                sp.dma_start(xt[:, g, :, :], x_v[:, g * G:(g + 1) * G, :]).then_inc(x_in[g], 16)
            with sp.Fori(1, GROUPS // 2) as i:
                for u in range(2):
                    sp.wait_ge(stored[u], 16 * i)
                    sp.dma_start(xt[:, u, :, :], x_v[:, bass.ds((2 * i + u) * G, G), :]).then_inc(x_in[u], 16)

        @block.gpsimd
        def _(pool):
            nc.gpsimd.memset(eps_sb[:], EPS).then_inc(eps_ready, 1)
            nc.gpsimd.tensor_scalar(inside[:], slots[:], float(last_slot), None, ALU.min).then_inc(inside_ready, 1)
            pool.wait_ge(inside_ready, 1)
            pool.wait_ge(eps_ready, 1)
            with pool.Fori(0, GROUPS // 2) as i:
                for u in range(2):
                    pool.wait_ge(summed, 2 * i + (u + 1))
                    nc.gpsimd.tensor_copy(inside_now[:, u, :], inside[:, bass.ds((2 * i + u) * G, G)]).then_inc(now_ready, 1)
                    pool.wait_ge(now_ready, 2 * i + (u + 1))
                    nc.gpsimd.tensor_tensor(spare_p[:], eps_sb[:], eps_sb[:], ALU.add)
                    for j in range(G):
                        nc.gpsimd.indirect_dma_start(y[:, u, j, :], None, eo[:],
                                                     bass.IndirectOffsetOnAxis(ap=inside_now[:, u, j:j + 1], axis=0)).then_inc(gathered[u], 16)

        @block.scalar
        def _(act):
            act.wait_ge(eps_ready, 1)
            with act.Fori(0, GROUPS // 2) as i:
                for u in range(2):
                    g = act.snap(2 * i + u)
                    act.wait_ge(var_ready, g + 1)
                    nc.scalar.activation(rstd[:], mv[:, :, 1], ACT.Sqrt, bias=eps_sb[:]).then_inc(std_ready, 1)
                    act.wait_ge(normed, g + 1)
                    act.dma_start(x2.rearrange("(i p) d -> p i d", p=P)[:, bass.ds(g * G, G), :], xt[:, u, :, :]).then_inc(stored[u], 16)
            for u in range(2):
                act.wait_ge(stored[u], 8 * GROUPS)

        @block.vector
        def _(dve):
            dve.sem_inc(summed, 2)
            with dve.Fori(0, GROUPS // 2) as i:
                for u in range(2):
                    g = dve.snap(2 * i + u)
                    rows = xt[:, u, :, :]
                    dve.wait_ge(x_in[u], i * 16 + 16)
                    dve.wait_ge(gathered[u], i * (16 * G) + 16 * G)
                    for j in range(G):
                        ins = nc.vector.scalar_tensor_tensor(out=rows[:, j, :], in0=y[:, u, j, :], scalar=weight[:, bass.ds(g * G + j, 1)],
                                                             in1=rows[:, j, :], op0=ALU.mult, op1=ALU.add)
                    ins.then_inc(summed, 1)
                    dve.wait_ge(summed, g + 3)
                    layernorm_tiles(nc, dve, rows, stats, mv, rstd, spare, G, g + 1, stat_step, var_ready, std_ready, rstd_ready, normed)
                    dve.wait_ge(normed, g + 1)

def sorted_experts(nc, x3, slot_table, tile_expert, w, b, eo):
    E, J = EXPERTS, SLOT_TILES
    with ExitStack() as stack:
        s = Scope(nc, stack, "top1")
        ident = s.sbuf("ident", [P, P])
        w_sb = s.sbuf("w", [P, KD, E * D])
        b_sb = s.sbuf("b", [1, E * D])
        one_row = s.sbuf("one_row", [1, P])
        ids = s.sbuf("ids", [P, J], I32)
        ids_now = s.sbuf("ids_now", [P, 2, 2], I32)
        spare = s.sbuf("spare", [P, 1])
        xg = s.sbuf("xg", [P, 2, D])
        xT = s.sbuf("xT", [P, 2, D])
        out_sb = s.sbuf("out", [P, J, D])
        t_ps = s.psum("t", [P, 2, BANK])
        o_ps = s.psum("o", [P, 2, BANK])

        zeroed = s.sem("zeroed")
        ident_ready = s.sem("ident_ready")
        ones_ready = s.sem("ones_ready")
        ids_in = s.sem("ids_in")
        w_in = s.sem("w_in")
        ids_ready = s.sem("ids_ready")
        gathered = [s.sem(f"gathered{u}") for u in range(2)]
        turned = s.sem("turned")
        xT_ready = s.sem("xT_ready")
        o_full = s.sem("o_full")
        o_ready = s.sem("o_ready")
        stored = s.sem("stored")
        block = stack.enter_context(nc.Block())

        @block.sync
        def _(sp):
            sp.dma_start(ids[:], slot_table[0:P * J, :].rearrange("(p j) a -> p (j a)", p=P)).then_inc(ids_in, 16)
            sp.dma_start(w_sb[:].rearrange("p k (e d) -> p k e d", e=E)[:, 0], w.rearrange("e (k p) d -> k p e d", p=P)[0]).then_inc(w_in, 16)
            sp.dma_start(w_sb[:].rearrange("p k (e d) -> p k e d", e=E)[:, 1], w.rearrange("e (k p) d -> k p e d", p=P)[1]).then_inc(w_in, 16)
            sp.dma_start(b_sb[:], b.rearrange("(a e) d -> a (e d)", a=1)).then_inc(w_in, 16)
            sp.wait_ge(o_ready, J + 2)
            sp.dma_start(eo.rearrange("(p j) d -> p j d", p=P), out_sb[:]).then_inc(stored, 16)
            sp.wait_ge(stored, 16)

        @block.gpsimd
        def _(pool):
            make_identity(nc, s, ident, pool, zeroed, ident_ready)
            nc.gpsimd.memset(one_row[:], 1.0).then_inc(ones_ready, 1)
            pool.wait_ge(ids_in, 16)
            pool.wait_ge(ident_ready, 1)
            with pool.Fori(0, J // 2) as i:
                for u in range(2):
                    pool.wait_ge(turned, 2 * i + (u + 1))
                    nc.gpsimd.tensor_copy(ids_now[:, u, 0:1], ids[:, bass.ds(2 * i + u, 1)]).then_inc(ids_ready, 1)
                    pool.wait_ge(ids_ready, 2 * i + (u + 1))
                    nc.gpsimd.tensor_tensor(spare[:], ident[:, 0:1], ident[:, 0:1], ALU.add)
                    nc.gpsimd.indirect_dma_start(xg[:, u, :], None, x3[:],
                                                 bass.IndirectOffsetOnAxis(ap=ids_now[:, u, 0:1], axis=0)).then_inc(gathered[u], 16)

        @block.scalar
        def _(act):
            with act.Fori(0, J // 2) as i:
                for u in range(2):
                    act.wait_ge(turned, 2 * i + (u + 3))
                    act.wait_ge(o_full, 2 * i + (u + 1))
                    nc.scalar.activation(xT[:, u, :], t_ps[:, u, 0:D], ACT.Copy).then_inc(xT_ready, 1)

        @block.tensor
        def _(pe):
            pe.wait_ge(ident_ready, 1)
            pe.wait_ge(ones_ready, 1)
            pe.wait_ge(w_in, 48)
            with pe.Fori(0, J // 2) as i:
                for u in range(2):
                    pe.wait_ge(gathered[u], 16 * i + 16)
                    pe.wait_ge(xT_ready, 2 * i + (u + 1))
                    for k in range(KD):
                        ins = nc.tensor.transpose(t_ps[:, u, k * P:(k + 1) * P], xg[:, u, k * P:(k + 1) * P], ident[:])
                    ins.then_inc(turned, 1)
                for u in range(2):
                    first = pe.value_load(tile_expert[0:1, bass.ds(2 * i + u, 1)], min_val=0, max_val=E - 1) * D
                    pe.wait_ge(xT_ready, 2 * i + (u + 3))
                    pe.wait_ge(o_ready, 2 * i + (u + 1))
                    for k in range(KD):
                        nc.tensor.matmul(o_ps[:, u, 0:D], xT[:, u, k * P:(k + 1) * P], w_sb[:, k, bass.ds(first, D)], start=(k == 0), stop=False)
                    nc.tensor.matmul(o_ps[:, u, 0:D], one_row[:], b_sb[:, bass.ds(first, D)], start=False, stop=True).then_inc(o_full, 1)

        @block.vector
        def _(dve):
            dve.sem_inc(turned, 2)
            dve.sem_inc(xT_ready, 2)
            dve.sem_inc(o_full, 2)
            dve.sem_inc(o_ready, 2)
            with dve.Fori(0, J // 2) as i:
                for u in range(2):
                    dve.wait_ge(o_full, 2 * i + (u + 3))
                    nc.vector.tensor_copy(out_sb[:, bass.ds(2 * i + u, 1), :].rearrange("p a d -> p (a d)"), o_ps[:, u, 0:D]).then_inc(o_ready, 1)


def retention_tables(nc, freqs, gamma, cos_t, decay_t, undo_t):
    HEAD = freqs.shape[1]
    M = freqs.shape[0] * HEAD // P
    HB = P // HEAD
    PI = 3.141592653589793
    MAGIC = 12582912.0
    parts, rest = [], 2 * PI
    for bits in (5, 14, 22):
        parts.append(int(rest * 2 ** bits) / 2 ** bits)
        rest -= parts[-1]
    parts.append(rest)
    with ExitStack() as stack:
        s = Scope(nc, stack, "tab")
        time_i = s.sbuf("time_i", [P, T], I32)
        time = s.sbuf("time", [P, T])
        freq_sb = s.sbuf("freq", [P, M])
        gam = s.sbuf("gam", [P, M])
        half_pi = s.sbuf("half_pi", [P, 1])
        angle = s.sbuf("angle", [P, 2, T])
        turns = s.sbuf("turns", [P, T])
        decay = s.sbuf("decay", [P, 2, T])
        undo = s.sbuf("undo", [P, 2, T])

        consts_in = s.sem("consts_in")
        filled = s.sem("filled")
        time_ready = s.sem("time_ready")
        gam_ready = s.sem("gam_ready")
        log_ready = s.sem("log_ready")
        step = s.sem("step")
        reduced = s.sem("reduced")
        folded = s.sem("folded")
        cos_ready = s.sem("cos_ready")
        decay_ready = s.sem("decay_ready")
        undo_ready = s.sem("undo_ready")
        stored = s.sem("stored")
        block = stack.enter_context(nc.Block())

        @block.sync
        def _(sp):
            sp.dma_start(freq_sb[:], freqs.rearrange("(m h) d -> (h d) m", m=M), allow_slow_non_contiguous=True).then_inc(consts_in, 16)
            for h in range(HB):
                src = gamma.rearrange("(m h) a b -> h (m a b)", m=M)[h]
                sp.dma_start(gam[h * HEAD:(h + 1) * HEAD, :], src.partition_broadcast(HEAD), allow_slow_non_contiguous=True).then_inc(consts_in, 16)
            for m in range(M):
                sp.wait_ge(decay_ready, m + 1)
                sp.dma_start(decay_t[m], decay[:, m % 2, :]).then_inc(stored, 16)
                sp.wait_ge(undo_ready, m + 1)
                sp.dma_start(undo_t[m], undo[:, m % 2, :]).then_inc(stored, 16)
                sp.wait_ge(cos_ready, m + 1)
                sp.dma_start(cos_t[m], angle[:, m % 2, :]).then_inc(stored, 16)
                sp.wait_ge(stored, 48 * (m + 1))

        @block.gpsimd
        def _(pool):
            nc.gpsimd.memset(half_pi[:], PI / 2).then_inc(filled, 1)
            nc.gpsimd.iota(time_i[:], pattern=[[1, T]], base=0, channel_multiplier=0).then_inc(filled, 1)

        @block.scalar
        def _(act):
            act.wait_ge(gam_ready, 1)
            nc.scalar.activation(gam[:], gam[:], ACT.Ln).then_inc(log_ready, 1)
            act.wait_ge(time_ready, 1)
            act.wait_ge(log_ready, 1)
            for m in range(M):
                if m >= 2:
                    act.wait_ge(stored, 48 * (m - 1))
                nc.scalar.activation(decay[:, m % 2, :], time[:], ACT.Exp, scale=gam[:, m:m + 1]).then_inc(decay_ready, 1)
                act.wait_ge(reduced, m + 1)
                nc.scalar.activation(angle[:, m % 2, :], angle[:, m % 2, :], ACT.Abs).then_inc(folded, 1)
                act.wait_ge(folded, m + 1)
                nc.scalar.activation(angle[:, m % 2, :], angle[:, m % 2, :], ACT.Sin, bias=half_pi[:], scale=-1.0).then_inc(cos_ready, 1)

        @block.vector
        def _(dve):
            done = [0]

            def after(ins):
                ins.then_inc(step, 1)
                done[0] += 1
                dve.wait_ge(step, done[0])

            v = nc.vector
            dve.wait_ge(filled, 2)
            v.tensor_copy(time[:], time_i[:]).then_inc(time_ready, 1)
            dve.wait_ge(consts_in, 16 * (1 + HB))
            v.tensor_scalar(gam[:], gam[:], 2.0 ** -64, None, ALU.max).then_inc(gam_ready, 1)
            dve.wait_ge(time_ready, 1)
            for m in range(M):
                r = angle[:, m % 2, :]
                if m >= 2:
                    dve.wait_ge(stored, 48 * (m - 1))
                after(v.tensor_scalar(r, time[:], freq_sb[:, m:m + 1], None, ALU.mult))
                after(v.tensor_scalar(turns[:], r, 1.0 / (2 * PI), MAGIC, ALU.mult, ALU.add))
                after(v.tensor_scalar(turns[:], turns[:], MAGIC, -1.0, ALU.subtract, ALU.mult))
                for k, part in enumerate(parts):
                    ins = v.scalar_tensor_tensor(out=r, in0=turns[:], scalar=float(part), in1=r, op0=ALU.mult, op1=ALU.add)
                    if k < len(parts) - 1:
                        after(ins)
                ins.then_inc(reduced, 1)
                dve.wait_ge(reduced, m + 1)
                dve.wait_ge(decay_ready, m + 1)
                after(v.tensor_scalar(undo[:, m % 2, :], decay[:, m % 2, :], 1e-6, None, ALU.add))
                v.reciprocal(undo[:, m % 2, :], undo[:, m % 2, :]).then_inc(undo_ready, 1)


def retention_layer(nc, x2, conv_w, conv_b, qk_w, v_w, g_w, g_b, o_w, ln_g, ln_b, cos_t, decay_t, undo_t, x3):
    E = qk_w.shape[1]
    M = E // P
    HEAD = 32
    TAPS = 4
    CH = BANK
    Q = T // CH
    G = CH // P
    with ExitStack() as stack:
        s = Scope(nc, stack, "ret")
        ident = s.sbuf("ident", [P, P])
        heads = s.sbuf("heads", [P, P])
        qk_sb = s.sbuf("qk_w", [P, KD, E])
        v_sb = s.sbuf("v_w", [P, KD, E])
        g_sb = s.sbuf("g_w", [P, KD, E])
        o_sb = s.sbuf("o_w", [P, M, D])
        gb_sb = s.sbuf("gb", [P, M])
        cw_sb = s.sbuf("cw", [P, KD, TAPS])
        cb_sb = s.sbuf("cb", [P, KD])
        lng_sb = s.sbuf("lng", [P, D])
        lnb_sb = s.sbuf("lnb", [P, D])
        eps_sb = s.sbuf("eps", [P, 1])
        xt = s.sbuf("xt", [P, 2, G, D])
        xpad = s.sbuf("xpad", [P, 2, KD, TAPS - 1 + CH])
        xc = s.sbuf("xc", [P, 2, KD, CH])
        qk = s.sbuf("qk", [P, 2, M, CH])
        val = s.sbuf("val", [P, 2, M, CH])
        gate = s.sbuf("gate", [P, 2, M, CH])
        norm = s.sbuf("norm", [P, M, CH])
        q = s.sbuf("q", [P, 2, M, CH + 1])
        mem = s.sbuf("mem", [P, M, CH])
        mem_last = s.sbuf("mem_last", [P, M])
        ones = s.sbuf("ones", [P, CH])
        o_in = s.sbuf("o_in", [P, M, CH])
        cos_sb = s.sbuf("cos", [P, 2, M, CH])
        decay_sb = s.sbuf("decay", [P, 2, M, CH])
        undo_sb = s.sbuf("undo", [P, 2, M, CH])
        z = s.sbuf("z", [P, G, D])
        stats = s.sbuf("stats", [P, G, 6])
        mv = s.sbuf("mv", [P, G, 2])
        rstd = s.sbuf("rstd", [P, G])
        spare = s.sbuf("spare", [P, 1])

        t_ps = s.psum("t", [P, KD, CH])
        q_ps = s.psum("q_ps", [P, CH])
        v_ps = s.psum("v_ps", [P, CH])
        g_ps = s.psum("g_ps", [P, CH])
        n_ps = s.psum("n_ps", [P, CH])
        o_ps = s.psum("o_ps", [P, G, D])

        consts_in = s.sem("consts_in")
        filled = s.sem("filled")
        x_in = [s.sem(f"x_in{u}") for u in range(2)]
        tab_in = [s.sem(f"tab_in{u}") for u in range(2)]
        turned = s.sem("turned")
        xpad_ready = s.sem("xpad_ready")
        conv_step = s.sem("conv_step")
        xc_ready = s.sem("xc_ready")
        q_full = s.sem("q_full")
        v_full = s.sem("v_full")
        g_full = s.sem("g_full")
        qk_ready = s.sem("qk_ready")
        val_ready = s.sem("val_ready")
        gate_ready = s.sem("gate_ready")
        squared = s.sem("squared")
        n_full = s.sem("n_full")
        norm_ready = s.sem("norm_ready")
        inv_step = s.sem("inv_step")
        q_ready = s.sem("q_ready")
        phase_ready = s.sem("phase_ready")
        gated = s.sem("gated")
        undo_ready = s.sem("undo_ready")
        mem_step = s.sem("mem_step")
        o_in_ready = s.sem("o_in_ready")
        o_full = s.sem("o_full")
        z_done = s.sem("z_done")
        z_step = s.sem("z_step")
        stat_step = s.sem("stat_step")
        var_ready = s.sem("var_ready")
        std_ready = s.sem("std_ready")
        rstd_ready = s.sem("rstd_ready")
        normed = s.sem("normed")
        x_biased = s.sem("x_biased")
        stored = [s.sem(f"stored{u}") for u in range(2)]

        loads = [
            (qk_sb[:], qk_w.rearrange("(k p) e -> p k e", p=P)),
            (v_sb[:], v_w.rearrange("(k p) e -> p k e", p=P)),
            (g_sb[:], g_w.rearrange("(k p) e -> p k e", p=P)),
            (o_sb[:], o_w.rearrange("(m p) d -> p m d", p=P)),
            (gb_sb[:], g_b.rearrange("(m p) -> p m", p=P)),
            (cw_sb[:], conv_w.rearrange("(k p) a t -> p k (a t)", p=P)),
            (cb_sb[:], conv_b.rearrange("(k p) -> p k", p=P)),
            (lng_sb[:], ln_g.rearrange("(a d) -> a d", a=1).partition_broadcast(P)),
            (lnb_sb[:], ln_b.rearrange("(a d) -> a d", a=1).partition_broadcast(P)),
        ]
        ALL_IN = 16 * len(loads)
        FILLS = 4
        block = stack.enter_context(nc.Block())

        @block.sync
        def _(sp):
            for dst, src in loads:
                sp.dma_start(dst, src, allow_slow_non_contiguous=True).then_inc(consts_in, 16)
            x_v = x2.rearrange("(i p) d -> p i d", p=P)
            with sp.Fori(0, B) as b:
                for c in range(Q):
                    u = c % 2
                    sp.wait_ge(stored[u], (16 * Q // 2) * b + 16 * (c // 2 + 1))
                    sp.dma_start(xt[:, u, :, :], x_v[:, bass.ds(b * (T // P) + c * G, G), :]).then_inc(x_in[u], 16)
                    sp.wait_ge(o_in_ready, b * Q + (c + 1))
                    for dst, src in ((cos_sb, cos_t), (decay_sb, decay_t), (undo_sb, undo_t)):
                        sp.dma_start(dst[:, u, :, :], src.rearrange("m p t -> p m t")[:, :, c * CH:(c + 1) * CH]).then_inc(tab_in[u], 16)

        @block.gpsimd
        def _(pool):
            fills = [(ident[:], 0.0), (heads[:], 0.0), (eps_sb[:], EPS), (ones[:], 1.0)]
            for k, (dst, value) in enumerate(fills):
                nc.gpsimd.memset(dst, value).then_inc(filled, 1)
                pool.wait_ge(filled, k + 1)
            nc.gpsimd.affine_select(out=ident[:], in_=ident[:], compare_op=ALU.not_equal, fill=1.0, base=0,
                                    pattern=[[-1, P]], channel_multiplier=1).then_inc(filled, 1)
            for h in range(P // HEAD):
                nc.gpsimd.memset(heads[h * HEAD:(h + 1) * HEAD, h * HEAD:(h + 1) * HEAD], 1.0).then_inc(filled, 1)
                pool.wait_ge(filled, FILLS + 2 + h)
            pool.wait_ge(consts_in, ALL_IN)
            with pool.Fori(0, B) as b:
                for c in range(Q):
                    u = c % 2
                    n = b * Q + (c + 1)
                    pool.wait_ge(qk_ready, M * n + 1)
                    pool.wait_ge(q_ready, n)
                    nc.gpsimd.tensor_tensor(norm[:], qk[:, u, :, :], qk[:, u, :, :], ALU.mult).then_inc(squared, 1)
                    pool.wait_ge(x_in[u], (16 * Q // 2) * b + 16 * (c // 2 + 1))
                    pool.wait_ge(turned, n)
                    nc.gpsimd.tensor_tensor(xt[:, u, :, :], xt[:, u, :, :], lnb_sb[:].unsqueeze(1).broadcast_to([P, G, D]), ALU.add).then_inc(x_biased, 1)
                    pool.wait_ge(tab_in[u], (48 * Q // 2) * b + 48 * (c // 2 + 1))
                    pool.wait_ge(gate_ready, M * n + 1)
                    nc.gpsimd.tensor_tensor(gate[:, u, :, :], gate[:, u, :, :], decay_sb[:, u, :, :], ALU.mult).then_inc(gated, 1)
                    pool.wait_ge(q_ready, n + 1)
                    nc.gpsimd.tensor_tensor(cos_sb[:, u, :, :], cos_sb[:, u, :, :], q[:, u, :, 0:CH], ALU.add).then_inc(phase_ready, 1)
                    nc.gpsimd.tensor_tensor(undo_sb[:, u, :, :], undo_sb[:, u, :, :], q[:, u, :, 1:CH + 1], ALU.mult).then_inc(undo_ready, 1)

        @block.scalar
        def _(act):
            act.wait_ge(consts_in, ALL_IN)
            with act.Fori(0, B) as b:
                for c in range(Q + 1):
                    u = c % 2
                    n = b * Q + (c + 1)
                    if c < Q:
                        act.wait_ge(turned, n)
                        act.wait_ge(xc_ready, n)
                        nc.scalar.activation(xpad[:, u, :, TAPS - 1:], t_ps[:], ACT.Copy).then_inc(xpad_ready, 1)
                        act.wait_ge(o_in_ready, n)
                        for m in range(M):
                            k = (b * Q + c) * M + (m + 1)
                            act.wait_ge(q_full, k)
                            nc.scalar.activation(qk[:, u, m, :], q_ps[:], ACT.Copy).then_inc(qk_ready, 1)
                            act.wait_ge(g_full, k)
                            nc.scalar.activation(gate[:, u, m, :], g_ps[:], ACT.Sigmoid, bias=gb_sb[:, m:m + 1]).then_inc(gate_ready, 1)
                            act.wait_ge(v_full, k)
                            nc.scalar.activation(val[:, u, m, :], v_ps[:], ACT.Copy).then_inc(val_ready, 1)
                    if c:
                        for r in range(2):
                            act.wait_ge(var_ready, (b * Q + c) * 2 + (r - 1))
                            nc.scalar.activation(rstd[:], mv[:, :, 1], ACT.Sqrt, bias=eps_sb[:]).then_inc(std_ready, 1)
                    if c < Q:
                        for m in range(M):
                            act.wait_ge(n_full, (b * Q + c) * M + (m + 1))
                            nc.scalar.activation(norm[:, m, :], n_ps[:], ACT.Sqrt).then_inc(norm_ready, 1)
                    if c:
                        v = (c - 1) % 2
                        act.wait_ge(normed, b * Q + c)
                        act.dma_start(x3.rearrange("(i p) d -> p i d", p=P)[:, bass.ds(b * (T // P) + (c - 1) * G, G), :], xt[:, v, :, :]).then_inc(stored[v], 16)
            for u in range(2):
                act.wait_ge(stored[u], 16 * (B * Q // 2 + 1))

        @block.tensor
        def _(pe):
            pe.wait_ge(consts_in, ALL_IN)
            pe.wait_ge(filled, FILLS + 1 + P // HEAD)
            with pe.Fori(0, B) as b:
                for c in range(Q + 1):
                    u = c % 2
                    n = b * Q + (c + 1)
                    if c < Q:
                        pe.wait_ge(x_in[u], (16 * Q // 2) * b + 16 * (c // 2 + 1))
                        pe.wait_ge(xpad_ready, n)
                        for j in range(G):
                            for k in range(KD):
                                ins = nc.tensor.transpose(t_ps[:, k, j * P:(j + 1) * P], xt[:, u, j, k * P:(k + 1) * P], ident[:])
                        ins.then_inc(turned, 1)
                        pe.wait_ge(xc_ready, n + 2)
                        for m in range(M):
                            k1 = (b * Q + c) * M + (m + 1)
                            for w, ps, free, full in ((qk_sb, q_ps, qk_ready, q_full), (g_sb, g_ps, gate_ready, g_full),
                                                      (v_sb, v_ps, val_ready, v_full)):
                                pe.wait_ge(free, k1)
                                for k in range(KD):
                                    ins = nc.tensor.matmul(ps[:], w[:, k, m * P:(m + 1) * P], xc[:, u, k, :], start=(k == 0), stop=(k == KD - 1))
                                ins.then_inc(full, 1)
                    if c:
                        pe.wait_ge(o_in_ready, n + 1)
                        pe.wait_ge(z_done, n - 1)
                        for j in range(G):
                            for m in range(M):
                                ins = nc.tensor.matmul(o_ps[:, j, :], o_in[:, m, j * P:(j + 1) * P], o_sb[:, m, :], start=(m == 0), stop=(m == M - 1))
                        ins.then_inc(o_full, 1)
                    if c < Q:
                        pe.wait_ge(squared, n)
                        for m in range(M):
                            k1 = (b * Q + c) * M + (m + 1)
                            pe.wait_ge(norm_ready, k1)
                            nc.tensor.matmul(n_ps[:], heads[:], norm[:, m, :], start=True, stop=True).then_inc(n_full, 1)

        @block.vector
        def _(dve):
            for sem, count in ((stored[0], 16), (stored[1], 16), (xpad_ready, 1), (xc_ready, 2), (qk_ready, 1), (gate_ready, 1),
                               (val_ready, 1), (norm_ready, 1), (o_in_ready, 2), (q_ready, 1), (o_full, 1), (z_done, 1)):
                dve.sem_inc(sem, count)
            dve.wait_ge(consts_in, ALL_IN)
            dve.wait_ge(filled, FILLS + 1 + P // HEAD)
            v = nc.vector
            with dve.Fori(0, B) as b:
                ahead = [int(c == 0) + int(c < Q - 1) for c in range(Q)]
                CONV = TAPS * KD - 1
                convs = dve.snap(b * (Q * CONV + sum(ahead)))
                invs = dve.snap(b * (Q * 2))
                mems = dve.snap(b * (Q * 4))

                def convolve(c, u, n):
                    if c == 0:
                        v.memset(xpad[:, u, :, 0:TAPS - 1], 0.0).then_inc(conv_step, 1)
                    dve.wait_ge(xpad_ready, n + 1)
                    if c < Q - 1:
                        v.tensor_copy(xpad[:, 1 - u, :, 0:TAPS - 1], xpad[:, u, :, CH:CH + TAPS - 1]).then_inc(conv_step, 1)
                    first = convs + (c * CONV + sum(ahead[:c + 1]))
                    for t in range(TAPS):
                        for k in range(KD):
                            src = xpad[:, u, k, t:t + CH]
                            dst = xc[:, u, k, :]
                            if t == 0:
                                dve.wait_ge(conv_step, first)
                                ins = v.tensor_scalar(dst, src, cw_sb[:, k, 0:1], cb_sb[:, k:k + 1], ALU.mult, ALU.add)
                            else:
                                dve.wait_ge(conv_step, first + ((t - 1) * KD + k + 1))
                                ins = v.scalar_tensor_tensor(out=dst, in0=src, scalar=cw_sb[:, k, t:t + 1], in1=dst, op0=ALU.mult, op1=ALU.add)
                            ins.then_inc(xc_ready if t == TAPS - 1 and k == KD - 1 else conv_step, 1)

                for c in range(Q + 1):
                    u = c % 2
                    n = dve.snap(b * Q + (c + 1))
                    if c < Q:
                        convolve(c, u, n)
                    if c:
                        rows = xt[:, 1 - u, :, :]
                        dve.wait_ge(o_full, n)
                        layernorm_tiles(nc, dve, o_ps, stats, mv, rstd, spare, G, 2 * n - 3, stat_step, var_ready, std_ready,
                                        rstd_ready, z_done, z)
                        dve.wait_ge(z_done, n)
                        v.tensor_tensor(z[:], z[:], lng_sb[:].unsqueeze(1).broadcast_to([P, G, D]), ALU.mult).then_inc(z_step, 1)
                        dve.wait_ge(z_step, 2 * n - 3)
                        dve.wait_ge(x_biased, n - 1)
                        v.tensor_tensor(rows, rows, z[:], ALU.add).then_inc(z_step, 1)
                        dve.wait_ge(z_step, 2 * n - 2)
                        layernorm_tiles(nc, dve, rows, stats, mv, rstd, spare, G, 2 * n - 2, stat_step, var_ready, std_ready,
                                        rstd_ready, normed)
                        dve.wait_ge(normed, n - 1)
                    if c < Q:
                        if c == 0:
                            v.memset(q[:, u, :, 0:1], 0.0)
                            v.memset(mem_last[:], 0.0).then_inc(mem_step, 1)
                        else:
                            dve.wait_ge(q_ready, n)
                            v.tensor_copy(q[:, u, :, 0:1], q[:, 1 - u, :, CH:CH + 1])
                        dve.wait_ge(norm_ready, M * n + 1)
                        v.tensor_scalar(norm[:], norm[:], 1e-12, None, ALU.max).then_inc(inv_step, 1)
                        dve.wait_ge(inv_step, invs + (2 * c + 1))
                        v.reciprocal(norm[:], norm[:]).then_inc(inv_step, 1)
                        dve.wait_ge(inv_step, invs + (2 * c + 2))
                        v.tensor_tensor(q[:, u, :, 1:CH + 1], qk[:, u, :, :], norm[:], ALU.mult).then_inc(q_ready, 1)
                        dve.wait_ge(phase_ready, n)
                        dve.wait_ge(val_ready, M * n + 1)
                        v.tensor_tensor(mem[:], cos_sb[:, u, :, :], val[:, u, :, :], ALU.mult).then_inc(mem_step, 1)
                        dve.wait_ge(mem_step, mems + (4 * c + 2))
                        dve.wait_ge(gated, n)
                        v.tensor_tensor(mem[:], mem[:], gate[:, u, :, :], ALU.mult).then_inc(mem_step, 1)
                        dve.wait_ge(mem_step, mems + (4 * c + 3))
                        for m in range(M):
                            ins = v.tensor_tensor_scan(mem[:, m, :], ones[:], mem[:, m, :], mem_last[:, m:m + 1], ALU.mult, ALU.add)
                        ins.then_inc(mem_step, 1)
                        dve.wait_ge(mem_step, mems + (4 * c + 4))
                        if c < Q - 1:
                            v.tensor_copy(mem_last[:], mem[:, :, CH - 1]).then_inc(mem_step, 1)
                        dve.wait_ge(undo_ready, n)
                        dve.wait_ge(o_full, n)
                        v.tensor_tensor(o_in[:], mem[:], undo_sb[:, u, :, :], ALU.mult).then_inc(o_in_ready, 1)


def program(nc, a, out):
    x1, x2, x3 = (nc.dram_tensor(name, [N, D], F32) for name in ("x1", "x2", "x3"))
    state_space_layer(nc, a["x_tok"], a["x_feat"], a["L0_attn_Win"], a["L0_attn_b_in"], a["L0_attn_A_log"],
                      a["L0_attn_B_param"], a["L0_attn_C_param"], a["L0_attn_Wdt"], a["L0_attn_b_dt"],
                      a["L0_attn_Wconv"], a["L0_attn_Wout"], a["L0_attn_b_out"], x1)
    capacity = max(-(-3 * N // (2 * EXPERTS)), 1)
    slot_table = nc.dram_tensor("slot_table", [EXPERTS * capacity + N, 1], I32)
    eo = nc.dram_tensor("eo", [EXPERTS * capacity, D], F32)
    with ExitStack() as stack:
        s = Scope(nc, stack, "moe")
        slots = s.sbuf("slots", [P, TOKEN_TILES], I32)
        weight = s.sbuf("weight", [P, TOKEN_TILES])
        route(nc, "route", x1, a["L0_ffn_router_w"], None, slot_table, slots, weight, capacity)
        capacity_experts(nc, x1, slot_table, a["L0_ffn_w1"], a["L0_ffn_b1"], a["L0_ffn_w2"], a["L0_ffn_b2"], eo, capacity)
        combine(nc, "comb", x1, eo, slots, weight, x2, EXPERTS * capacity - 1)
    H, HD = a["L1_attn_freqs"].shape
    cos_t, decay_t, undo_t = (nc.dram_tensor(name, [H * HD // P, P, T], F32) for name in ("cos_t", "decay_t", "undo_t"))
    retention_tables(nc, a["L1_attn_freqs"], a["L1_attn_gamma"], cos_t, decay_t, undo_t)
    retention_layer(nc, x2, a["L1_attn_conv_w"], a["L1_attn_conv_b"], a["L1_attn_qk_w"], a["L1_attn_v_w"],
                    a["L1_attn_g_w"], a["L1_attn_g_b"], a["L1_attn_o_w"], a["L1_attn_ln_g"], a["L1_attn_ln_b"],
                    cos_t, decay_t, undo_t, x3)
    slot_table2 = nc.dram_tensor("slot_table2", [P * SLOT_TILES, 1], I32)
    eo2 = nc.dram_tensor("eo2", [P * SLOT_TILES, D], F32)
    with ExitStack() as stack:
        s = Scope(nc, stack, "moe2")
        slots = s.sbuf("slots", [P, TOKEN_TILES], I32)
        weight = s.sbuf("weight", [P, TOKEN_TILES])
        tile_expert = s.sbuf("tile_expert", [1, SLOT_TILES], I32)
        route(nc, "route2", x3, a["L1_ffn_router_w"], a["L1_ffn_router_b"], slot_table2, slots, weight, None, tile_expert)
        sorted_experts(nc, x3, slot_table2, tile_expert, a["L1_ffn_expert_w"], a["L1_ffn_expert_b"], eo2)
        combine(nc, "comb2", x3, eo2, slots, weight, out, P * SLOT_TILES - 1)


TRANSPOSED = ["L0_attn_Win", "L0_attn_Wdt", "L0_attn_Wout", "L0_ffn_router_w", "L1_attn_qk_w", "L1_attn_v_w",
              "L1_attn_g_w", "L1_attn_o_w", "L1_ffn_router_w"]


def kernel(**inputs):
    import numpy as np
    import concourse.bacc as bacc
    from concourse.bass_utils import run_bass_kernel_spmd

    arrays = {}
    for name, value in inputs.items():
        value = np.asarray(value)
        if name == "L0_attn_input":
            tokens = value.reshape(N, D)
            arrays["x_tok"] = np.ascontiguousarray(tokens)
            arrays["x_feat"] = np.ascontiguousarray(tokens.T)
        elif name in TRANSPOSED:
            arrays[name] = np.ascontiguousarray(value.T)
        elif name == "L1_ffn_expert_w":
            arrays[name] = np.ascontiguousarray(value.transpose(0, 2, 1))
        else:
            arrays[name] = np.ascontiguousarray(value)
    nc = bacc.Bacc("TRN2", target_bir_lowering=False, num_devices=1)
    a = {n: nc.dram_tensor(f"in_{n}", v.shape, mybir.dt.from_np(v.dtype), kind="ExternalInput").ap() for n, v in arrays.items()}
    out = nc.dram_tensor("out", (N, D), F32, kind="ExternalOutput").ap()
    program(nc, a, out)
    r = run_bass_kernel_spmd(nc, [{f"in_{n}": v for n, v in arrays.items()}], core_ids=[0])
    return r.results[0]["out"].reshape(B, T, D)
```

```python
from contextlib import ExitStack

import concourse.bass as bass
from concourse import mybir

F32 = mybir.dt.float32
BF16 = mybir.dt.bfloat16
I32 = mybir.dt.int32
U32 = mybir.dt.uint32
ALU = mybir.AluOpType
ACT = mybir.ActivationFunctionType
AX = mybir.AxisListType

P = 128
B, T, D = 2, 2048, 256
N = B * T
KD = D // P
EPS = 1e-5
BANK = 512


class Scope:

    def __init__(self, nc, stack, prefix):
        self.nc, self.stack, self.prefix, self.sems = nc, stack, prefix, []
        stack.callback(self.clear)

    def sbuf(self, name, shape, dtype=F32):
        return self.stack.enter_context(self.nc.sbuf_tensor(f"{self.prefix}_{name}", shape, dtype))

    def psum(self, name, shape, dtype=F32):
        return self.stack.enter_context(self.nc.psum_tensor(f"{self.prefix}_{name}", shape, dtype))

    def sem(self, name):
        self.sems.append(self.nc.alloc_semaphore(f"{self.prefix}_{name}"))
        return self.sems[-1]

    def clear(self):
        if self.sems:
            self.nc.clear_and_free_semaphores(self.sems)
            self.nc.all_engine_barrier()

    def dram(self, name, shape, dtype=F32):
        return self.nc.dram_tensor(f"{self.prefix}_{name}", shape, dtype)


def make_identity(nc, s, ident, engine, zeroed, made):
    nc.gpsimd.memset(ident[:], 0.0).then_inc(zeroed, 1)
    engine.wait_ge(zeroed, 1)
    nc.gpsimd.affine_select(out=ident[:], in_=ident[:], compare_op=ALU.not_equal, fill=1.0, base=0,
                            pattern=[[-1, P]], channel_multiplier=1).then_inc(made, 1)


EXPERTS = 8
TOKEN_TILES = N // P
SLOT_TILES = TOKEN_TILES + EXPERTS


def layernorm_tiles(nc, dve, rows, stats, mv, rstd, spare, tiles, k, stat_step, var_ready, std_ready,
                    rstd_ready, normed, dst=None):
    dst = rows if dst is None else dst
    for j in range(tiles):
        ins = nc.vector.bn_stats(stats[:, j, :], rows[:, j, :])
    ins.then_inc(stat_step, 1)
    dve.wait_ge(stat_step, k)
    nc.vector.memset(spare[:], 0.0)
    for j in range(tiles):
        ins = nc.vector.bn_aggr(mv[:, j, :], stats[:, j, :])
    ins.then_inc(var_ready, 1)
    dve.wait_ge(std_ready, k)
    nc.vector.reciprocal(rstd[:], rstd[:]).then_inc(rstd_ready, 1)
    dve.wait_ge(rstd_ready, k)
    for j in range(tiles):
        ins = nc.vector.tensor_scalar(dst[:, j, :], rows[:, j, :], mv[:, j, 0:1], rstd[:, j:j + 1], ALU.subtract, ALU.mult)
    ins.then_inc(normed, 1)


def layernorm_stats(nc, dve, rows, stats, mv, spare, tiles, k, stat_step, var_ready):
    for j in range(tiles):
        ins = nc.vector.bn_stats(stats[:, j, :], rows[:, j, :])
    ins.then_inc(stat_step, 1)
    dve.wait_ge(stat_step, k)
    nc.vector.memset(spare[:], 0.0)
    for j in range(tiles):
        ins = nc.vector.bn_aggr(mv[:, j, :], stats[:, j, :])
    ins.then_inc(var_ready, 1)


def layernorm_apply(nc, dve, rows, dst, mv, rstd, tiles, k, std_ready, rstd_ready, normed):
    dve.wait_ge(std_ready, k)
    nc.vector.reciprocal(rstd[:], rstd[:]).then_inc(rstd_ready, 1)
    dve.wait_ge(rstd_ready, k)
    for j in range(tiles):
        ins = nc.vector.tensor_scalar(dst[:, j, :], rows[:, j, :], mv[:, j, 0:1], rstd[:, j:j + 1], ALU.subtract, ALU.mult)
    ins.then_inc(normed, 1)


def held(engine, value):
    return value if isinstance(value, int) else engine.snap(value)


def state_space_layer(nc, x_tok, x_feat, win, b_in, a_log, b_param, c_param, wdt, b_dt, wconv, wout,
                      b_out, x1):
    DI, NS, RANK, TAPS = 512, 16, 64, 4
    M = DI // P
    CH = 1024
    CHUNKS = N // CH
    HALVES = CH // BANK
    STEPS = M * NS
    TILES = CH // P
    TG = 4
    OUTS = TILES // TG
    A_RING, DBX_RING, H_RING = 2, 4, 4
    COLS = DI * 2 + RANK + NS
    B_LO = 96
    B_HI = B_LO + NS
    RB = 2 * DI

    with ExitStack() as stack:
        s = Scope(nc, stack, "ssm")
        win_sb = s.sbuf("win", [P, KD, RB + B_HI])
        wout_sb = s.sbuf("wout", [P, M, D])
        wdt_sb = s.sbuf("wdt", [RANK + 1, DI])
        conv_sb = s.sbuf("conv", [P, M, TAPS])
        bv_sb = s.sbuf("bv", [P, M])
        bx_sb = s.sbuf("bx", [P, M])
        brb_sb = s.sbuf("brb", [B_HI, 1])
        bparam_sb = s.sbuf("bparam", [B_HI, 1])
        a_sb = s.sbuf("a", [P, M, NS])
        c_sb = s.sbuf("c", [P, M, NS])
        bout_sb = s.sbuf("bout", [P, D])
        ident = s.sbuf("ident", [P, P])
        diag_c = s.sbuf("diag_c", [P, H_RING, P])
        keep = s.sbuf("keep", [P, CHUNKS])
        eps_sb = s.sbuf("eps", [P, 1])
        xf = s.sbuf("xf", [P, KD, CH])
        xt = s.sbuf("xt", [P, TILES, D])
        rank = s.sbuf("rank", [B_HI, CH])
        b_all = s.sbuf("b_all", [P, NS, CH])
        xpad = s.sbuf("xpad", [P, TAPS - 1 + CH])
        hist = s.sbuf("hist", [P, M, TAPS - 1])
        xs = s.sbuf("xs", [P, 2, CH])
        delta = s.sbuf("delta", [P, 2, CH])
        gate = s.sbuf("gate", [P, M, CH])
        sp_e = s.sbuf("sp_e", [P, CH])
        sp_u = s.sbuf("sp_u", [P, CH])
        sp_l = s.sbuf("sp_l", [P, CH])
        dbx = s.sbuf("dbx", [P, DBX_RING, CH])
        h = s.sbuf("h", [P, H_RING, CH])
        carry = s.sbuf("carry", [P, STEPS])
        stats = s.sbuf("stats", [P, TILES, 6])
        mv = s.sbuf("mv", [P, TILES, 2])
        rstd = s.sbuf("rstd", [P, TILES])
        spare = s.sbuf("spare", [P, 1])

        decay = s.psum("decay", [P, A_RING, CH])
        y_ps = s.psum("y", [P, CH])
        proj = s.psum("proj", [P, CH])

        b_dram = s.dram("b", [NS, N])

        consts_in = s.sem("consts_in")
        zeroed = s.sem("zeroed")
        ident_ready = s.sem("ident_ready")
        pool_consts = s.sem("pool_consts")
        neg_a = s.sem("neg_a")
        a_ready = s.sem("a_ready")
        brb_ready = s.sem("brb_ready")
        xf_in = s.sem("xf_in")
        xt_in = s.sem("xt_in")
        rb_full = s.sem("rb_full")
        x_full = s.sem("x_full")
        v_full = s.sem("v_full")
        dt_full = s.sem("dt_full")
        o_full = s.sem("o_full")
        b_ready = s.sem("b_ready")
        b_stored = s.sem("b_stored")
        b_in_all = [s.sem(f"b_in_all{n}") for n in range(NS)]
        xpad_ready = s.sem("xpad_ready")
        xpad_free = s.sem("xpad_free")
        conv_step = s.sem("conv_step")
        conv_ready = s.sem("conv_ready")
        silu_ready = s.sem("silu_ready")
        gate_ready = s.sem("gate_ready")
        soft_abs = s.sem("soft_abs")
        soft_exp = s.sem("soft_exp")
        soft_add = s.sem("soft_add")
        soft_ready = s.sem("soft_ready")
        soft_step = s.sem("soft_step")
        delta_ready = s.sem("delta_ready")
        dx_ready = s.sem("dx_ready")
        decay_ready = s.sem("decay_ready")
        dbx_ready = s.sem("dbx_ready")
        scan_done = s.sem("scan_done")
        carried = s.sem("carried")
        h_used = s.sem("h_used")
        gated = s.sem("gated")
        xt_biased = s.sem("xt_biased")
        res_ready = s.sem("res_ready")
        stat_step = s.sem("stat_step")
        var_ready = s.sem("var_ready")
        std_ready = s.sem("std_ready")
        rstd_ready = s.sem("rstd_ready")
        normed = s.sem("normed")
        stored = s.sem("stored")

        win_v = win.rearrange("(k p) c -> p k c", p=P)
        loads = [
            (win_sb[:, :, 0:2 * DI], win_v[:, :, 0:2 * DI]),
            (win_sb[:, :, RB:RB + RANK], win_v[:, :, 2 * DI + NS:COLS]),
            (win_sb[:, :, RB + B_LO:RB + B_HI], win_v[:, :, 2 * DI:2 * DI + NS]),
            (wout_sb[:], wout.rearrange("(m p) c -> p m c", p=P)),
            (wdt_sb[0:RANK, :], wdt),
            (wdt_sb[RANK:RANK + 1, :], b_dt.rearrange("(a d) -> a d", a=1)),
            (conv_sb[:], wconv.rearrange("(m p) a k -> p m (a k)", p=P)),
            (bv_sb[:], b_in[0:DI].rearrange("(m p) -> p m", p=P)),
            (bx_sb[:], b_in[DI:2 * DI].rearrange("(m p) -> p m", p=P)),
            (brb_sb[0:RANK, :], b_in[2 * DI + NS:COLS].rearrange("(p a) -> p a", a=1)),
            (brb_sb[B_LO:B_HI, :], b_in[2 * DI:2 * DI + NS].rearrange("(p a) -> p a", a=1)),
            (bparam_sb[B_LO:B_HI, :], b_param.rearrange("(p a) -> p a", a=1)),
            (a_sb[:], a_log.rearrange("(m p) n -> p m n", p=P)),
            (c_sb[:], c_param.rearrange("(m p) n -> p m n", p=P)),
            (bout_sb[:], b_out.rearrange("(a d) -> a d", a=1).partition_broadcast(P)),
        ]
        ALL_IN = 16 * len(loads)
        POOL_FILLS = 5 + CHUNKS

        SIDE = [
            dict(pe_x=0, act_x=2, conv=2, pe_v={14: 0}, act_v={15: 0}, act_silu=6, pe_dt=2, act_soft=4, dve_soft=6,
                 pe_o0=7, dve_o0=10, pe_o1=10, dve_o1=13, act_root=15, dve_n0=15, dve_n1=15, act_store=15),
            dict(pe_x=0, act_x=2, conv=2, pe_v={2: 1}, act_v={6: 1}, act_silu=6, pe_dt=5, act_soft=9, dve_soft=10),
            dict(pe_x=0, act_x=2, conv=2, pe_v={2: 2, 5: 3}, act_v={6: 2, 7: 3}, act_silu=7, pe_dt=8, act_soft=11, dve_soft=12),
            dict(pe_rb=0, act_rb=2, pe_x=1, act_x=5, conv=4, pe_v={}, act_v={}, act_silu=8, pe_dt=6, act_soft=8, dve_soft=10),
        ]

        def run_units(engine, unit, head):
            head()
            unit(0, 0, False, True)
            with engine.Fori(0, CHUNKS - 1) as c:
                for m in range(1, M):
                    unit(c, m, False, True)
                unit(c + 1, 0, True, True)
            for m in range(1, M):
                unit(CHUNKS - 1, m, False, m < M - 1)

        def side(m, tail):
            if m == 0 and not tail:
                return SIDE[1] | dict(pe_v={2: 0}, act_v={6: 0})
            return SIDE[m]

        block = stack.enter_context(nc.Block())

        @block.sync
        def _(sp):
            for dst, src in loads:
                sp.dma_start(dst, src, allow_slow_non_contiguous=True).then_inc(consts_in, 16)

            def load_xf(c):
                sp.dma_start(xf[:], x_feat.rearrange("(k p) t -> p k t", p=P)[:, :, bass.ds(c * CH, CH)]).then_inc(xf_in, 16)

            def load_xt(c):
                sp.dma_start(xt[:], x_tok.rearrange("(i p) d -> p i d", p=P)[:, bass.ds(c * TILES, TILES), :]).then_inc(xt_in, 16)

            def spread_b(c, first):
                sp.wait_ge(b_ready, 2 * c + 2)
                sp.dma_start(b_dram[:, bass.ds(c * CH, CH)], rank[B_LO:B_HI, :]).then_inc(b_stored, 16)
                sp.wait_ge(b_stored, 16 * c + 16)
                for n in range(NS):
                    if not first:
                        sp.wait_ge(dbx_ready, c * STEPS + (n + 1 - NS))
                    sp.dma_start(b_all[:, n, :], b_dram[n, bass.ds(c * CH, CH)].partition_broadcast(P)).then_inc(b_in_all[n], 16)

            load_xf(0)
            load_xt(0)
            spread_b(0, True)
            with sp.Fori(1, CHUNKS) as c:
                sp.wait_ge(v_full, M * c)
                load_xf(c)
                spread_b(c, False)
                sp.wait_ge(stored, 16 * c + 16)
                load_xt(c)

        @block.gpsimd
        def _(pool):
            fills = [(eps_sb[:], EPS), (hist[:], 0.0), (rank[RANK:RANK + 1, :], 1.0), (carry[:], 0.0),
                     (win_sb[:, :, RB + RANK:RB + B_LO], 0.0)]
            fills += [(keep[:, c:c + 1], 0.0 if (c + 1) * CH % T == 0 else 1.0) for c in range(CHUNKS)]
            for k, (dst, value) in enumerate(fills):
                nc.gpsimd.memset(dst, value).then_inc(pool_consts, 1)
                pool.wait_ge(pool_consts, k + 1)
            make_identity(nc, s, ident, pool, zeroed, ident_ready)
            pool.wait_ge(consts_in, ALL_IN)

            def unit(c, m, tail, more):
                base = held(pool, c * STEPS)
                if m == 0:
                    dmas = held(pool, (c + 1) * 16)
                pool.wait_ge(dx_ready, held(pool, c * M + (m + 1)))
                for n in range(NS):
                    i = m * NS + n
                    if m == 0:
                        pool.wait_ge(b_in_all[n], dmas)
                    pool.wait_ge(scan_done, base + (i + 1))
                    nc.gpsimd.tensor_tensor(dbx[:, i % DBX_RING, :], xs[:, m % 2, :], b_all[:, n, :], ALU.mult).then_inc(dbx_ready, 1)

            run_units(pool, unit, lambda: None)

        @block.scalar
        def _(act):
            act.wait_ge(consts_in, ALL_IN)
            nc.scalar.activation(a_sb[:], a_sb[:], ACT.Exp).then_inc(neg_a, 1)
            act.wait_ge(pool_consts, POOL_FILLS)
            act.wait_ge(brb_ready, 1)
            act.wait_ge(a_ready, 1)

            def take_rank_b(c):
                act.wait_ge(rb_full, held(act, c + 1))
                nc.scalar.activation(rank[0:RANK, :], proj[0:RANK, :], ACT.Identity, bias=brb_sb[0:RANK, :]).then_inc(b_ready, 1)
                nc.scalar.activation(rank[B_LO:B_HI, :], proj[B_LO:B_HI, :], ACT.Identity, bias=brb_sb[B_LO:B_HI, :]).then_inc(b_ready, 1)

            def take_x(k, m):
                act.wait_ge(x_full, k + 1)
                act.wait_ge(xpad_free, k + 1)
                nc.scalar.activation(xpad[:, TAPS - 1:], proj[:], ACT.Identity, bias=bx_sb[:, m:m + 1]).then_inc(xpad_ready, 1)

            def silu_x(k, m):
                act.wait_ge(conv_ready, k + 1)
                nc.scalar.activation(xs[:, m % 2, :], xs[:, m % 2, :], ACT.Silu).then_inc(silu_ready, 1)

            def silu_v(k, m):
                act.wait_ge(v_full, k + 1)
                nc.scalar.activation(gate[:, m, :], proj[:], ACT.Silu, bias=bv_sb[:, m:m + 1]).then_inc(gate_ready, 1)

            def soft(k, part):
                if part == 0:
                    act.wait_ge(dt_full, k + 1)
                    act.wait_ge(delta_ready, k + 1)
                    nc.scalar.activation(sp_e[:], proj[:], ACT.Abs).then_inc(soft_abs, 1)
                    act.wait_ge(soft_abs, k + 1)
                    nc.scalar.activation(sp_e[:], sp_e[:], ACT.Exp, scale=-1.0).then_inc(soft_exp, 1)
                elif part == 1:
                    act.wait_ge(soft_exp, k + 1)
                    nc.scalar.activation(sp_u[:], sp_e[:], ACT.Identity, bias=1.0).then_inc(soft_add, 1)
                else:
                    act.wait_ge(soft_add, k + 1)
                    nc.scalar.activation(sp_l[:], sp_u[:], ACT.Ln).then_inc(soft_ready, 1)

            def root(c):
                act.wait_ge(var_ready, c + 1)
                nc.scalar.activation(rstd[:], mv[:, :, 1], ACT.Sqrt, bias=eps_sb[:]).then_inc(std_ready, 1)

            def store(c):
                act.wait_ge(normed, held(act, c + 1))
                act.dma_start(x1.rearrange("(i p) d -> p i d", p=P)[:, bass.ds(c * TILES, TILES), :], xt[:]).then_inc(stored, 16)

            def head():
                take_rank_b(0)
                take_x(0, 0)
                silu_x(0, 0)
                for part in range(3):
                    soft(0, part)

            def unit(c, m, tail, more):
                base = held(act, c * STEPS)
                k = held(act, c * M + m)
                at = side(m, tail)
                nxt = (m + 1) % M
                act.wait_ge(delta_ready, k + 2)
                for n in range(NS):
                    i = m * NS + n
                    act.wait_ge(scan_done, base + (i + 1 + DBX_RING - A_RING))
                    nc.scalar.activation(decay[:, i % A_RING, :], delta[:, m % 2, :], ACT.Exp, scale=a_sb[:, m, n:n + 1]).then_inc(decay_ready, 1)
                    if tail and n == at["act_root"]:
                        root(held(act, c - 1))
                    if tail and n == at["act_store"]:
                        store(c - 1)
                    if n == at.get("act_rb") and more:
                        take_rank_b(c + 1)
                    if n == at["act_x"] and more:
                        take_x(k + 1, nxt)
                    if n in at["act_v"]:
                        silu_v(k - m + at["act_v"][n], at["act_v"][n])
                    if n == at["act_silu"] and more:
                        silu_x(k + 1, nxt)
                    if 0 <= n - at["act_soft"] < 3 and more:
                        soft(k + 1, n - at["act_soft"])

            run_units(act, unit, head)
            root(CHUNKS - 1)
            store(CHUNKS - 1)
            act.wait_ge(stored, 16 * CHUNKS + 16)

        @block.vector
        def _(dve):
            dve.wait_ge(consts_in, ALL_IN)
            dve.wait_ge(pool_consts, POOL_FILLS)
            dve.sem_inc(xpad_free, 1)
            dve.sem_inc(delta_ready, 1)
            dve.sem_inc(scan_done, DBX_RING)
            dve.sem_inc(h_used, H_RING)
            dve.sem_inc(gated, 1)
            dve.sem_inc(carried, STEPS)
            dve.sem_inc(stored, 16)
            nc.vector.tensor_tensor(brb_sb[B_LO:B_HI, :], brb_sb[B_LO:B_HI, :], bparam_sb[B_LO:B_HI, :], ALU.add).then_inc(brb_ready, 1)
            dve.wait_ge(ident_ready, 1)
            dve.wait_ge(neg_a, 1)
            nc.vector.tensor_scalar(a_sb[:], a_sb[:], -1.0, None, ALU.mult).then_inc(a_ready, 1)
            def conv(c, k, m, t):
                steps = held(dve, k * TAPS)
                if t == 0:
                    dve.wait_ge(xpad_free, k + 1)
                    nc.vector.tensor_copy(xpad[:, 0:TAPS - 1], hist[:, m, :]).then_inc(conv_step, 1)
                    dve.wait_ge(conv_step, steps + 1)
                    dve.wait_ge(xpad_ready, k + 1)
                    nc.vector.tensor_scalar(xs[:, m % 2, :], xpad[:, 0:CH], conv_sb[:, m, 0:1], None, ALU.mult).then_inc(conv_step, 1)
                    return
                dve.wait_ge(conv_step, steps + (1 + t))
                ins = nc.vector.scalar_tensor_tensor(out=xs[:, m % 2, :], in0=xpad[:, t:t + CH], scalar=conv_sb[:, m, t:t + 1],
                                                     in1=xs[:, m % 2, :], op0=ALU.mult, op1=ALU.add)
                ins.then_inc(conv_ready if t == TAPS - 1 else conv_step, 1)
                if t == TAPS - 1:
                    nc.vector.tensor_scalar(hist[:, m, :], xpad[:, CH:CH + TAPS - 1], keep[:, bass.ds(c, 1)], None, ALU.mult).then_inc(xpad_free, 1)

            def soft(k, m, part):
                if part == 0:
                    dve.wait_ge(soft_add, k + 1)
                    dve.wait_ge(soft_ready, k + 1)
                    nc.vector.scalar_tensor_tensor(out=sp_u[:], in0=sp_u[:], scalar=-1.0, in1=sp_e[:], op0=ALU.add, op1=ALU.subtract).then_inc(soft_step, 1)
                elif part == 1:
                    nc.vector.scalar_tensor_tensor(out=sp_l[:], in0=proj[:], scalar=0.0, in1=sp_l[:], op0=ALU.max, op1=ALU.add).then_inc(soft_step, 1)
                    dve.wait_ge(soft_step, held(dve, 2 * k + 2))
                    nc.vector.tensor_tensor(delta[:, m % 2, :], sp_l[:], sp_u[:], ALU.subtract).then_inc(delta_ready, 1)
                else:
                    dve.wait_ge(delta_ready, k + 2)
                    dve.wait_ge(silu_ready, k + 1)
                    nc.vector.tensor_tensor(xs[:, m % 2, :], xs[:, m % 2, :], delta[:, m % 2, :], ALU.mult).then_inc(dx_ready, 1)

            def gate_y(c, k, m):
                dve.wait_ge(h_used, held(dve, c * STEPS + ((m + 1) * NS + H_RING)))
                dve.wait_ge(gate_ready, k + 1)
                nc.vector.tensor_tensor(gate[:, m, :], y_ps[:], gate[:, m, :], ALU.mult).then_inc(gated, 1)

            def group(g):
                return xt[:, g * TG:(g + 1) * TG, :]

            def residual(c, g):
                done = held(dve, c * OUTS + (g + 1))
                dve.wait_ge(o_full, done)
                nc.vector.tensor_tensor(group(g), proj[:].rearrange("p (i d) -> p i d", d=D), group(g), ALU.add).then_inc(res_ready, 1)
                dve.wait_ge(res_ready, done)
                for j in range(g * TG, (g + 1) * TG):
                    ins = nc.vector.bn_stats(stats[:, j, :], xt[:, j, :])
                ins.then_inc(stat_step, 1)
                if g == OUTS - 1:
                    dve.wait_ge(stat_step, done)
                    nc.vector.memset(spare[:], 0.0)
                    for j in range(TILES):
                        ins = nc.vector.bn_aggr(mv[:, j, :], stats[:, j, :])
                    ins.then_inc(var_ready, 1)

            def normalise(c, g):
                if g == 0:
                    dve.wait_ge(std_ready, held(dve, c + 1))
                    nc.vector.reciprocal(rstd[:], rstd[:]).then_inc(rstd_ready, 1)
                    dve.wait_ge(rstd_ready, held(dve, c + 1))
                for j in range(g * TG, (g + 1) * TG):
                    ins = nc.vector.tensor_scalar(xt[:, j, :], xt[:, j, :], mv[:, j, 0:1], rstd[:, j:j + 1], ALU.subtract, ALU.mult)
                if g == OUTS - 1:
                    ins.then_inc(normed, 1)

            def bias_xt(c):
                dve.wait_ge(xt_in, held(dve, (c + 1) * 16))
                nc.vector.tensor_tensor(xt[:], xt[:], bout_sb[:].unsqueeze(1).broadcast_to([P, TILES, D]), ALU.add).then_inc(xt_biased, 1)

            def head():
                for t in range(TAPS):
                    conv(0, 0, 0, t)
                for part in range(3):
                    soft(0, 0, part)

            def unit(c, m, tail, more):
                base = held(dve, c * STEPS)
                k = held(dve, c * M + m)
                at = side(m, tail)
                nxt = (m + 1) % M

                def save(i):
                    dve.wait_ge(scan_done, base + (i + 1 + DBX_RING))
                    nc.vector.tensor_scalar(carry[:, i:i + 1], h[:, i % H_RING, CH - 1:CH], keep[:, bass.ds(c, 1)], None, ALU.mult).then_inc(carried, 1)

                dve.wait_ge(carried, base + (m + 1) * NS)
                for n in range(NS):
                    i = m * NS + n
                    dve.wait_ge(h_used, base + (i + 1))
                    nc.vector.tensor_scalar(diag_c[:, i % H_RING, :], ident[:], c_sb[:, m, n:n + 1], None, ALU.mult)
                    dve.wait_ge(decay_ready, base + (i + 1))
                    dve.wait_ge(dbx_ready, base + (i + 1))
                    nc.vector.tensor_tensor_scan(h[:, i % H_RING, :], decay[:, i % A_RING, :], dbx[:, i % DBX_RING, :],
                                                 carry[:, i:i + 1], ALU.mult, ALU.add).then_inc(scan_done, 1)
                    if n:
                        save(i - 1)
                    if n == 1 and (m or tail):
                        gate_y(c if m else c - 1, k - 1, (m - 1) % M)
                    if m == 1 and n == 13:
                        bias_xt(c)
                    if tail:
                        for g in range(OUTS):
                            if n == at[f"dve_o{g}"]:
                                residual(c - 1, g)
                            if n == at[f"dve_n{g}"]:
                                normalise(c - 1, g)
                    if 0 <= n - at["conv"] < TAPS and more:
                        conv(c if m < M - 1 else c + 1, k + 1, nxt, n - at["conv"])
                    if 0 <= n - at["dve_soft"] < 3 and more:
                        soft(k + 1, nxt, n - at["dve_soft"])
                save(m * NS + NS - 1)

            run_units(dve, unit, head)
            c = CHUNKS - 1
            gate_y(c, c * M + M - 1, M - 1)
            for g in range(OUTS):
                residual(c, g)
            for g in range(OUTS):
                normalise(c, g)

        @block.tensor
        def _(pe):
            pe.wait_ge(consts_in, ALL_IN)
            pe.wait_ge(pool_consts, POOL_FILLS)

            def project(rows, lhs, rhs):
                for half in range(HALVES):
                    cols = slice(half * BANK, (half + 1) * BANK)
                    for j in range(len(lhs)):
                        ins = nc.tensor.matmul(proj[0:rows, cols], lhs[j], rhs[j][:, cols], start=(j == 0), stop=(j == len(lhs) - 1))
                return ins

            xf_k = [xf[:, k, :] for k in range(KD)]

            def project_rb(c):
                pe.wait_ge(xf_in, held(pe, (c + 1) * 16))
                project(B_HI, [win_sb[:, k, RB:RB + B_HI] for k in range(KD)], xf_k).then_inc(rb_full, 1)

            def project_x(m):
                project(P, [win_sb[:, k, DI + m * P:DI + (m + 1) * P] for k in range(KD)], xf_k).then_inc(x_full, 1)

            def project_v(m):
                project(P, [win_sb[:, k, m * P:(m + 1) * P] for k in range(KD)], xf_k).then_inc(v_full, 1)

            def project_dt(m):
                project(P, [wdt_sb[:, m * P:(m + 1) * P]], [rank[0:RANK + 1, :]]).then_inc(dt_full, 1)

            def project_out(g):
                for j in range(TG):
                    t = (g * TG + j) * P
                    for m in range(M):
                        ins = nc.tensor.matmul(proj[:, j * D:(j + 1) * D], gate[:, m, t:t + P], wout_sb[:, m, :],
                                               start=(m == 0), stop=(m == M - 1))
                ins.then_inc(o_full, 1)

            def head():
                project_rb(0)
                pe.wait_ge(b_ready, 2)
                project_x(0)
                pe.wait_ge(xpad_ready, 1)
                project_dt(0)

            def out_group(c, k, g):
                if g == 0:
                    pe.wait_ge(gated, k + 1)
                    pe.wait_ge(delta_ready, k + 3)
                else:
                    pe.wait_ge(res_ready, held(pe, c * OUTS + g))
                project_out(g)

            def unit(c, m, tail, more):
                base = held(pe, c * STEPS)
                k = held(pe, c * M + m)
                at = side(m, tail)
                nxt = (m + 1) % M
                for n in range(NS):
                    i = m * NS + n
                    if tail:
                        for g in range(OUTS):
                            if n == at[f"pe_o{g}"]:
                                out_group(c - 1, k, g)
                    if n == at.get("pe_rb") and more:
                        pe.wait_ge(delta_ready, k + 2)
                        pe.wait_ge(gate_ready, k + 1)
                        project_rb(c + 1)
                    if n == at["pe_x"] and more:
                        if m == M - 1:
                            pe.wait_ge(b_ready, held(pe, 2 * c + 4))
                        elif m == 1:
                            pe.wait_ge(gate_ready, k)
                        else:
                            pe.wait_ge(delta_ready, k + 2)
                        project_x(nxt)
                    if n in at["pe_v"]:
                        v = at["pe_v"][n]
                        if tail:
                            pe.wait_ge(res_ready, held(pe, c * OUTS))
                        elif v > m:
                            pe.wait_ge(gate_ready, k + 1)
                        else:
                            pe.wait_ge(xpad_ready, k + 2)
                        project_v(v)
                    if n == at["pe_dt"] and more:
                        if 0 < m < M - 1 or m == 0 and not tail:
                            pe.wait_ge(gate_ready, k + (1 + max(at["pe_v"].values()) - m))
                        else:
                            pe.wait_ge(xpad_ready, k + 2)
                        project_dt(nxt)
                    if n == 0:
                        pe.wait_ge(gated, k + 1)
                    pe.wait_ge(scan_done, base + (i + 1 + DBX_RING))
                    for half in range(HALVES):
                        cols = slice(half * BANK, (half + 1) * BANK)
                        ins = nc.tensor.matmul(y_ps[:, cols], diag_c[:, i % H_RING, :], h[:, i % H_RING, cols], start=(n == 0), stop=(n == NS - 1))
                    ins.then_inc(h_used, 1)

            run_units(pe, unit, head)
            c = CHUNKS - 1
            pe.wait_ge(gated, c * M + M + 1)
            pe.wait_ge(gate_ready, c * M + M)
            for g in range(OUTS):
                if g:
                    pe.wait_ge(res_ready, c * OUTS + g)
                project_out(g)


def route(nc, prefix, x1, router, router_b, slot_table, slots, weight, capacity, tile_expert=None):
    E, NT = EXPERTS, TOKEN_TILES
    G = 4
    GROUPS = NT // G
    SLOTS = E * capacity if capacity else P * SLOT_TILES
    with ExitStack() as stack:
        s = Scope(nc, stack, prefix)
        router_sb = s.sbuf("router", [P, KD, E])
        bias_sb = s.sbuf("bias", [P, E])
        ident = s.sbuf("ident", [P, P])
        xt = s.sbuf("xt", [P, 2, G, D])
        xT = s.sbuf("xT", [P, 2, G, D])
        logits = s.sbuf("logits", [P, NT, E])
        ex = s.sbuf("ex", [P, NT, E])
        row = s.sbuf("row", [P, 6, NT])
        big, total, p, best, pos, slot = (row[:, k, :] for k in range(6))
        hot = s.sbuf("hot", [P, NT, E])
        hot_b = s.sbuf("hot_b", [P, NT, E], BF16)
        rev = s.sbuf("rev", [P, E])
        base = s.sbuf("base", [P, E])
        token = s.sbuf("token", [P, NT], I32)
        token_f = s.sbuf("token_f", [P, NT])
        iota_i = s.sbuf("iota_i", [P, 2 * E], I32)
        zeros = s.sbuf("zeros", [P, SLOTS // P], I32)
        ones_row = s.sbuf("ones_row", [P, NT])
        upper = s.sbuf("upper", [P, P], BF16)
        ones = s.sbuf("ones", [P, P], BF16)
        before = s.sbuf("before", [P, NT, E])
        small = s.sbuf("small", [P, 4, E])
        small_i = s.sbuf("small_i", [P, E], I32)
        tile_no = s.sbuf("tile_no", [P, SLOT_TILES, E])
        tile_no_i = s.sbuf("tile_no_i", [P, SLOT_TILES, E], I32)
        tile_f = s.sbuf("tile_f", [P, SLOT_TILES])
        low = s.sbuf("low", [P, NT], I32)
        t_ps = s.psum("t", [P, 2, G * D])
        l_ps = s.psum("l", [P, 2, BANK])
        c_ps = s.psum("c", [P, 2, NT, E])

        router_in = s.sem("router_in")
        zeroed = s.sem("zeroed")
        ident_ready = s.sem("ident_ready")
        consts = s.sem("consts")
        x_in = [s.sem(f"x_in{u}") for u in range(2)]
        turned = s.sem("turned")
        xT_ready = s.sem("xT_ready")
        logit_ps = s.sem("logit_ps")
        logit_ready = s.sem("logit_ready")
        step = s.sem("step")
        ex_ready = s.sem("ex_ready")
        hot_ready = s.sem("hot_ready")
        counted = s.sem("counted")
        slots_ready = s.sem("slots_ready")
        table_zero = s.sem("table_zero")
        scattered = s.sem("scattered")
        CONSTS = 8
        ROUTER_IN = 16 if router_b is None else 32

        block = stack.enter_context(nc.Block())

        @block.sync
        def _(sp):
            sp.dma_start(router_sb[:], router.rearrange("(k p) e -> p k e", p=P)).then_inc(router_in, 16)
            if router_b is not None:
                sp.dma_start(bias_sb[:], router_b.rearrange("(a e) -> a e", a=1).partition_broadcast(P)).then_inc(router_in, 16)
            x_v = x1.rearrange("(i p) d -> p i d", p=P)
            for g in range(2):
                sp.dma_start(xt[:, g, :, :], x_v[:, g * G:(g + 1) * G, :]).then_inc(x_in[g], 16)
            sp.wait_ge(consts, CONSTS)
            sp.dma_start(slot_table[0:SLOTS, :].rearrange("(p a) b -> p (a b)", p=P), zeros[:]).then_inc(table_zero, 16)
            with sp.Fori(1, GROUPS // 2) as i:
                for u in range(2):
                    sp.wait_ge(turned, 2 * i + (u - 1))
                    sp.dma_start(xt[:, u, :, :], x_v[:, bass.ds((2 * i + u) * G, G), :]).then_inc(x_in[u], 16)

        @block.gpsimd
        def _(pool):
            nc.gpsimd.memset(ident[:], 0.0).then_inc(zeroed, 1)
            nc.gpsimd.memset(upper[:], 1.0).then_inc(zeroed, 1)
            pool.wait_ge(zeroed, 2)
            nc.gpsimd.affine_select(out=ident[:], in_=ident[:], compare_op=ALU.not_equal, fill=1.0, base=0,
                                    pattern=[[-1, P]], channel_multiplier=1).then_inc(ident_ready, 1)
            nc.gpsimd.affine_select(out=upper[:], in_=upper[:], compare_op=ALU.is_ge, fill=0.0, base=0,
                                    pattern=[[1, P]], channel_multiplier=-1).then_inc(consts, 1)
            nc.gpsimd.memset(ones[:], 1.0).then_inc(consts, 1)
            nc.gpsimd.memset(ones_row[:], 1.0).then_inc(consts, 1)
            nc.gpsimd.memset(zeros[:], 0).then_inc(consts, 1)
            nc.gpsimd.iota(token[:], pattern=[[P, NT]], base=0, channel_multiplier=1).then_inc(zeroed, 1)
            nc.gpsimd.iota(iota_i[:, 0:E], pattern=[[-1, E]], base=E, channel_multiplier=0).then_inc(zeroed, 1)
            nc.gpsimd.iota(iota_i[:, E:2 * E], pattern=[[capacity or 0, E]], base=0, channel_multiplier=0).then_inc(zeroed, 1)
            nc.gpsimd.iota(tile_no_i[:], pattern=[[1, SLOT_TILES], [0, E]], base=0, channel_multiplier=0).then_inc(zeroed, 1)
            pool.wait_ge(zeroed, 6)
            pool.wait_ge(consts, 4)
            nc.gpsimd.tensor_copy(token_f[:], token[:]).then_inc(consts, 1)
            nc.gpsimd.tensor_copy(tile_no[:], tile_no_i[:]).then_inc(consts, 1)
            nc.gpsimd.tensor_copy(rev[:], iota_i[:, 0:E]).then_inc(consts, 1)
            nc.gpsimd.tensor_copy(base[:], iota_i[:, E:2 * E]).then_inc(consts, 1)
            pool.wait_ge(consts, CONSTS)
            pool.wait_ge(slots_ready, 1)
            pool.wait_ge(table_zero, 16)
            for t in range(NT):
                nc.gpsimd.indirect_dma_start(slot_table[:], bass.IndirectOffsetOnAxis(ap=slots[:, t:t + 1], axis=0),
                                             token[:, t:t + 1], None).then_inc(scattered, 16)
            pool.wait_ge(scattered, 16 * NT)

        @block.scalar
        def _(act):
            with act.Fori(0, GROUPS // 2) as i:
                for u in range(2):
                    act.wait_ge(turned, 2 * i + (u + 1))
                    act.wait_ge(logit_ps, 2 * i + (u + 1))
                    nc.scalar.activation(xT[:, u, :, :], t_ps[:, u, :].rearrange("p (g d) -> p g d", d=D), ACT.Copy).then_inc(xT_ready, 1)
            act.wait_ge(step, 2 if router_b is None else 3)
            nc.scalar.activation(ex[:], ex[:], ACT.Exp).then_inc(ex_ready, 1)

        @block.tensor
        def _(pe):
            pe.wait_ge(router_in, ROUTER_IN)
            pe.wait_ge(ident_ready, 1)
            with pe.Fori(0, GROUPS // 2) as i:
                for u in range(2):
                    pe.wait_ge(x_in[u], 16 * i + 16)
                    pe.wait_ge(xT_ready, 2 * i + (u + 1))
                    for j in range(G):
                        for k in range(KD):
                            ins = nc.tensor.transpose(t_ps[:, u, j * D + k * P:j * D + (k + 1) * P], xt[:, u, j, k * P:(k + 1) * P], ident[:])
                    ins.then_inc(turned, 1)
                for u in range(2):
                    pe.wait_ge(xT_ready, 2 * i + (u + 3))
                    pe.wait_ge(logit_ready, 2 * i + (u + 1))
                    for j in range(G):
                        for k in range(KD):
                            ins = nc.tensor.matmul(l_ps[:, u, j * E:(j + 1) * E], xT[:, u, j, k * P:(k + 1) * P], router_sb[:, k, :],
                                                   start=(k == 0), stop=(k == KD - 1))
                    ins.then_inc(logit_ps, 1)
            pe.wait_ge(consts, CONSTS)
            pe.wait_ge(hot_ready, 1)
            nc.tensor.matmul(c_ps[:, 0, :, :], upper[:], hot_b[:], start=True, stop=True)
            nc.tensor.matmul(c_ps[:, 1, :, :], ones[:], hot_b[:], start=True, stop=True).then_inc(counted, 1)

        @block.vector
        def _(dve):
            dve.sem_inc(xT_ready, 2)
            dve.sem_inc(logit_ready, 2)
            dve.sem_inc(logit_ps, 2)
            with dve.Fori(0, GROUPS // 2) as i:
                for u in range(2):
                    dve.wait_ge(logit_ps, 2 * i + (u + 3))
                    nc.vector.tensor_copy(logits[:, bass.ds((2 * i + u) * G, G), :],
                                          l_ps[:, u, 0:G * E].rearrange("p (g e) -> p g e", e=E)).then_inc(logit_ready, 1)
            dve.wait_ge(logit_ready, GROUPS + 2)
            dve.wait_ge(consts, CONSTS)
            done = [0]

            def after(ins):
                ins.then_inc(step, 1)
                done[0] += 1
                dve.wait_ge(step, done[0])

            def per_expert(x):
                return x.unsqueeze(1).broadcast_to([P, NT, E])

            def per_token(x):
                return x.unsqueeze(2).broadcast_to([P, NT, E])

            v = nc.vector
            if router_b is not None:
                dve.wait_ge(router_in, ROUTER_IN)
                after(v.tensor_tensor(logits[:], logits[:], per_expert(bias_sb[:]), ALU.add))
            after(v.tensor_reduce(big, logits[:], AX.X, ALU.max))
            after(v.tensor_tensor(ex[:], logits[:], per_token(big), ALU.subtract))
            dve.wait_ge(ex_ready, 1)
            after(v.tensor_reduce(total, ex[:], AX.X, ALU.add))
            after(v.reciprocal(p, total))
            scores = ex if capacity else logits
            after(v.tensor_reduce(big, scores[:], AX.X, ALU.max))
            after(v.tensor_tensor(hot[:], scores[:], per_token(big), ALU.is_ge))
            after(v.tensor_tensor(hot[:], hot[:], per_expert(rev[:]), ALU.mult))
            after(v.tensor_reduce(best, hot[:], AX.X, ALU.max))
            after(v.tensor_tensor(hot[:], per_expert(rev[:]), per_token(best), ALU.is_equal))
            v.tensor_copy(hot_b[:], hot[:]).then_inc(hot_ready, 1)
            dve.wait_ge(counted, 1)
            after(v.tensor_copy(ex[:], c_ps[:, 1, :, :]))
            for e in range(E):
                ins = v.tensor_tensor_scan(before[:, :, e], ones_row[:], ex[:, :, e], 0.0, ALU.mult, ALU.add)
            after(ins)
            if not capacity:
                counts, tiles, ends, starts = (small[:, k, :] for k in range(4))
                after(v.tensor_scalar(counts, before[:, NT - 1, :], P / 2 - 0.5, 1.0 / P, ALU.add, ALU.mult))
                after(v.tensor_copy(small_i[:], counts))
                after(v.tensor_copy(tiles, small_i[:]))
                after(v.tensor_tensor_scan(ends, ones_row[:, 0:E], tiles, 0.0, ALU.mult, ALU.add))
                after(v.tensor_tensor(starts, ends, tiles, ALU.subtract))
                after(v.tensor_scalar(base[:], starts, float(P), None, ALU.mult))
                after(v.tensor_tensor(tile_no[:], tile_no[:], ends.unsqueeze(1).broadcast_to([P, SLOT_TILES, E]), ALU.is_ge))
                after(v.tensor_reduce(tile_f[:], tile_no[:], AX.X, ALU.add))
                after(v.tensor_scalar(tile_f[:], tile_f[:], float(E - 1), None, ALU.min))
                after(v.tensor_copy(tile_expert[:], tile_f[0:1, :]))
            after(v.tensor_tensor(before[:], before[:], ex[:], ALU.subtract))
            after(v.tensor_tensor(before[:], before[:], c_ps[:, 0, :, :], ALU.add))
            after(v.tensor_tensor(ex[:], before[:], hot[:], ALU.mult))
            after(v.tensor_reduce(pos, ex[:], AX.X, ALU.add))
            after(v.tensor_tensor(ex[:], per_expert(base[:]), hot[:], ALU.mult))
            after(v.tensor_reduce(slot, ex[:], AX.X, ALU.add))
            after(v.scalar_tensor_tensor(out=slot, in0=slot, scalar=-1.0, in1=pos, op0=ALU.add, op1=ALU.add))
            if not capacity:
                after(v.tensor_copy(weight[:], p))
                after(v.tensor_copy(slots[:], slot))
                after(v.tensor_scalar(low[:], slots[:], P - 1, None, ALU.bitwise_and))
                after(v.tensor_scalar(slots[:], slots[:], P.bit_length() - 1, None, ALU.logical_shift_right))
                after(v.tensor_copy(pos, low[:]))
                after(v.tensor_copy(slot, slots[:]))
                after(v.scalar_tensor_tensor(out=slot, in0=pos, scalar=float(SLOT_TILES), in1=slot, op0=ALU.mult, op1=ALU.add))
                v.tensor_copy(slots[:], slot).then_inc(slots_ready, 1)
                return
            after(v.tensor_scalar(pos, pos, float(capacity), None, ALU.is_le))
            after(v.tensor_tensor(weight[:], p, pos, ALU.mult))
            after(v.tensor_scalar(token_f[:], token_f[:], float(SLOTS), None, ALU.add))
            after(v.tensor_tensor(slot, slot, token_f[:], ALU.subtract))
            after(v.tensor_tensor(slot, slot, pos, ALU.mult))
            after(v.tensor_tensor(slot, slot, token_f[:], ALU.add))
            v.tensor_copy(slots[:], slot).then_inc(slots_ready, 1)


def capacity_experts(nc, x1, slot_table, w1, b1, w2, b2, eo, capacity):
    E, F = EXPERTS, w1.shape[2]
    FB = F // P
    J = capacity // P
    HALF = capacity // 2
    H_BANKS, O_BANKS = 4, 2
    with ExitStack() as stack:
        s = Scope(nc, stack, "ffn")
        ident = s.sbuf("ident", [P, P])
        w1_sb = s.sbuf("w1", [P, 2, KD, F])
        w2_sb = s.sbuf("w2", [P, 2, FB, D])
        b1_rows = s.sbuf("b1_rows", [E * FB, P])
        b1_sb = s.sbuf("b1", [P, E * FB])
        b2_sb = s.sbuf("b2", [P, E, D])
        ids = s.sbuf("ids", [P, E, J], I32)
        ids_now = s.sbuf("ids_now", [P, 2, J], I32)
        b1_now = s.sbuf("b1_now", [P, 2, FB])
        spare = s.sbuf("spare", [P, 1])
        xg = s.sbuf("xg", [P, 2, J, D])
        xT = s.sbuf("xT", [P, 2, KD, capacity])
        hT = s.sbuf("hT", [P, 2, FB, capacity])
        out_sb = s.sbuf("out", [P, 2, J, D])
        t_ps = s.psum("t", [P, 2, BANK])
        h_ps = s.psum("h", [P, H_BANKS, BANK])
        o_ps = s.psum("o", [P, O_BANKS, BANK])

        zeroed = s.sem("zeroed")
        ident_ready = s.sem("ident_ready")
        ids_in = s.sem("ids_in")
        b1_in = s.sem("b1_in")
        b2_in = s.sem("b2_in")
        b1_turned = s.sem("b1_turned")
        b1_ready = s.sem("b1_ready")
        w1_in = [s.sem(f"w1_in{u}") for u in range(2)]
        w2_in = [s.sem(f"w2_in{u}") for u in range(2)]
        ids_ready = s.sem("ids_ready")
        gathered = [s.sem(f"gathered{u}") for u in range(2)]
        turned = s.sem("turned")
        xT_ready = s.sem("xT_ready")
        h_full = s.sem("h_full")
        h_ready = s.sem("h_ready")
        o_full = s.sem("o_full")
        o_ready = s.sem("o_ready")
        stored = [s.sem(f"stored{u}") for u in range(2)]
        TG = J // 2
        HG = 2 * FB

        block = stack.enter_context(nc.Block())

        @block.sync
        def _(sp):
            sp.dma_start(ids[:], slot_table[0:E * capacity, :].rearrange("(e p j) a -> p e (j a)", p=P, e=E)).then_inc(ids_in, 16)
            sp.dma_start(b1_rows[:], b1.rearrange("e (f p) -> (e f) p", p=P)).then_inc(b1_in, 16)

            def load(e, u):
                sp.dma_start(w1_sb[:, u, :, :], w1[bass.ds(e, 1), :, :].rearrange("a (k p) f -> p (a k) f", p=P)).then_inc(w1_in[u], 16)
                sp.dma_start(w2_sb[:, u, :, :], w2[bass.ds(e, 1), :, :].rearrange("a (f p) d -> p (a f) d", p=P)).then_inc(w2_in[u], 16)

            load(0, 0)
            load(1, 1)
            sp.dma_start(b2_sb[:], b2.partition_broadcast(P)).then_inc(b2_in, 16)

            def store(e, u):
                sp.wait_ge(o_ready, (e + 1) * J + O_BANKS)
                sp.dma_start(eo.rearrange("(e p j) d -> p e (j d)", e=E, p=P)[:, bass.ds(e, 1), :].rearrange("p a b -> p (a b)"),
                             out_sb[:, u, :, :].rearrange("p j d -> p (j d)")).then_inc(stored[u], 16)

            with sp.Fori(0, E // 2 - 1) as i:
                for u in range(2):
                    store(2 * i + u, u)
                    sp.wait_ge(o_full, (2 * i + (u + 3)) * J)
                    load(2 * i + (u + 2), u)
            store(E - 2, 0)
            store(E - 1, 1)
            for u in range(2):
                sp.wait_ge(stored[u], 8 * E + 16)

        @block.gpsimd
        def _(pool):
            make_identity(nc, s, ident, pool, zeroed, ident_ready)
            pool.wait_ge(ids_in, 16)
            pool.wait_ge(ident_ready, 1)
            with pool.Fori(0, E // 2) as i:
                for u in range(2):
                    pool.wait_ge(turned, (2 * i + (u + 1)) * TG)
                    nc.gpsimd.tensor_copy(ids_now[:, u, :], ids[:, bass.ds(2 * i + u, 1), :].rearrange("p a j -> p (a j)")).then_inc(ids_ready, 1)
                    pool.wait_ge(ids_ready, 2 * i + (u + 1))
                    nc.gpsimd.tensor_tensor(spare[:], ident[:, 0:1], ident[:, 0:1], ALU.add)
                    for j in range(J):
                        nc.gpsimd.indirect_dma_start(xg[:, u, j, :], None, x1[:],
                                                     bass.IndirectOffsetOnAxis(ap=ids_now[:, u, j:j + 1], axis=0)).then_inc(gathered[u], 16)

        @block.scalar
        def _(act):
            act.wait_ge(b1_turned, 1)
            nc.scalar.activation(b1_sb[:], t_ps[:, 0, 0:E * FB], ACT.Copy).then_inc(b1_ready, 1)
            act.wait_ge(b1_ready, 1)
            with act.Fori(0, E // 2) as i:
                for u in range(2):
                    groups = act.snap((2 * i + u) * HG)
                    act.wait_ge(o_full, (2 * i + (u + 1)) * J)
                    nc.scalar.activation(b1_now[:, u, :], b1_sb[:, bass.ds((2 * i + u) * FB, FB)], ACT.Copy).then_inc(b1_ready, 1)
                    act.wait_ge(b1_ready, 2 * i + (u + 2))
                    for f in range(FB):
                        for half in range(2):
                            k = 2 * f + half
                            act.wait_ge(h_full, groups + (k + 1))
                            nc.scalar.activation(hT[:, u, f, half * HALF:(half + 1) * HALF], h_ps[:, (u * HG + k) % H_BANKS, 0:HALF],
                                                 ACT.Gelu, bias=b1_now[:, u, f:f + 1]).then_inc(h_ready, 1)

        @block.tensor
        def _(pe):
            pe.wait_ge(ident_ready, 1)
            pe.wait_ge(b1_in, 16)
            nc.tensor.transpose(t_ps[:, 0, 0:E * FB], b1_rows[:], ident[0:E * FB, 0:E * FB]).then_inc(b1_turned, 1)
            pe.wait_ge(b1_ready, 1)
            with pe.Fori(0, E // 2) as i:
                for u in range(2):
                    e = 2 * i + u
                    tgroups = pe.snap(e * TG)
                    hgroups = pe.snap(e * HG)
                    ogroups = pe.snap(e * J)
                    pe.wait_ge(gathered[u], (16 * J) * i + 16 * J)
                    for g in range(TG):
                        b = (u * TG + g) % 2
                        pe.wait_ge(xT_ready, tgroups + (g + 1))
                        for jj in range(2):
                            for k in range(KD):
                                ins = nc.tensor.transpose(t_ps[:, b, (2 * jj + k) * P:(2 * jj + k + 1) * P], xg[:, u, 2 * g + jj, k * P:(k + 1) * P], ident[:])
                        ins.then_inc(turned, 1)
                    pe.wait_ge(xT_ready, tgroups + (TG + 2))
                    pe.wait_ge(w1_in[u], 16 * i + 16)
                    for f in range(FB):
                        for half in range(2):
                            n = 2 * f + half
                            pe.wait_ge(h_ready, hgroups + (n + 1))
                            for k in range(KD):
                                ins = nc.tensor.matmul(h_ps[:, (u * HG + n) % H_BANKS, 0:HALF], w1_sb[:, u, k, f * P:(f + 1) * P],
                                                       xT[:, u, k, half * HALF:(half + 1) * HALF], start=(k == 0), stop=(k == KD - 1))
                            ins.then_inc(h_full, 1)
                    pe.wait_ge(h_ready, hgroups + (HG + H_BANKS))
                    pe.wait_ge(w2_in[u], 16 * i + 16)
                    for j in range(J):
                        pe.wait_ge(o_ready, ogroups + (j + 1))
                        for f in range(FB):
                            ins = nc.tensor.matmul(o_ps[:, j % O_BANKS, 0:D], hT[:, u, f, j * P:(j + 1) * P], w2_sb[:, u, f, :],
                                                   start=(f == 0), stop=(f == FB - 1))
                        ins.then_inc(o_full, 1)

        @block.vector
        def _(dve):
            dve.sem_inc(xT_ready, 2)
            dve.sem_inc(h_ready, H_BANKS)
            dve.sem_inc(o_ready, O_BANKS)
            dve.sem_inc(turned, 2 * TG)
            dve.sem_inc(o_full, 2 * J)
            dve.sem_inc(stored[0], 16)
            dve.sem_inc(stored[1], 16)
            dve.wait_ge(b2_in, 16)
            with dve.Fori(0, E // 2) as i:
                for u in range(2):
                    e = 2 * i + u
                    tgroups = dve.snap(e * TG)
                    ogroups = dve.snap(e * J)
                    for g in range(TG):
                        b = (u * TG + g) % 2
                        dve.wait_ge(turned, tgroups + (2 * TG + g + 1))
                        nc.vector.tensor_copy(xT[:, u, :, 2 * g * P:(2 * g + 2) * P].rearrange("p k (j t) -> p j k t", t=P),
                                              t_ps[:, b, :].rearrange("p (j k t) -> p j k t", k=KD, t=P)).then_inc(xT_ready, 1)
                    dve.wait_ge(stored[u], 16 * i + 16)
                    for j in range(J):
                        dve.wait_ge(o_full, ogroups + (2 * J + j + 1))
                        nc.vector.tensor_tensor(out_sb[:, u, j, :], o_ps[:, j % O_BANKS, 0:D], b2_sb[:, bass.ds(e, 1), :].rearrange("p a d -> p (a d)"), ALU.add).then_inc(o_ready, 1)


def combine(nc, prefix, x1, eo, slots, weight, x2, last_slot):
    NT = TOKEN_TILES
    G = 4
    GROUPS = NT // G
    with ExitStack() as stack:
        s = Scope(nc, stack, prefix)
        xt = s.sbuf("xt", [P, 2, G, D])
        y = s.sbuf("y", [P, 2, G, D])
        inside = s.sbuf("inside", [P, NT], I32)
        inside_now = s.sbuf("inside_now", [P, 2, G], I32)
        spare_p = s.sbuf("spare_p", [P, 1])
        stats = s.sbuf("stats", [P, G, 6])
        mv = s.sbuf("mv", [P, G, 2])
        rstd = s.sbuf("rstd", [P, G])
        spare = s.sbuf("spare", [P, 1])
        eps_sb = s.sbuf("eps", [P, 1])

        eps_ready = s.sem("eps_ready")
        inside_ready = s.sem("inside_ready")
        now_ready = s.sem("now_ready")
        gathered = [s.sem(f"gathered{u}") for u in range(2)]
        x_in = [s.sem(f"x_in{u}") for u in range(2)]
        summed = s.sem("summed")
        stat_step = s.sem("stat_step")
        var_ready = s.sem("var_ready")
        std_ready = s.sem("std_ready")
        rstd_ready = s.sem("rstd_ready")
        normed = s.sem("normed")
        stored = [s.sem(f"stored{u}") for u in range(2)]

        block = stack.enter_context(nc.Block())

        @block.sync
        def _(sp):
            x_v = x1.rearrange("(i p) d -> p i d", p=P)
            for g in range(2):
                sp.dma_start(xt[:, g, :, :], x_v[:, g * G:(g + 1) * G, :]).then_inc(x_in[g], 16)
            with sp.Fori(1, GROUPS // 2) as i:
                for u in range(2):
                    sp.wait_ge(stored[u], 16 * i)
                    sp.dma_start(xt[:, u, :, :], x_v[:, bass.ds((2 * i + u) * G, G), :]).then_inc(x_in[u], 16)

        @block.gpsimd
        def _(pool):
            nc.gpsimd.memset(eps_sb[:], EPS).then_inc(eps_ready, 1)
            nc.gpsimd.tensor_scalar(inside[:], slots[:], float(last_slot), None, ALU.min).then_inc(inside_ready, 1)
            pool.wait_ge(inside_ready, 1)
            pool.wait_ge(eps_ready, 1)
            with pool.Fori(0, GROUPS // 2) as i:
                for u in range(2):
                    pool.wait_ge(summed, 2 * i + (u + 1))
                    nc.gpsimd.tensor_copy(inside_now[:, u, :], inside[:, bass.ds((2 * i + u) * G, G)]).then_inc(now_ready, 1)
                    pool.wait_ge(now_ready, 2 * i + (u + 1))
                    nc.gpsimd.tensor_tensor(spare_p[:], eps_sb[:], eps_sb[:], ALU.add)
                    for j in range(G):
                        nc.gpsimd.indirect_dma_start(y[:, u, j, :], None, eo[:],
                                                     bass.IndirectOffsetOnAxis(ap=inside_now[:, u, j:j + 1], axis=0)).then_inc(gathered[u], 16)

        @block.scalar
        def _(act):
            act.wait_ge(eps_ready, 1)
            with act.Fori(0, GROUPS // 2) as i:
                for u in range(2):
                    g = act.snap(2 * i + u)
                    act.wait_ge(var_ready, g + 1)
                    nc.scalar.activation(rstd[:], mv[:, :, 1], ACT.Sqrt, bias=eps_sb[:]).then_inc(std_ready, 1)
                    act.wait_ge(normed, g + 1)
                    act.dma_start(x2.rearrange("(i p) d -> p i d", p=P)[:, bass.ds(g * G, G), :], xt[:, u, :, :]).then_inc(stored[u], 16)
            for u in range(2):
                act.wait_ge(stored[u], 8 * GROUPS)

        @block.vector
        def _(dve):
            dve.sem_inc(summed, 2)
            with dve.Fori(0, GROUPS // 2) as i:
                for u in range(2):
                    g = dve.snap(2 * i + u)
                    rows = xt[:, u, :, :]
                    dve.wait_ge(x_in[u], i * 16 + 16)
                    dve.wait_ge(gathered[u], i * (16 * G) + 16 * G)
                    for j in range(G):
                        ins = nc.vector.scalar_tensor_tensor(out=rows[:, j, :], in0=y[:, u, j, :], scalar=weight[:, bass.ds(g * G + j, 1)],
                                                             in1=rows[:, j, :], op0=ALU.mult, op1=ALU.add)
                    ins.then_inc(summed, 1)
                    dve.wait_ge(summed, g + 3)
                    layernorm_tiles(nc, dve, rows, stats, mv, rstd, spare, G, g + 1, stat_step, var_ready, std_ready, rstd_ready, normed)
                    dve.wait_ge(normed, g + 1)

def sorted_experts(nc, x3, slot_table, tile_expert, w, b, eo):
    E, J = EXPERTS, SLOT_TILES
    with ExitStack() as stack:
        s = Scope(nc, stack, "top1")
        ident = s.sbuf("ident", [P, P])
        w_sb = s.sbuf("w", [P, KD, E * D])
        b_sb = s.sbuf("b", [1, E * D])
        one_row = s.sbuf("one_row", [1, P])
        ids = s.sbuf("ids", [P, J], I32)
        ids_now = s.sbuf("ids_now", [P, 2, 2], I32)
        spare = s.sbuf("spare", [P, 1])
        xg = s.sbuf("xg", [P, 2, D])
        xT = s.sbuf("xT", [P, 2, D])
        out_sb = s.sbuf("out", [P, J, D])
        t_ps = s.psum("t", [P, 2, BANK])
        o_ps = s.psum("o", [P, 2, BANK])

        zeroed = s.sem("zeroed")
        ident_ready = s.sem("ident_ready")
        ones_ready = s.sem("ones_ready")
        ids_in = s.sem("ids_in")
        w_in = s.sem("w_in")
        ids_ready = s.sem("ids_ready")
        gathered = [s.sem(f"gathered{u}") for u in range(2)]
        turned = s.sem("turned")
        xT_ready = s.sem("xT_ready")
        o_full = s.sem("o_full")
        o_ready = s.sem("o_ready")
        stored = s.sem("stored")
        block = stack.enter_context(nc.Block())

        @block.sync
        def _(sp):
            sp.dma_start(ids[:], slot_table[0:P * J, :].rearrange("(p j) a -> p (j a)", p=P)).then_inc(ids_in, 16)
            sp.dma_start(w_sb[:].rearrange("p k (e d) -> p k e d", e=E)[:, 0], w.rearrange("e (k p) d -> k p e d", p=P)[0]).then_inc(w_in, 16)
            sp.dma_start(w_sb[:].rearrange("p k (e d) -> p k e d", e=E)[:, 1], w.rearrange("e (k p) d -> k p e d", p=P)[1]).then_inc(w_in, 16)
            sp.dma_start(b_sb[:], b.rearrange("(a e) d -> a (e d)", a=1)).then_inc(w_in, 16)
            sp.wait_ge(o_ready, J + 2)
            sp.dma_start(eo.rearrange("(p j) d -> p j d", p=P), out_sb[:]).then_inc(stored, 16)
            sp.wait_ge(stored, 16)

        @block.gpsimd
        def _(pool):
            make_identity(nc, s, ident, pool, zeroed, ident_ready)
            nc.gpsimd.memset(one_row[:], 1.0).then_inc(ones_ready, 1)
            pool.wait_ge(ids_in, 16)
            pool.wait_ge(ident_ready, 1)
            with pool.Fori(0, J // 2) as i:
                for u in range(2):
                    pool.wait_ge(turned, 2 * i + (u + 1))
                    nc.gpsimd.tensor_copy(ids_now[:, u, 0:1], ids[:, bass.ds(2 * i + u, 1)]).then_inc(ids_ready, 1)
                    pool.wait_ge(ids_ready, 2 * i + (u + 1))
                    nc.gpsimd.tensor_tensor(spare[:], ident[:, 0:1], ident[:, 0:1], ALU.add)
                    nc.gpsimd.indirect_dma_start(xg[:, u, :], None, x3[:],
                                                 bass.IndirectOffsetOnAxis(ap=ids_now[:, u, 0:1], axis=0)).then_inc(gathered[u], 16)

        @block.scalar
        def _(act):
            with act.Fori(0, J // 2) as i:
                for u in range(2):
                    act.wait_ge(turned, 2 * i + (u + 3))
                    act.wait_ge(o_full, 2 * i + (u + 1))
                    nc.scalar.activation(xT[:, u, :], t_ps[:, u, 0:D], ACT.Copy).then_inc(xT_ready, 1)

        @block.tensor
        def _(pe):
            pe.wait_ge(ident_ready, 1)
            pe.wait_ge(ones_ready, 1)
            pe.wait_ge(w_in, 48)
            with pe.Fori(0, J // 2) as i:
                for u in range(2):
                    pe.wait_ge(gathered[u], 16 * i + 16)
                    pe.wait_ge(xT_ready, 2 * i + (u + 1))
                    for k in range(KD):
                        ins = nc.tensor.transpose(t_ps[:, u, k * P:(k + 1) * P], xg[:, u, k * P:(k + 1) * P], ident[:])
                    ins.then_inc(turned, 1)
                for u in range(2):
                    first = pe.value_load(tile_expert[0:1, bass.ds(2 * i + u, 1)], min_val=0, max_val=E - 1) * D
                    pe.wait_ge(xT_ready, 2 * i + (u + 3))
                    pe.wait_ge(o_ready, 2 * i + (u + 1))
                    for k in range(KD):
                        nc.tensor.matmul(o_ps[:, u, 0:D], xT[:, u, k * P:(k + 1) * P], w_sb[:, k, bass.ds(first, D)], start=(k == 0), stop=False)
                    nc.tensor.matmul(o_ps[:, u, 0:D], one_row[:], b_sb[:, bass.ds(first, D)], start=False, stop=True).then_inc(o_full, 1)

        @block.vector
        def _(dve):
            dve.sem_inc(turned, 2)
            dve.sem_inc(xT_ready, 2)
            dve.sem_inc(o_full, 2)
            dve.sem_inc(o_ready, 2)
            with dve.Fori(0, J // 2) as i:
                for u in range(2):
                    dve.wait_ge(o_full, 2 * i + (u + 3))
                    nc.vector.tensor_copy(out_sb[:, bass.ds(2 * i + u, 1), :].rearrange("p a d -> p (a d)"), o_ps[:, u, 0:D]).then_inc(o_ready, 1)


def retention_tables(nc, freqs, gamma, cos_t, decay_t, undo_t):
    HEAD = freqs.shape[1]
    M = freqs.shape[0] * HEAD // P
    HB = P // HEAD
    PI = 3.141592653589793
    MAGIC = 12582912.0
    parts, rest = [], 2 * PI
    for bits in (5, 14, 22):
        parts.append(int(rest * 2 ** bits) / 2 ** bits)
        rest -= parts[-1]
    parts.append(rest)
    with ExitStack() as stack:
        s = Scope(nc, stack, "tab")
        time_i = s.sbuf("time_i", [P, T], I32)
        time = s.sbuf("time", [P, T])
        freq_sb = s.sbuf("freq", [P, M])
        gam = s.sbuf("gam", [P, M])
        half_pi = s.sbuf("half_pi", [P, 1])
        angle = s.sbuf("angle", [P, 2, T])
        turns = s.sbuf("turns", [P, T])
        decay = s.sbuf("decay", [P, 2, T])
        undo = s.sbuf("undo", [P, 2, T])

        consts_in = s.sem("consts_in")
        filled = s.sem("filled")
        time_ready = s.sem("time_ready")
        gam_ready = s.sem("gam_ready")
        log_ready = s.sem("log_ready")
        step = s.sem("step")
        reduced = s.sem("reduced")
        folded = s.sem("folded")
        cos_ready = s.sem("cos_ready")
        decay_ready = s.sem("decay_ready")
        undo_ready = s.sem("undo_ready")
        stored = s.sem("stored")
        block = stack.enter_context(nc.Block())

        @block.sync
        def _(sp):
            sp.dma_start(freq_sb[:], freqs.rearrange("(m h) d -> (h d) m", m=M), allow_slow_non_contiguous=True).then_inc(consts_in, 16)
            for h in range(HB):
                src = gamma.rearrange("(m h) a b -> h (m a b)", m=M)[h]
                sp.dma_start(gam[h * HEAD:(h + 1) * HEAD, :], src.partition_broadcast(HEAD), allow_slow_non_contiguous=True).then_inc(consts_in, 16)
            for m in range(M):
                sp.wait_ge(decay_ready, m + 1)
                sp.dma_start(decay_t[m], decay[:, m % 2, :]).then_inc(stored, 16)
                sp.wait_ge(undo_ready, m + 1)
                sp.dma_start(undo_t[m], undo[:, m % 2, :]).then_inc(stored, 16)
                sp.wait_ge(cos_ready, m + 1)
                sp.dma_start(cos_t[m], angle[:, m % 2, :]).then_inc(stored, 16)
                sp.wait_ge(stored, 48 * (m + 1))

        @block.gpsimd
        def _(pool):
            nc.gpsimd.memset(half_pi[:], PI / 2).then_inc(filled, 1)
            nc.gpsimd.iota(time_i[:], pattern=[[1, T]], base=0, channel_multiplier=0).then_inc(filled, 1)

        @block.scalar
        def _(act):
            act.wait_ge(gam_ready, 1)
            nc.scalar.activation(gam[:], gam[:], ACT.Ln).then_inc(log_ready, 1)
            act.wait_ge(time_ready, 1)
            act.wait_ge(log_ready, 1)
            for m in range(M):
                if m >= 2:
                    act.wait_ge(stored, 48 * (m - 1))
                nc.scalar.activation(decay[:, m % 2, :], time[:], ACT.Exp, scale=gam[:, m:m + 1]).then_inc(decay_ready, 1)
                act.wait_ge(reduced, m + 1)
                nc.scalar.activation(angle[:, m % 2, :], angle[:, m % 2, :], ACT.Abs).then_inc(folded, 1)
                act.wait_ge(folded, m + 1)
                nc.scalar.activation(angle[:, m % 2, :], angle[:, m % 2, :], ACT.Sin, bias=half_pi[:], scale=-1.0).then_inc(cos_ready, 1)

        @block.vector
        def _(dve):
            done = [0]

            def after(ins):
                ins.then_inc(step, 1)
                done[0] += 1
                dve.wait_ge(step, done[0])

            v = nc.vector
            dve.wait_ge(filled, 2)
            v.tensor_copy(time[:], time_i[:]).then_inc(time_ready, 1)
            dve.wait_ge(consts_in, 16 * (1 + HB))
            v.tensor_scalar(gam[:], gam[:], 2.0 ** -64, None, ALU.max).then_inc(gam_ready, 1)
            dve.wait_ge(time_ready, 1)
            for m in range(M):
                r = angle[:, m % 2, :]
                if m >= 2:
                    dve.wait_ge(stored, 48 * (m - 1))
                after(v.tensor_scalar(r, time[:], freq_sb[:, m:m + 1], None, ALU.mult))
                after(v.tensor_scalar(turns[:], r, 1.0 / (2 * PI), MAGIC, ALU.mult, ALU.add))
                after(v.tensor_scalar(turns[:], turns[:], MAGIC, -1.0, ALU.subtract, ALU.mult))
                for k, part in enumerate(parts):
                    ins = v.scalar_tensor_tensor(out=r, in0=turns[:], scalar=float(part), in1=r, op0=ALU.mult, op1=ALU.add)
                    if k < len(parts) - 1:
                        after(ins)
                ins.then_inc(reduced, 1)
                dve.wait_ge(reduced, m + 1)
                dve.wait_ge(decay_ready, m + 1)
                after(v.tensor_scalar(undo[:, m % 2, :], decay[:, m % 2, :], 1e-6, None, ALU.add))
                v.reciprocal(undo[:, m % 2, :], undo[:, m % 2, :]).then_inc(undo_ready, 1)


def retention_layer(nc, x2, conv_w, conv_b, qk_w, v_w, g_w, g_b, o_w, ln_g, ln_b, cos_t, decay_t, undo_t, x3):
    E = qk_w.shape[1]
    M = E // P
    HEAD = 32
    HEADS = E // HEAD
    HB = P // HEAD
    TAPS = 4
    CH = BANK
    Q = T // CH
    G = CH // P
    KINDS = 3
    PROJ_RING, R_RING = 2, 2
    assert B == 2
    with ExitStack() as stack:
        s = Scope(nc, stack, "ret")
        ident = s.sbuf("ident", [P, P])
        heads = s.sbuf("heads", [P, HB])
        members = s.sbuf("members", [HEADS, E])
        inv_t = s.sbuf("inv_t", [HEADS, CH])
        qk_sb = s.sbuf("qk_w", [P, KD, E])
        v_sb = s.sbuf("v_w", [P, KD, E])
        g_sb = s.sbuf("g_w", [P, KD, E])
        o_sb = s.sbuf("o_w", [P, M, D])
        gb_sb = s.sbuf("gb", [P, M])
        cw_sb = s.sbuf("cw", [P, KD, TAPS])
        cb_sb = s.sbuf("cb", [P, KD])
        lng_sb = s.sbuf("lng", [P, D])
        lnb_sb = s.sbuf("lnb", [P, D])
        eps_sb = s.sbuf("eps", [P, 1])
        ones = s.sbuf("ones", [P, CH])
        xt = s.sbuf("xt", [P, B, G, D])
        res = s.sbuf("res", [P, B, G, D])
        xpad = s.sbuf("xpad", [P, B, KD, TAPS - 1 + CH])
        xc = s.sbuf("xc", [P, B, KD, CH])
        qk = s.sbuf("qk", [P, B, M, CH])
        square = s.sbuf("square", [P, M, CH])
        val = s.sbuf("val", [P, B, M, CH])
        gate = s.sbuf("gate", [P, B, M, CH])
        norm = s.sbuf("norm", [P, G * HEADS])
        q = s.sbuf("q", [P, B, M, CH + 1])
        mem = s.sbuf("mem", [P, B, M, CH])
        mem_last = s.sbuf("mem_last", [P, B, M])
        o_in = s.sbuf("o_in", [P, B, M, CH])
        cos_sb = s.sbuf("cos", [P, M, CH])
        decay_sb = s.sbuf("decay", [P, M, CH])
        undo_sb = s.sbuf("undo", [P, M, CH])
        z = s.sbuf("z", [P, G, D])
        stats = s.sbuf("stats", [P, G, 6])
        mv = s.sbuf("mv", [P, 2, G, 2])
        rstd = s.sbuf("rstd", [P, 2, G])
        spare = s.sbuf("spare", [P, 1])

        t_ps = s.psum("t", [P, CH])
        proj = s.psum("proj", [P, PROJ_RING, CH])
        n_ps = s.psum("n_ps", [P, G * HEADS])
        r_ps = s.psum("r_ps", [P, R_RING, CH])
        o_ps = s.psum("o_ps", [P, G, D])

        consts_in = s.sem("consts_in")
        filled = s.sem("filled")
        x_in = [s.sem(f"x_in{b}") for b in range(B)]
        res_in = [s.sem(f"res_in{b}") for b in range(B)]
        tab_in = s.sem("tab_in")
        turned = s.sem("turned")
        xpad_ready = s.sem("xpad_ready")
        xpad_free = s.sem("xpad_free")
        conv_step = s.sem("conv_step")
        xc_ready = s.sem("xc_ready")
        proj_full = s.sem("proj_full")
        proj_taken = s.sem("proj_taken")
        n_full = s.sem("n_full")
        norm_ready = s.sem("norm_ready")
        inv_step = s.sem("inv_step")
        inv_turned = s.sem("inv_turned")
        inv_ready = s.sem("inv_ready")
        r_full = s.sem("r_full")
        q_ready = s.sem("q_ready")
        q_kept = s.sem("q_kept")
        phase_ready = s.sem("phase_ready")
        gated = s.sem("gated")
        undo_ready = s.sem("undo_ready")
        mem_step = s.sem("mem_step")
        o_in_ready = s.sem("o_in_ready")
        o_full = s.sem("o_full")
        o_taken = s.sem("o_taken")
        z_step = s.sem("z_step")
        stat_step = s.sem("stat_step")
        var_ready = s.sem("var_ready")
        std_ready = s.sem("std_ready")
        rstd_ready = s.sem("rstd_ready")
        normed = s.sem("normed")
        res_biased = s.sem("res_biased")
        stored = [s.sem(f"stored{b}") for b in range(B)]

        loads = [
            (qk_sb[:], qk_w.rearrange("(k p) e -> p k e", p=P)),
            (v_sb[:], v_w.rearrange("(k p) e -> p k e", p=P)),
            (g_sb[:], g_w.rearrange("(k p) e -> p k e", p=P)),
            (o_sb[:], o_w.rearrange("(m p) d -> p m d", p=P)),
            (gb_sb[:], g_b.rearrange("(m p) -> p m", p=P)),
            (cw_sb[:], conv_w.rearrange("(k p) a t -> p k (a t)", p=P)),
            (cb_sb[:], conv_b.rearrange("(k p) -> p k", p=P)),
            (lng_sb[:], ln_g.rearrange("(a d) -> a d", a=1).partition_broadcast(P)),
            (lnb_sb[:], ln_b.rearrange("(a d) -> a d", a=1).partition_broadcast(P)),
        ]
        ALL_IN = 16 * len(loads)
        fills = [(ident[:], 0.0), (heads[:], 0.0), (eps_sb[:], EPS), (ones[:], 1.0), (q[:, :, :, 0:1], 0.0), (mem_last[:], 0.0),
                 (xpad[:, :, :, 0:TAPS - 1], 0.0), (members[:], 1.0)]
        ALL_FILLED = len(fills) + 3 + HB
        SUMS = KINDS * M
        TAP_STEPS = (TAPS - 1) * KD
        MEM_STEPS = 4

        def at(c, b):
            return c * B + b

        def neighbours(c, b):
            ahead = (c, 1) if b == 0 else (c + 1, 0)
            back = (c - 1, 1) if b == 0 else (c, 0)
            return ahead, (c, b), back, (c - 1, b)

        def run_steps(engine, step):
            step(-1, 1, True, False, False, False)
            step(0, 0, True, True, False, False)
            step(0, 1, True, True, True, False)
            with engine.Fori(1, Q - 1) as c:
                for b in range(B):
                    step(c, b, True, True, True, True)
            step(Q - 1, 0, True, True, True, True)
            step(Q - 1, 1, False, True, True, True)
            step(Q, 0, False, False, True, True)
            step(Q, 1, False, False, False, True)

        def later(c):
            return not isinstance(c, int) or c > 0

        block = stack.enter_context(nc.Block())

        @block.sync
        def _(sp):
            x_v = x2.rearrange("(i p) d -> p i d", p=P)

            def load_tokens(dst, tile, sem):
                sp.dma_start(dst, x_v[:, bass.ds(tile, G), :]).then_inc(sem, 16)

            def load_table(k, first):
                dst, src = ((cos_sb, cos_t), (decay_sb, decay_t), (undo_sb, undo_t))[k]
                sp.dma_start(dst[:], src.rearrange("m p t -> p m t")[:, :, bass.ds(first, CH)]).then_inc(tab_in, 16)

            for dst, src in loads:
                sp.dma_start(dst, src, allow_slow_non_contiguous=True).then_inc(consts_in, 16)

            def step(c, b, ahead, here, back, last):
                if not ahead and not here:
                    return
                if not here:
                    for b1 in range(B):
                        load_tokens(xt[:, b1, :, :], b1 * (T // P), x_in[b1])
                    for k in range(3):
                        load_table(k, 0)
                    return
                n = held(sp, at(c, b))
                time = held(sp, c * CH)
                tile = held(sp, c * G + b * (T // P))
                gone = held(sp, c * 16)
                if not isinstance(c, int) or c < Q - 1:
                    after = held(sp, (c + 1) * G + b * (T // P))
                    done = held(sp, at(c, b) * KD + KD)
                    sp.wait_ge(turned, done)
                    load_tokens(xt[:, b, :, :], after, x_in[b])
                if b == 0 and later(c):
                    for k, used in enumerate((phase_ready, gated, undo_ready)):
                        sp.wait_ge(used, n)
                        load_table(k, time)
                if later(c):
                    sp.wait_ge(stored[b], gone)
                load_tokens(res[:, b, :, :], tile, res_in[b])

            run_steps(sp, step)

        @block.gpsimd
        def _(pool):
            for k, (dst, value) in enumerate(fills):
                nc.gpsimd.memset(dst, value).then_inc(filled, 1)
                pool.wait_ge(filled, k + 1)
            nc.gpsimd.affine_select(out=ident[:], in_=ident[:], compare_op=ALU.not_equal, fill=1.0, base=0,
                                    pattern=[[-1, P]], channel_multiplier=1).then_inc(filled, 1)
            nc.gpsimd.affine_select(out=members[:], in_=members[:], compare_op=ALU.is_ge, fill=0.0, base=0,
                                    pattern=[[1, E]], channel_multiplier=-HEAD).then_inc(filled, 1)
            pool.wait_ge(filled, len(fills) + 2)
            nc.gpsimd.affine_select(out=members[:], in_=members[:], compare_op=ALU.is_ge, fill=0.0, base=HEAD - 1,
                                    pattern=[[-1, E]], channel_multiplier=HEAD).then_inc(filled, 1)
            for h in range(HB):
                nc.gpsimd.memset(heads[h * HEAD:(h + 1) * HEAD, h:h + 1], 1.0).then_inc(filled, 1)
                pool.wait_ge(filled, len(fills) + 4 + h)
            pool.wait_ge(consts_in, ALL_IN)

            def step(c, b, ahead, here, back, last):
                if not back:
                    return
                c1, b1 = neighbours(c, b)[2]
                n = at(c1, b1)
                pool.wait_ge(q_ready, M * (n + 1))
                pool.wait_ge(tab_in, c1 * 48 + 48)
                if later(c1):
                    pool.wait_ge(o_in_ready, n - 1)
                nc.gpsimd.tensor_tensor(mem[:, b1, :, :], cos_sb[:], q[:, b1, :, 0:CH], ALU.add).then_inc(phase_ready, 1)
                pool.wait_ge(proj_taken, SUMS * (n + 1))
                nc.gpsimd.tensor_tensor(gate[:, b1, :, :], gate[:, b1, :, :], decay_sb[:], ALU.mult).then_inc(gated, 1)
                if later(c1):
                    pool.wait_ge(o_full, n - 1)
                nc.gpsimd.tensor_tensor(o_in[:, b1, :, :], undo_sb[:], q[:, b1, :, 1:CH + 1], ALU.mult).then_inc(undo_ready, 1)
                pool.wait_ge(res_in[b1], c1 * 16 + 16)
                nc.gpsimd.tensor_tensor(res[:, b1, :, :], res[:, b1, :, :], lnb_sb[:].unsqueeze(1).broadcast_to([P, G, D]), ALU.add).then_inc(res_biased, 1)

            run_steps(pool, step)

        @block.scalar
        def _(act):
            act.wait_ge(consts_in, ALL_IN)
            act.wait_ge(filled, ALL_FILLED)

            def step(c, b, ahead, here, back, last):
                (c0, b0), _, _, (c2, b2) = neighbours(c, b)

                def take_turned(k):
                    n = at(c0, b0)
                    act.wait_ge(turned, KD * n + (k + 1))
                    if later(c0):
                        act.wait_ge(xpad_free, n - 1)
                    nc.scalar.activation(xpad[:, b0, k, TAPS - 1:], t_ps[:], ACT.Copy).then_inc(xpad_ready, 1)

                def take(kind, m):
                    n = at(c, b)
                    i = kind * M + m
                    bank = proj[:, i % PROJ_RING, :]
                    act.wait_ge(proj_full, SUMS * n + (i + 1))
                    if kind == 0:
                        nc.scalar.activation(qk[:, b, m, :], bank, ACT.Copy)
                        ins = nc.scalar.activation(square[:, m, :], bank, ACT.Square)
                    elif kind == 1:
                        ins = nc.scalar.activation(val[:, b, m, :], bank, ACT.Copy)
                    else:
                        ins = nc.scalar.activation(gate[:, b, m, :], bank, ACT.Sigmoid, bias=gb_sb[:, m:m + 1])
                    ins.then_inc(proj_taken, 1)

                def root(r):
                    n = at(c2, b2)
                    act.wait_ge(var_ready, 2 * n + (r + 1))
                    nc.scalar.activation(rstd[:, r, :], mv[:, r, :, 1], ACT.Sqrt, bias=eps_sb[:]).then_inc(std_ready, 1)

                if ahead:
                    take_turned(0)
                if here:
                    n = at(c, b)
                    if later(c):
                        act.wait_ge(o_in_ready, n - 1)
                    if not isinstance(n, int) or n > 0:
                        act.wait_ge(n_full, n)
                    take(0, 0)
                    take(0, 1)
                if last:
                    root(0)
                if here:
                    take(0, 2)
                if ahead:
                    take_turned(1)
                if here:
                    take(0, 3)
                    take(1, 0)
                if last:
                    root(1)
                if here:
                    take(1, 1)
                    take(1, 2)
                    take(1, 3)
                    n = at(c, b)
                    act.wait_ge(n_full, n + 1)
                    if not isinstance(n, int) or n > 0:
                        act.wait_ge(inv_turned, n)
                    nc.scalar.activation(norm[:], n_ps[:], ACT.Sqrt).then_inc(norm_ready, 1)
                    for m in range(M):
                        take(2, m)
                    act.wait_ge(inv_turned, n + 1)
                    if not isinstance(n, int) or n > 0:
                        act.wait_ge(r_full, M * n)
                    nc.scalar.activation(inv_t[:], t_ps[0:HEADS, :], ACT.Copy).then_inc(inv_ready, 1)
                if last:
                    act.wait_ge(normed, at(c2, b2) + 1)
                    act.dma_start(x3.rearrange("(i p) d -> p i d", p=P)[:, bass.ds(b2 * (T // P) + c2 * G, G), :], res[:, b2, :, :]).then_inc(stored[b2], 16)

            run_steps(act, step)
            for b in range(B):
                act.wait_ge(stored[b], 16 * Q)

        @block.tensor
        def _(pe):
            pe.wait_ge(consts_in, ALL_IN)
            pe.wait_ge(filled, ALL_FILLED)

            def step(c, b, ahead, here, back, last):
                (c0, b0), _, (c1, b1), _ = neighbours(c, b)

                def turn(k):
                    n = at(c0, b0)
                    pe.wait_ge(x_in[b0], c0 * 16 + 16)
                    if k:
                        pe.wait_ge(xpad_ready, KD * n + k)
                    elif not isinstance(n, int) or n > 0:
                        if here and (not isinstance(at(c, b), int) or at(c, b) > 0):
                            pe.wait_ge(inv_ready, at(c, b))
                        else:
                            pe.wait_ge(xpad_ready, KD * n)
                    for j in range(G):
                        ins = nc.tensor.transpose(t_ps[:, j * P:(j + 1) * P], xt[:, b0, j, k * P:(k + 1) * P], ident[:])
                    ins.then_inc(turned, 1)

                def project(kind, m):
                    n = at(c, b)
                    i = kind * M + m
                    if i >= PROJ_RING or not isinstance(n, int) or n > 0:
                        pe.wait_ge(proj_taken, SUMS * n + (i + 1 - PROJ_RING))
                    w = (qk_sb, v_sb, g_sb)[kind]
                    for k in range(KD):
                        ins = nc.tensor.matmul(proj[:, i % PROJ_RING, :], w[:, k, m * P:(m + 1) * P], xc[:, b, k, :], start=(k == 0), stop=(k == KD - 1))
                    ins.then_inc(proj_full, 1)

                def turn_inverse():
                    n = at(c, b)
                    pe.wait_ge(inv_step, 2 * n + 2)
                    if ahead:
                        pe.wait_ge(xpad_ready, KD * (at(c0, b0) + 1))
                    for j in range(G):
                        ins = nc.tensor.transpose(t_ps[0:HEADS, j * P:(j + 1) * P], norm[:, j * HEADS:(j + 1) * HEADS], ident[:])
                    ins.then_inc(inv_turned, 1)

                def spread(m):
                    n = at(c, b)
                    pe.wait_ge(inv_ready, n + 1)
                    if m >= R_RING or not isinstance(n, int) or n > 0:
                        pe.wait_ge(q_ready, M * n + (m + 1 - R_RING))
                    nc.tensor.matmul(r_ps[:, m % R_RING, :], members[:, m * P:(m + 1) * P], inv_t[:], start=True, stop=True).then_inc(r_full, 1)

                if ahead:
                    turn(0)
                if here:
                    pe.wait_ge(xc_ready, KD * (at(c, b) + 1))
                    for m in range(M - 1):
                        project(0, m)
                if ahead:
                    turn(1)
                if here:
                    project(0, M - 1)
                    for m in range(M):
                        project(1, m)
                    n = at(c, b)
                    pe.wait_ge(proj_taken, SUMS * n + M)
                    if not isinstance(n, int) or n > 0:
                        pe.wait_ge(norm_ready, n)
                    for j in range(G):
                        for m in range(M):
                            first = j * HEADS + m * HB
                            ins = nc.tensor.matmul(n_ps[:, first:first + HB], square[:, m, j * P:(j + 1) * P], heads[:], start=True, stop=True)
                    ins.then_inc(n_full, 1)
                    for m in range(M):
                        project(2, m)
                    turn_inverse()
                if back:
                    n = at(c1, b1)
                    pe.wait_ge(o_in_ready, n + 1)
                    if not isinstance(n, int) or n > 0:
                        pe.wait_ge(o_taken, n)
                    for j in range(G):
                        for m in range(M):
                            ins = nc.tensor.matmul(o_ps[:, j, :], o_in[:, b1, m, j * P:(j + 1) * P], o_sb[:, m, :], start=(m == 0), stop=(m == M - 1))
                    ins.then_inc(o_full, 1)
                if here:
                    for m in range(M):
                        spread(m)

            run_steps(pe, step)

        @block.vector
        def _(dve):
            dve.wait_ge(consts_in, ALL_IN)
            dve.wait_ge(filled, ALL_FILLED)
            v = nc.vector

            def step(c, b, ahead, here, back, last):
                (c0, b0), _, (c1, b1), (c2, b2) = neighbours(c, b)

                def tap(t):
                    n = at(c0, b0)
                    for k in range(KD):
                        src = xpad[:, b0, k, t:t + CH]
                        dst = xc[:, b0, k, :]
                        if t == 0:
                            dve.wait_ge(xpad_ready, KD * n + (k + 1))
                            if later(c0):
                                dve.wait_ge(proj_full, SUMS * (n - 1))
                            ins = v.tensor_scalar(dst, src, cw_sb[:, k, 0:1], cb_sb[:, k:k + 1], ALU.mult, ALU.add)
                        else:
                            dve.wait_ge(conv_step, TAP_STEPS * n + ((t - 1) * KD + k + 1))
                            ins = v.scalar_tensor_tensor(out=dst, in0=src, scalar=cw_sb[:, k, t:t + 1], in1=dst, op0=ALU.mult, op1=ALU.add)
                        ins.then_inc(xc_ready if t == TAPS - 1 else conv_step, 1)

                def keep_history():
                    dve.wait_ge(xc_ready, KD * (at(c0, b0) + 1))
                    v.tensor_copy(xpad[:, b0, :, 0:TAPS - 1], xpad[:, b0, :, CH:CH + TAPS - 1]).then_inc(xpad_free, 1)

                def statistics(rows, r):
                    n = at(c2, b2)
                    for j in range(G):
                        ins = v.bn_stats(stats[:, j, :], rows[:, j, :])
                    ins.then_inc(stat_step, 1)
                    dve.wait_ge(stat_step, 2 * n + (r + 1))
                    v.memset(spare[:], 0.0)
                    for j in range(G):
                        ins = v.bn_aggr(mv[:, r, j, :], stats[:, j, :])
                    ins.then_inc(var_ready, 1)

                def invert_root(r):
                    n = at(c2, b2)
                    dve.wait_ge(std_ready, 2 * n + (r + 1))
                    v.reciprocal(rstd[:, r, :], rstd[:, r, :]).then_inc(rstd_ready, 1)
                    dve.wait_ge(rstd_ready, 2 * n + (r + 1))

                if last:
                    n = at(c2, b2)
                    rows = res[:, b2, :, :]
                    dve.wait_ge(o_full, n + 1)
                    statistics(o_ps, 0)
                    dve.wait_ge(var_ready, 2 * n + 1)
                    for j in range(G):
                        ins = v.scalar_tensor_tensor(out=z[:, j, :], in0=o_ps[:, j, :], scalar=mv[:, 0, j, 0:1], in1=lng_sb[:], op0=ALU.subtract, op1=ALU.mult)
                    ins.then_inc(o_taken, 1)
                if ahead:
                    tap(0)
                    tap(1)
                if last:
                    invert_root(0)
                    dve.wait_ge(o_taken, n + 1)
                    dve.wait_ge(res_biased, n + 1)
                    for j in range(G):
                        ins = v.scalar_tensor_tensor(out=rows[:, j, :], in0=z[:, j, :], scalar=rstd[:, 0, j:j + 1], in1=rows[:, j, :], op0=ALU.mult, op1=ALU.add)
                    ins.then_inc(z_step, 1)
                    dve.wait_ge(z_step, n + 1)
                    statistics(rows, 1)
                if ahead:
                    tap(2)
                    tap(3)
                    keep_history()
                if back:
                    n1 = at(c1, b1)
                    rows1 = mem[:, b1, :, :]
                    dve.wait_ge(phase_ready, n1 + 1)
                    v.tensor_tensor(rows1, rows1, val[:, b1, :, :], ALU.mult).then_inc(mem_step, 1)
                    dve.wait_ge(mem_step, MEM_STEPS * n1 + 1)
                    dve.wait_ge(gated, n1 + 1)
                    v.tensor_tensor(rows1, rows1, gate[:, b1, :, :], ALU.mult).then_inc(mem_step, 1)
                if last:
                    invert_root(1)
                    for j in range(G):
                        ins = v.tensor_scalar(rows[:, j, :], rows[:, j, :], mv[:, 1, j, 0:1], rstd[:, 1, j:j + 1], ALU.subtract, ALU.mult)
                    ins.then_inc(normed, 1)
                if here:
                    n3 = at(c, b)
                    dve.wait_ge(norm_ready, n3 + 1)
                    v.tensor_scalar(norm[:], norm[:], 1e-12, None, ALU.max).then_inc(inv_step, 1)
                    dve.wait_ge(inv_step, 2 * n3 + 1)
                    v.reciprocal(norm[:], norm[:]).then_inc(inv_step, 1)
                if back:
                    dve.wait_ge(mem_step, MEM_STEPS * n1 + 2)
                    for m in range(M):
                        ins = v.tensor_tensor_scan(mem[:, b1, m, :], ones[:], mem[:, b1, m, :], mem_last[:, b1, m:m + 1], ALU.mult, ALU.add)
                    ins.then_inc(mem_step, 1)
                    dve.wait_ge(mem_step, MEM_STEPS * n1 + 3)
                    v.tensor_copy(mem_last[:, b1, :], mem[:, b1, :, CH - 1]).then_inc(mem_step, 1)
                    dve.wait_ge(undo_ready, n1 + 1)
                    v.tensor_tensor(o_in[:, b1, :, :], rows1, o_in[:, b1, :, :], ALU.mult).then_inc(o_in_ready, 1)
                if here:
                    if later(c):
                        dve.wait_ge(undo_ready, n3 - 1)
                        v.tensor_copy(q[:, b, :, 0:1], q[:, b, :, CH:CH + 1]).then_inc(q_kept, 1)
                        dve.wait_ge(q_kept, n3 - 1)
                    for m in range(M):
                        dve.wait_ge(r_full, M * n3 + (m + 1))
                        v.tensor_tensor(q[:, b, m, 1:CH + 1], qk[:, b, m, :], r_ps[:, m % R_RING, :], ALU.mult).then_inc(q_ready, 1)

            run_steps(dve, step)


def program(nc, a, out):
    x1, x2, x3 = (nc.dram_tensor(name, [N, D], F32) for name in ("x1", "x2", "x3"))
    state_space_layer(nc, a["x_tok"], a["x_feat"], a["L0_attn_Win"], a["L0_attn_b_in"], a["L0_attn_A_log"],
                      a["L0_attn_B_param"], a["L0_attn_C_param"], a["L0_attn_Wdt"], a["L0_attn_b_dt"],
                      a["L0_attn_Wconv"], a["L0_attn_Wout"], a["L0_attn_b_out"], x1)
    capacity = max(-(-3 * N // (2 * EXPERTS)), 1)
    slot_table = nc.dram_tensor("slot_table", [EXPERTS * capacity + N, 1], I32)
    eo = nc.dram_tensor("eo", [EXPERTS * capacity, D], F32)
    with ExitStack() as stack:
        s = Scope(nc, stack, "moe")
        slots = s.sbuf("slots", [P, TOKEN_TILES], I32)
        weight = s.sbuf("weight", [P, TOKEN_TILES])
        route(nc, "route", x1, a["L0_ffn_router_w"], None, slot_table, slots, weight, capacity)
        capacity_experts(nc, x1, slot_table, a["L0_ffn_w1"], a["L0_ffn_b1"], a["L0_ffn_w2"], a["L0_ffn_b2"], eo, capacity)
        combine(nc, "comb", x1, eo, slots, weight, x2, EXPERTS * capacity - 1)
    H, HD = a["L1_attn_freqs"].shape
    cos_t, decay_t, undo_t = (nc.dram_tensor(name, [H * HD // P, P, T], F32) for name in ("cos_t", "decay_t", "undo_t"))
    retention_tables(nc, a["L1_attn_freqs"], a["L1_attn_gamma"], cos_t, decay_t, undo_t)
    retention_layer(nc, x2, a["L1_attn_conv_w"], a["L1_attn_conv_b"], a["L1_attn_qk_w"], a["L1_attn_v_w"],
                    a["L1_attn_g_w"], a["L1_attn_g_b"], a["L1_attn_o_w"], a["L1_attn_ln_g"], a["L1_attn_ln_b"],
                    cos_t, decay_t, undo_t, x3)
    slot_table2 = nc.dram_tensor("slot_table2", [P * SLOT_TILES, 1], I32)
    eo2 = nc.dram_tensor("eo2", [P * SLOT_TILES, D], F32)
    with ExitStack() as stack:
        s = Scope(nc, stack, "moe2")
        slots = s.sbuf("slots", [P, TOKEN_TILES], I32)
        weight = s.sbuf("weight", [P, TOKEN_TILES])
        tile_expert = s.sbuf("tile_expert", [1, SLOT_TILES], I32)
        route(nc, "route2", x3, a["L1_ffn_router_w"], a["L1_ffn_router_b"], slot_table2, slots, weight, None, tile_expert)
        sorted_experts(nc, x3, slot_table2, tile_expert, a["L1_ffn_expert_w"], a["L1_ffn_expert_b"], eo2)
        combine(nc, "comb2", x3, eo2, slots, weight, out, P * SLOT_TILES - 1)


TRANSPOSED = ["L0_attn_Win", "L0_attn_Wdt", "L0_attn_Wout", "L0_ffn_router_w", "L1_attn_qk_w", "L1_attn_v_w",
              "L1_attn_g_w", "L1_attn_o_w", "L1_ffn_router_w"]


def kernel(**inputs):
    import numpy as np
    import concourse.bacc as bacc
    from concourse.bass_utils import run_bass_kernel_spmd

    arrays = {}
    for name, value in inputs.items():
        value = np.asarray(value)
        if name == "L0_attn_input":
            tokens = value.reshape(N, D)
            arrays["x_tok"] = np.ascontiguousarray(tokens)
            arrays["x_feat"] = np.ascontiguousarray(tokens.T)
        elif name in TRANSPOSED:
            arrays[name] = np.ascontiguousarray(value.T)
        elif name == "L1_ffn_expert_w":
            arrays[name] = np.ascontiguousarray(value.transpose(0, 2, 1))
        else:
            arrays[name] = np.ascontiguousarray(value)
    nc = bacc.Bacc("TRN2", target_bir_lowering=False, num_devices=1)
    a = {n: nc.dram_tensor(f"in_{n}", v.shape, mybir.dt.from_np(v.dtype), kind="ExternalInput").ap() for n, v in arrays.items()}
    out = nc.dram_tensor("out", (N, D), F32, kind="ExternalOutput").ap()
    program(nc, a, out)
    r = run_bass_kernel_spmd(nc, [{f"in_{n}": v for n, v in arrays.items()}], core_ids=[0])
    return r.results[0]["out"].reshape(B, T, D)
```

```python
from contextlib import ExitStack

import concourse.bass as bass
from concourse import mybir

F32 = mybir.dt.float32
BF16 = mybir.dt.bfloat16
I32 = mybir.dt.int32
U32 = mybir.dt.uint32
ALU = mybir.AluOpType
ACT = mybir.ActivationFunctionType
AX = mybir.AxisListType

P = 128
B, T, D = 2, 2048, 256
N = B * T
KD = D // P
EPS = 1e-5
BANK = 512


class Scope:

    def __init__(self, nc, stack, prefix):
        self.nc, self.stack, self.prefix, self.sems = nc, stack, prefix, []
        stack.callback(self.clear)

    def sbuf(self, name, shape, dtype=F32):
        return self.stack.enter_context(self.nc.sbuf_tensor(f"{self.prefix}_{name}", shape, dtype))

    def psum(self, name, shape, dtype=F32):
        return self.stack.enter_context(self.nc.psum_tensor(f"{self.prefix}_{name}", shape, dtype))

    def sem(self, name):
        self.sems.append(self.nc.alloc_semaphore(f"{self.prefix}_{name}"))
        return self.sems[-1]

    def clear(self):
        if self.sems:
            self.nc.clear_and_free_semaphores(self.sems)
            self.nc.all_engine_barrier()

    def dram(self, name, shape, dtype=F32):
        return self.nc.dram_tensor(f"{self.prefix}_{name}", shape, dtype)


def make_identity(nc, s, ident, engine, zeroed, made):
    nc.gpsimd.memset(ident[:], 0.0).then_inc(zeroed, 1)
    engine.wait_ge(zeroed, 1)
    nc.gpsimd.affine_select(out=ident[:], in_=ident[:], compare_op=ALU.not_equal, fill=1.0, base=0,
                            pattern=[[-1, P]], channel_multiplier=1).then_inc(made, 1)


EXPERTS = 8
TOKEN_TILES = N // P
SLOT_TILES = TOKEN_TILES + EXPERTS


def layernorm_tiles(nc, dve, rows, stats, mv, rstd, spare, tiles, k, stat_step, var_ready, std_ready,
                    rstd_ready, normed, dst=None):
    dst = rows if dst is None else dst
    for j in range(tiles):
        ins = nc.vector.bn_stats(stats[:, j, :], rows[:, j, :])
    ins.then_inc(stat_step, 1)
    dve.wait_ge(stat_step, k)
    nc.vector.memset(spare[:], 0.0)
    for j in range(tiles):
        ins = nc.vector.bn_aggr(mv[:, j, :], stats[:, j, :])
    ins.then_inc(var_ready, 1)
    dve.wait_ge(std_ready, k)
    nc.vector.reciprocal(rstd[:], rstd[:]).then_inc(rstd_ready, 1)
    dve.wait_ge(rstd_ready, k)
    for j in range(tiles):
        ins = nc.vector.tensor_scalar(dst[:, j, :], rows[:, j, :], mv[:, j, 0:1], rstd[:, j:j + 1], ALU.subtract, ALU.mult)
    ins.then_inc(normed, 1)


def layernorm_stats(nc, dve, rows, stats, mv, spare, tiles, k, stat_step, var_ready):
    for j in range(tiles):
        ins = nc.vector.bn_stats(stats[:, j, :], rows[:, j, :])
    ins.then_inc(stat_step, 1)
    dve.wait_ge(stat_step, k)
    nc.vector.memset(spare[:], 0.0)
    for j in range(tiles):
        ins = nc.vector.bn_aggr(mv[:, j, :], stats[:, j, :])
    ins.then_inc(var_ready, 1)


def layernorm_apply(nc, dve, rows, dst, mv, rstd, tiles, k, std_ready, rstd_ready, normed):
    dve.wait_ge(std_ready, k)
    nc.vector.reciprocal(rstd[:], rstd[:]).then_inc(rstd_ready, 1)
    dve.wait_ge(rstd_ready, k)
    for j in range(tiles):
        ins = nc.vector.tensor_scalar(dst[:, j, :], rows[:, j, :], mv[:, j, 0:1], rstd[:, j:j + 1], ALU.subtract, ALU.mult)
    ins.then_inc(normed, 1)


def held(engine, value):
    return value if isinstance(value, int) else engine.snap(value)


def state_space_layer(nc, x_tok, x_feat, win, b_in, a_log, b_param, c_param, wdt, b_dt, wconv, wout,
                      b_out, x1):
    DI, NS, RANK, TAPS = 512, 16, 64, 4
    M = DI // P
    CH = 1024
    CHUNKS = N // CH
    HALVES = CH // BANK
    STEPS = M * NS
    TILES = CH // P
    TG = 4
    OUTS = TILES // TG
    A_RING, DBX_RING, H_RING = 2, 4, 4
    COLS = DI * 2 + RANK + NS
    B_LO = 96
    B_HI = B_LO + NS
    RB = 2 * DI

    with ExitStack() as stack:
        s = Scope(nc, stack, "ssm")
        win_sb = s.sbuf("win", [P, KD, RB + B_HI])
        wout_sb = s.sbuf("wout", [P, M, D])
        wdt_sb = s.sbuf("wdt", [RANK + 1, DI])
        conv_sb = s.sbuf("conv", [P, M, TAPS])
        bv_sb = s.sbuf("bv", [P, M])
        bx_sb = s.sbuf("bx", [P, M])
        brb_sb = s.sbuf("brb", [B_HI, 1])
        bparam_sb = s.sbuf("bparam", [B_HI, 1])
        a_sb = s.sbuf("a", [P, M, NS])
        c_sb = s.sbuf("c", [P, M, NS])
        bout_sb = s.sbuf("bout", [P, D])
        ident = s.sbuf("ident", [P, P])
        diag_c = s.sbuf("diag_c", [P, H_RING, P])
        keep = s.sbuf("keep", [P, CHUNKS])
        eps_sb = s.sbuf("eps", [P, 1])
        xf = s.sbuf("xf", [P, KD, CH])
        xt = s.sbuf("xt", [P, TILES, D])
        rank = s.sbuf("rank", [B_HI, CH])
        b_all = s.sbuf("b_all", [P, NS, CH])
        xpad = s.sbuf("xpad", [P, TAPS - 1 + CH])
        hist = s.sbuf("hist", [P, M, TAPS - 1])
        xs = s.sbuf("xs", [P, 2, CH])
        tanh_x = s.sbuf("tanh_x", [P, CH])
        tanh_v = s.sbuf("tanh_v", [P, 2, CH])
        delta = s.sbuf("delta", [P, 2, CH])
        gate = s.sbuf("gate", [P, M, CH])
        sp_e = s.sbuf("sp_e", [P, CH])
        sp_u = s.sbuf("sp_u", [P, CH])
        sp_l = s.sbuf("sp_l", [P, CH])
        dbx = s.sbuf("dbx", [P, DBX_RING, CH])
        h = s.sbuf("h", [P, H_RING, CH])
        carry = s.sbuf("carry", [P, STEPS])
        stats = s.sbuf("stats", [P, TILES, 6])
        mv = s.sbuf("mv", [P, TILES, 2])
        rstd = s.sbuf("rstd", [P, TILES])
        spare = s.sbuf("spare", [P, 1])

        decay = s.psum("decay", [P, A_RING, CH])
        y_ps = s.psum("y", [P, CH])
        proj = s.psum("proj", [P, CH])

        b_dram = s.dram("b", [NS, N])

        win_in = s.sem("win_in")
        consts_in = s.sem("consts_in")
        zeroed = s.sem("zeroed")
        ident_ready = s.sem("ident_ready")
        pool_consts = s.sem("pool_consts")
        neg_a = s.sem("neg_a")
        a_ready = s.sem("a_ready")
        brb_ready = s.sem("brb_ready")
        xf_in = s.sem("xf_in")
        xt_in = s.sem("xt_in")
        rb_full = s.sem("rb_full")
        x_full = s.sem("x_full")
        v_full = s.sem("v_full")
        dt_full = s.sem("dt_full")
        o_full = s.sem("o_full")
        b_ready = s.sem("b_ready")
        b_stored = s.sem("b_stored")
        b_in_all = [s.sem(f"b_in_all{n}") for n in range(NS)]
        xpad_ready = s.sem("xpad_ready")
        xpad_free = s.sem("xpad_free")
        conv_step = s.sem("conv_step")
        conv_ready = s.sem("conv_ready")
        silu_ready = s.sem("silu_ready")
        gate_ready = s.sem("gate_ready")
        halved = s.sem("halved")
        x_silu_ready = s.sem("x_silu_ready")
        v_silu_ready = s.sem("v_silu_ready")
        soft_abs = s.sem("soft_abs")
        soft_exp = s.sem("soft_exp")
        soft_add = s.sem("soft_add")
        soft_ready = s.sem("soft_ready")
        soft_step = s.sem("soft_step")
        delta_ready = s.sem("delta_ready")
        dx_ready = s.sem("dx_ready")
        decay_ready = s.sem("decay_ready")
        dbx_ready = s.sem("dbx_ready")
        scan_done = s.sem("scan_done")
        carried = s.sem("carried")
        h_used = s.sem("h_used")
        gated = s.sem("gated")
        xt_biased = s.sem("xt_biased")
        res_ready = s.sem("res_ready")
        stat_step = s.sem("stat_step")
        var_ready = s.sem("var_ready")
        std_ready = s.sem("std_ready")
        rstd_ready = s.sem("rstd_ready")
        normed = s.sem("normed")
        stored = s.sem("stored")

        win_v = win.rearrange("(k p) c -> p k c", p=P)
        first_loads = [
            (win_sb[:, :, 0:2 * DI], win_v[:, :, 0:2 * DI]),
            (win_sb[:, :, RB:RB + RANK], win_v[:, :, 2 * DI + NS:COLS]),
            (win_sb[:, :, RB + B_LO:RB + B_HI], win_v[:, :, 2 * DI:2 * DI + NS]),
        ]
        loads = [
            (wout_sb[:], wout.rearrange("(m p) c -> p m c", p=P)),
            (wdt_sb[0:RANK, :], wdt),
            (wdt_sb[RANK:RANK + 1, :], b_dt.rearrange("(a d) -> a d", a=1)),
            (conv_sb[:], wconv.rearrange("(m p) a k -> p m (a k)", p=P)),
            (bv_sb[:], b_in[0:DI].rearrange("(m p) -> p m", p=P)),
            (bx_sb[:], b_in[DI:2 * DI].rearrange("(m p) -> p m", p=P)),
            (brb_sb[0:RANK, :], b_in[2 * DI + NS:COLS].rearrange("(p a) -> p a", a=1)),
            (brb_sb[B_LO:B_HI, :], b_in[2 * DI:2 * DI + NS].rearrange("(p a) -> p a", a=1)),
            (bparam_sb[B_LO:B_HI, :], b_param.rearrange("(p a) -> p a", a=1)),
            (a_sb[:], a_log.rearrange("(m p) n -> p m n", p=P)),
            (c_sb[:], c_param.rearrange("(m p) n -> p m n", p=P)),
            (bout_sb[:], b_out.rearrange("(a d) -> a d", a=1).partition_broadcast(P)),
        ]
        ALL_IN = 16 * len(loads)
        POOL_FILLS = 5 + CHUNKS

        SIDE = [
            dict(conv=0, pe_v={12: 0}, act_v={15: 0}, act_silu=5, pe_dt=0, act_soft=1, dve_soft=5, pe_o0=7, dve_o0=10,
                 pe_o1=10, dve_o1=13, act_root=15, dve_n0=15, dve_n1=15, act_store=15),
            dict(pe_x=0, act_x=2, conv=2, pe_v={2: 1}, act_v={6: 1}, act_silu=6, pe_dt=5, act_soft=10, dve_soft=11,
                 pe_x2=13, act_x2=15),
            dict(conv=0, pe_v={0: 2, 3: 3}, act_v={4: 2, 6: 3}, act_silu=7, pe_dt=5, act_soft=9, dve_soft=11),
            dict(pe_rb=0, act_rb=2, pe_x=1, act_x=5, conv=4, pe_v={}, act_v={}, act_silu=8, pe_dt=6,
                 act_soft=8, dve_soft=10, pe_x2=12, act_x2=15),
        ]
        HEAD = dict(pe_x=0, act_x=2, conv=2, pe_v={2: 0}, act_v={6: 0}, act_silu=6, pe_dt=5, act_soft=9, dve_soft=10)

        def run_units(engine, unit, head):
            head()
            unit(0, 0, False, True)
            with engine.Fori(0, CHUNKS - 1) as c:
                for m in range(1, M):
                    unit(c, m, False, True)
                unit(c + 1, 0, True, True)
            for m in range(1, M):
                unit(CHUNKS - 1, m, False, m < M - 1)

        def side(m, tail):
            if m == 0 and not tail:
                return HEAD
            return SIDE[m]

        block = stack.enter_context(nc.Block())

        @block.sync
        def _(sp):
            def load_xf(c):
                sp.dma_start(xf[:], x_feat.rearrange("(k p) t -> p k t", p=P)[:, :, bass.ds(c * CH, CH)]).then_inc(xf_in, 16)

            def load_xt(c):
                sp.dma_start(xt[:], x_tok.rearrange("(i p) d -> p i d", p=P)[:, bass.ds(c * TILES, TILES), :]).then_inc(xt_in, 16)

            def spread_b(c, first):
                sp.wait_ge(b_ready, 2 * c + 2)
                sp.dma_start(b_dram[:, bass.ds(c * CH, CH)], rank[B_LO:B_HI, :]).then_inc(b_stored, 16)
                sp.wait_ge(b_stored, 16 * c + 16)
                for n in range(NS):
                    if not first:
                        sp.wait_ge(dbx_ready, c * STEPS + (n + 1 - NS))
                    sp.dma_start(b_all[:, n, :], b_dram[n, bass.ds(c * CH, CH)].partition_broadcast(P)).then_inc(b_in_all[n], 16)

            load_xf(0)
            for dst, src in first_loads:
                sp.dma_start(dst, src, allow_slow_non_contiguous=True).then_inc(win_in, 16)
            for dst, src in loads:
                sp.dma_start(dst, src, allow_slow_non_contiguous=True).then_inc(consts_in, 16)
            load_xt(0)
            spread_b(0, True)
            with sp.Fori(1, CHUNKS) as c:
                sp.wait_ge(v_full, M * c)
                load_xf(c)
                spread_b(c, False)
                sp.wait_ge(stored, 16 * c + 16)
                load_xt(c)

        @block.gpsimd
        def _(pool):
            fills = [(eps_sb[:], EPS), (hist[:], 0.0), (rank[RANK:RANK + 1, :], 1.0), (carry[:], 0.0),
                     (win_sb[:, :, RB + RANK:RB + B_LO], 0.0)]
            fills += [(keep[:, c:c + 1], 0.0 if (c + 1) * CH % T == 0 else 1.0) for c in range(CHUNKS)]
            for k, (dst, value) in enumerate(fills):
                nc.gpsimd.memset(dst, value).then_inc(pool_consts, 1)
                pool.wait_ge(pool_consts, k + 1)
            make_identity(nc, s, ident, pool, zeroed, ident_ready)
            pool.wait_ge(consts_in, ALL_IN)

            def unit(c, m, tail, more):
                base = held(pool, c * STEPS)
                if m == 0:
                    dmas = held(pool, (c + 1) * 16)
                pool.wait_ge(dx_ready, held(pool, c * M + (m + 1)))
                for n in range(NS):
                    i = m * NS + n
                    if m == 0:
                        pool.wait_ge(b_in_all[n], dmas)
                    pool.wait_ge(scan_done, base + (i + 1))
                    nc.gpsimd.tensor_tensor(dbx[:, i % DBX_RING, :], xs[:, m % 2, :], b_all[:, n, :], ALU.mult).then_inc(dbx_ready, 1)

            run_units(pool, unit, lambda: None)

        @block.scalar
        def _(act):
            act.wait_ge(consts_in, ALL_IN)
            nc.scalar.activation(a_sb[:], a_sb[:], ACT.Exp).then_inc(neg_a, 1)
            act.wait_ge(pool_consts, POOL_FILLS)
            act.wait_ge(brb_ready, 1)
            act.wait_ge(halved, 2)
            act.wait_ge(a_ready, 1)

            def take_rank_b(c):
                act.wait_ge(rb_full, held(act, c + 1))
                nc.scalar.activation(rank[0:RANK, :], proj[0:RANK, :], ACT.Identity, bias=brb_sb[0:RANK, :]).then_inc(b_ready, 1)
                nc.scalar.activation(rank[B_LO:B_HI, :], proj[B_LO:B_HI, :], ACT.Identity, bias=brb_sb[B_LO:B_HI, :]).then_inc(b_ready, 1)

            def take_x(k, m):
                act.wait_ge(x_full, k + 1)
                act.wait_ge(xpad_free, k + 1)
                nc.scalar.activation(xpad[:, TAPS - 1:], proj[:], ACT.Identity, bias=bx_sb[:, m:m + 1]).then_inc(xpad_ready, 1)

            def tanh_of_x(k, m):
                act.wait_ge(conv_ready, k + 1)
                act.wait_ge(x_silu_ready, k + 1)
                nc.scalar.activation(tanh_x[:], xs[:, m % 2, :], ACT.Tanh).then_inc(silu_ready, 1)

            def take_v(k, m):
                act.wait_ge(v_full, k + 1)
                act.wait_ge(v_silu_ready, k + 1)
                nc.scalar.activation(gate[:, m, :], proj[:], ACT.Identity, scale=0.5, bias=bv_sb[:, m:m + 1])
                nc.scalar.activation(tanh_v[:, m % 2, :], proj[:], ACT.Tanh, scale=0.5, bias=bv_sb[:, m:m + 1]).then_inc(gate_ready, 1)

            def soft(k, part):
                if part == 0:
                    act.wait_ge(dt_full, k + 1)
                    act.wait_ge(delta_ready, k + 1)
                    nc.scalar.activation(sp_e[:], proj[:], ACT.Abs).then_inc(soft_abs, 1)
                    act.wait_ge(soft_abs, k + 1)
                    nc.scalar.activation(sp_e[:], sp_e[:], ACT.Exp, scale=-1.0).then_inc(soft_exp, 1)
                elif part == 1:
                    act.wait_ge(soft_exp, k + 1)
                    nc.scalar.activation(sp_u[:], sp_e[:], ACT.Identity, bias=1.0).then_inc(soft_add, 1)
                else:
                    act.wait_ge(soft_add, k + 1)
                    nc.scalar.activation(sp_l[:], sp_u[:], ACT.Ln).then_inc(soft_ready, 1)

            def root(c):
                act.wait_ge(var_ready, c + 1)
                nc.scalar.activation(rstd[:], mv[:, :, 1], ACT.Sqrt, bias=eps_sb[:]).then_inc(std_ready, 1)

            def store(c):
                act.wait_ge(normed, held(act, c + 1))
                act.dma_start(x1.rearrange("(i p) d -> p i d", p=P)[:, bass.ds(c * TILES, TILES), :], xt[:]).then_inc(stored, 16)

            def head():
                take_x(0, 0)
                take_rank_b(0)
                tanh_of_x(0, 0)
                for part in range(3):
                    soft(0, part)

            def unit(c, m, tail, more):
                base = held(act, c * STEPS)
                k = held(act, c * M + m)
                at = side(m, tail)
                nxt = (m + 1) % M
                act.wait_ge(delta_ready, k + 2)
                for n in range(NS):
                    i = m * NS + n
                    act.wait_ge(scan_done, base + (i + 1 + DBX_RING - A_RING))
                    nc.scalar.activation(decay[:, i % A_RING, :], delta[:, m % 2, :], ACT.Exp, scale=a_sb[:, m, n:n + 1]).then_inc(decay_ready, 1)
                    if tail and n == at["act_root"]:
                        root(held(act, c - 1))
                    if tail and n == at["act_store"]:
                        store(c - 1)
                    if n == at.get("act_rb") and more:
                        take_rank_b(c + 1)
                    if n == at.get("act_x") and more:
                        take_x(k + 1, nxt)
                    if n == at.get("act_x2") and more:
                        take_x(k + 2, (m + 2) % M)
                    if n in at["act_v"]:
                        take_v(k - m + at["act_v"][n], at["act_v"][n])
                    if n == at["act_silu"] and more:
                        tanh_of_x(k + 1, nxt)
                    if 0 <= n - at["act_soft"] < 3 and more:
                        soft(k + 1, n - at["act_soft"])

            run_units(act, unit, head)
            root(CHUNKS - 1)
            store(CHUNKS - 1)
            act.wait_ge(stored, 16 * CHUNKS + 16)

        @block.vector
        def _(dve):
            dve.wait_ge(consts_in, ALL_IN)
            dve.wait_ge(pool_consts, POOL_FILLS)
            dve.sem_inc(xpad_free, 1)
            dve.sem_inc(delta_ready, 1)
            dve.sem_inc(scan_done, DBX_RING)
            dve.sem_inc(h_used, H_RING)
            dve.sem_inc(gated, 1)
            dve.sem_inc(carried, STEPS)
            dve.sem_inc(stored, 16)
            nc.vector.tensor_tensor(brb_sb[B_LO:B_HI, :], brb_sb[B_LO:B_HI, :], bparam_sb[B_LO:B_HI, :], ALU.add).then_inc(brb_ready, 1)
            dve.sem_inc(x_silu_ready, 1)
            dve.sem_inc(v_silu_ready, 2)
            nc.vector.tensor_scalar(conv_sb[:], conv_sb[:], 0.5, None, ALU.mult).then_inc(halved, 1)
            nc.vector.tensor_scalar(bv_sb[:], bv_sb[:], 0.5, None, ALU.mult).then_inc(halved, 1)
            dve.wait_ge(halved, 2)
            dve.wait_ge(ident_ready, 1)
            dve.wait_ge(neg_a, 1)
            nc.vector.tensor_scalar(a_sb[:], a_sb[:], -1.0, None, ALU.mult).then_inc(a_ready, 1)
            def conv(c, k, m, t):
                steps = held(dve, k * TAPS)
                if t == 0:
                    dve.wait_ge(xpad_free, k + 1)
                    nc.vector.tensor_copy(xpad[:, 0:TAPS - 1], hist[:, m, :]).then_inc(conv_step, 1)
                    dve.wait_ge(conv_step, steps + 1)
                    dve.wait_ge(xpad_ready, k + 1)
                    nc.vector.tensor_scalar(xs[:, m % 2, :], xpad[:, 0:CH], conv_sb[:, m, 0:1], None, ALU.mult).then_inc(conv_step, 1)
                    return
                dve.wait_ge(conv_step, steps + (1 + t))
                ins = nc.vector.scalar_tensor_tensor(out=xs[:, m % 2, :], in0=xpad[:, t:t + CH], scalar=conv_sb[:, m, t:t + 1],
                                                     in1=xs[:, m % 2, :], op0=ALU.mult, op1=ALU.add)
                ins.then_inc(conv_ready if t == TAPS - 1 else conv_step, 1)
                if t == TAPS - 1:
                    nc.vector.tensor_scalar(hist[:, m, :], xpad[:, CH:CH + TAPS - 1], keep[:, bass.ds(c, 1)], None, ALU.mult).then_inc(xpad_free, 1)

            def soft(k, m, part):
                if part == 0:
                    dve.wait_ge(silu_ready, k + 1)
                    nc.vector.scalar_tensor_tensor(out=xs[:, m % 2, :], in0=tanh_x[:], scalar=1.0, in1=xs[:, m % 2, :],
                                                   op0=ALU.add, op1=ALU.mult).then_inc(x_silu_ready, 1)
                    dve.wait_ge(soft_add, k + 1)
                    dve.wait_ge(soft_ready, k + 1)
                    nc.vector.scalar_tensor_tensor(out=sp_u[:], in0=sp_u[:], scalar=-1.0, in1=sp_e[:], op0=ALU.add, op1=ALU.subtract).then_inc(soft_step, 1)
                elif part == 1:
                    nc.vector.scalar_tensor_tensor(out=sp_l[:], in0=proj[:], scalar=0.0, in1=sp_l[:], op0=ALU.max, op1=ALU.add).then_inc(soft_step, 1)
                    dve.wait_ge(soft_step, held(dve, 2 * k + 2))
                    nc.vector.tensor_tensor(delta[:, m % 2, :], sp_l[:], sp_u[:], ALU.subtract).then_inc(delta_ready, 1)
                else:
                    dve.wait_ge(delta_ready, k + 2)
                    dve.wait_ge(x_silu_ready, k + 2)
                    nc.vector.tensor_tensor(xs[:, m % 2, :], xs[:, m % 2, :], delta[:, m % 2, :], ALU.mult).then_inc(dx_ready, 1)

            def silu_v(k, m):
                dve.wait_ge(gate_ready, k + 1)
                nc.vector.scalar_tensor_tensor(out=gate[:, m, :], in0=tanh_v[:, m % 2, :], scalar=1.0, in1=gate[:, m, :],
                                               op0=ALU.add, op1=ALU.mult).then_inc(v_silu_ready, 1)

            def gate_y(c, k, m):
                dve.wait_ge(h_used, held(dve, c * STEPS + ((m + 1) * NS + H_RING)))
                dve.wait_ge(v_silu_ready, k + 3)
                nc.vector.tensor_tensor(gate[:, m, :], y_ps[:], gate[:, m, :], ALU.mult).then_inc(gated, 1)

            def group(g):
                return xt[:, g * TG:(g + 1) * TG, :]

            def residual(c, g):
                done = held(dve, c * OUTS + (g + 1))
                dve.wait_ge(o_full, done)
                nc.vector.tensor_tensor(group(g), proj[:].rearrange("p (i d) -> p i d", d=D), group(g), ALU.add).then_inc(res_ready, 1)
                dve.wait_ge(res_ready, done)
                for j in range(g * TG, (g + 1) * TG):
                    ins = nc.vector.bn_stats(stats[:, j, :], xt[:, j, :])
                ins.then_inc(stat_step, 1)
                if g == OUTS - 1:
                    dve.wait_ge(stat_step, done)
                    nc.vector.memset(spare[:], 0.0)
                    for j in range(TILES):
                        ins = nc.vector.bn_aggr(mv[:, j, :], stats[:, j, :])
                    ins.then_inc(var_ready, 1)

            def normalise(c, g):
                if g == 0:
                    dve.wait_ge(std_ready, held(dve, c + 1))
                    nc.vector.reciprocal(rstd[:], rstd[:]).then_inc(rstd_ready, 1)
                    dve.wait_ge(rstd_ready, held(dve, c + 1))
                for j in range(g * TG, (g + 1) * TG):
                    ins = nc.vector.tensor_scalar(xt[:, j, :], xt[:, j, :], mv[:, j, 0:1], rstd[:, j:j + 1], ALU.subtract, ALU.mult)
                if g == OUTS - 1:
                    ins.then_inc(normed, 1)

            def bias_xt(c):
                dve.wait_ge(xt_in, held(dve, (c + 1) * 16))
                nc.vector.tensor_tensor(xt[:], xt[:], bout_sb[:].unsqueeze(1).broadcast_to([P, TILES, D]), ALU.add).then_inc(xt_biased, 1)

            def head():
                for t in range(TAPS):
                    conv(0, 0, 0, t)
                for part in range(3):
                    soft(0, 0, part)

            def unit(c, m, tail, more):
                base = held(dve, c * STEPS)
                k = held(dve, c * M + m)
                at = side(m, tail)
                nxt = (m + 1) % M

                def save(i):
                    dve.wait_ge(scan_done, base + (i + 1 + DBX_RING))
                    nc.vector.tensor_scalar(carry[:, i:i + 1], h[:, i % H_RING, CH - 1:CH], keep[:, bass.ds(c, 1)], None, ALU.mult).then_inc(carried, 1)

                dve.wait_ge(carried, base + (m + 1) * NS)
                for n in range(NS):
                    i = m * NS + n
                    dve.wait_ge(h_used, base + (i + 1))
                    nc.vector.tensor_scalar(diag_c[:, i % H_RING, :], ident[:], c_sb[:, m, n:n + 1], None, ALU.mult)
                    dve.wait_ge(decay_ready, base + (i + 1))
                    dve.wait_ge(dbx_ready, base + (i + 1))
                    nc.vector.tensor_tensor_scan(h[:, i % H_RING, :], decay[:, i % A_RING, :], dbx[:, i % DBX_RING, :],
                                                 carry[:, i:i + 1], ALU.mult, ALU.add).then_inc(scan_done, 1)
                    if n:
                        save(i - 1)
                    if n == 0 and (m or tail):
                        silu_v(k - 1, (m - 1) % M)
                    if n == 1 and (m or tail):
                        gate_y(c if m else c - 1, k - 1, (m - 1) % M)
                    if m == 1 and n == 13:
                        bias_xt(c)
                    if tail:
                        for g in range(OUTS):
                            if n == at[f"dve_o{g}"]:
                                residual(c - 1, g)
                            if n == at[f"dve_n{g}"]:
                                normalise(c - 1, g)
                    if 0 <= n - at["conv"] < TAPS and more:
                        conv(c if m < M - 1 else c + 1, k + 1, nxt, n - at["conv"])
                    if 0 <= n - at["dve_soft"] < 3 and more:
                        soft(k + 1, nxt, n - at["dve_soft"])
                save(m * NS + NS - 1)

            run_units(dve, unit, head)
            c = CHUNKS - 1
            silu_v(c * M + M - 1, M - 1)
            gate_y(c, c * M + M - 1, M - 1)
            for g in range(OUTS):
                residual(c, g)
            for g in range(OUTS):
                normalise(c, g)

        @block.tensor
        def _(pe):
            pe.wait_ge(win_in, 16 * len(first_loads))
            pe.wait_ge(pool_consts, POOL_FILLS)

            def project(rows, lhs, rhs):
                for half in range(HALVES):
                    cols = slice(half * BANK, (half + 1) * BANK)
                    for j in range(len(lhs)):
                        ins = nc.tensor.matmul(proj[0:rows, cols], lhs[j], rhs[j][:, cols], start=(j == 0), stop=(j == len(lhs) - 1))
                return ins

            xf_k = [xf[:, k, :] for k in range(KD)]

            def project_rb(c):
                pe.wait_ge(xf_in, held(pe, (c + 1) * 16))
                project(B_HI, [win_sb[:, k, RB:RB + B_HI] for k in range(KD)], xf_k).then_inc(rb_full, 1)

            def project_x(m):
                project(P, [win_sb[:, k, DI + m * P:DI + (m + 1) * P] for k in range(KD)], xf_k).then_inc(x_full, 1)

            def project_v(m):
                project(P, [win_sb[:, k, m * P:(m + 1) * P] for k in range(KD)], xf_k).then_inc(v_full, 1)

            def project_dt(m):
                project(P, [wdt_sb[:, m * P:(m + 1) * P]], [rank[0:RANK + 1, :]]).then_inc(dt_full, 1)

            def project_out(g):
                for j in range(TG):
                    t = (g * TG + j) * P
                    for m in range(M):
                        ins = nc.tensor.matmul(proj[:, j * D:(j + 1) * D], gate[:, m, t:t + P], wout_sb[:, m, :],
                                               start=(m == 0), stop=(m == M - 1))
                ins.then_inc(o_full, 1)

            def head():
                pe.wait_ge(xf_in, 16)
                project_x(0)
                pe.wait_ge(xpad_ready, 1)
                project_rb(0)
                pe.wait_ge(b_ready, 2)
                pe.wait_ge(consts_in, ALL_IN)
                project_dt(0)

            def out_group(c, k, g):
                if g == 0:
                    pe.wait_ge(gated, k + 1)
                    pe.wait_ge(delta_ready, k + 3)
                else:
                    pe.wait_ge(res_ready, held(pe, c * OUTS + g))
                project_out(g)

            def unit(c, m, tail, more):
                base = held(pe, c * STEPS)
                k = held(pe, c * M + m)
                at = side(m, tail)
                nxt = (m + 1) % M
                for n in range(NS):
                    i = m * NS + n
                    if tail:
                        for g in range(OUTS):
                            if n == at[f"pe_o{g}"]:
                                out_group(c - 1, k, g)
                    if n == at.get("pe_rb") and more:
                        pe.wait_ge(delta_ready, k + 2)
                        pe.wait_ge(gate_ready, k + 1)
                        project_rb(c + 1)
                    if n == at.get("pe_x2") and more:
                        pe.wait_ge(delta_ready, k + 3)
                        project_x((m + 2) % M)
                    if n == at.get("pe_x") and more:
                        if m == M - 1:
                            pe.wait_ge(b_ready, held(pe, 2 * c + 4))
                        elif m == 1:
                            pe.wait_ge(gate_ready, k)
                        else:
                            pe.wait_ge(delta_ready, k + 2)
                        project_x(nxt)
                    if n in at["pe_v"]:
                        v = at["pe_v"][n]
                        if tail:
                            pe.wait_ge(res_ready, held(pe, c * OUTS))
                        elif v > m:
                            pe.wait_ge(gate_ready, k + 1)
                        else:
                            pe.wait_ge(xpad_ready, k + 2)
                        project_v(v)
                    if n == at["pe_dt"] and more:
                        if 0 < m < M - 1 or m == 0 and not tail:
                            pe.wait_ge(gate_ready, k + (1 + max(at["pe_v"].values()) - m))
                        else:
                            pe.wait_ge(xpad_ready, k + 2)
                        project_dt(nxt)
                    if n == 0:
                        pe.wait_ge(gated, k + 1)
                    pe.wait_ge(scan_done, base + (i + 1 + DBX_RING))
                    for half in range(HALVES):
                        cols = slice(half * BANK, (half + 1) * BANK)
                        ins = nc.tensor.matmul(y_ps[:, cols], diag_c[:, i % H_RING, :], h[:, i % H_RING, cols], start=(n == 0), stop=(n == NS - 1))
                    ins.then_inc(h_used, 1)

            run_units(pe, unit, head)
            c = CHUNKS - 1
            pe.wait_ge(gated, c * M + M + 1)
            pe.wait_ge(gate_ready, c * M + M)
            for g in range(OUTS):
                if g:
                    pe.wait_ge(res_ready, c * OUTS + g)
                project_out(g)


def route(nc, prefix, x1, router, router_b, ids, slots, weight, capacity, tile_expert=None):
    E, NT = EXPERTS, TOKEN_TILES
    G = 4
    GROUPS = NT // G
    HT = E * capacity // P if capacity else SLOT_TILES
    BUFS = 4
    assert ids.shape[1] == HT
    with ExitStack() as stack:
        s = Scope(nc, stack, prefix)
        router_sb = s.sbuf("router", [P, KD, E])
        bias_sb = s.sbuf("bias", [P, E])
        ident = s.sbuf("ident", [P, P])
        xt = s.sbuf("xt", [P, BUFS, G, D])
        xT = s.sbuf("xT", [P, 2, G, D])
        logits = s.sbuf("logits", [P, NT, E])
        ex = s.sbuf("ex", [P, NT, E])
        row = s.sbuf("row", [P, 6, NT])
        big, total, p, best, pos, slot = (row[:, k, :] for k in range(6))
        hot = s.sbuf("hot", [P, NT, E])
        hot_b = s.sbuf("hot_b", [P, NT, E], BF16)
        rev = s.sbuf("rev", [P, E])
        base = s.sbuf("base", [P, E])
        overflow = s.sbuf("overflow", [P, NT])
        column_i = s.sbuf("column_i", [P, P], I32)
        column = s.sbuf("column", [P, P])
        tile_i = s.sbuf("tile_i", [P, NT], I32)
        tile_of = s.sbuf("tile_of", [P, NT])
        row_i = s.sbuf("row_i", [P, NT], I32)
        row_of = s.sbuf("row_of", [P, NT])
        hot_row = s.sbuf("hot_row", [P, NT, P], BF16)
        hot_tile = s.sbuf("hot_tile", [P, NT, HT])
        hot_token = s.sbuf("hot_token", [P, NT, 2, HT], BF16)
        ids_f = s.sbuf("ids_f", [P, HT])
        iota_i = s.sbuf("iota_i", [P, 2 * E], I32)
        ones_row = s.sbuf("ones_row", [P, NT])
        upper = s.sbuf("upper", [P, P], BF16)
        ones = s.sbuf("ones", [P, P], BF16)
        before = s.sbuf("before", [P, NT, E])
        small = s.sbuf("small", [P, 4, E])
        small_i = s.sbuf("small_i", [P, E], I32)
        tile_no = s.sbuf("tile_no", [P, SLOT_TILES, E])
        tile_no_i = s.sbuf("tile_no_i", [P, SLOT_TILES, E], I32)
        tile_f = s.sbuf("tile_f", [P, SLOT_TILES])
        low = s.sbuf("low", [P, NT], I32)
        t_ps = s.psum("t", [P, 2, G * D])
        l_ps = s.psum("l", [P, 2, BANK])
        c_ps = s.psum("c", [P, 2, NT, E])
        i_ps = s.psum("i", [P, 2, HT])

        router_in = s.sem("router_in")
        zeroed = s.sem("zeroed")
        ident_ready = s.sem("ident_ready")
        consts = s.sem("consts")
        x_in = [s.sem(f"x_in{u}") for u in range(BUFS)]
        turned = s.sem("turned")
        xT_ready = s.sem("xT_ready")
        logit_ps = s.sem("logit_ps")
        logit_ready = s.sem("logit_ready")
        step = s.sem("step")
        ex_ready = s.sem("ex_ready")
        hot_ready = s.sem("hot_ready")
        counted = s.sem("counted")
        tokens_hot = s.sem("tokens_hot")
        ids_summed = s.sem("ids_summed")
        CONSTS = 10
        ROUTER_IN = 16 if router_b is None else 32

        block = stack.enter_context(nc.Block())

        @block.sync
        def _(sp):
            sp.dma_start(router_sb[:], router.rearrange("(k p) e -> p k e", p=P)).then_inc(router_in, 16)
            if router_b is not None:
                sp.dma_start(bias_sb[:], router_b.rearrange("(a e) -> a e", a=1).partition_broadcast(P)).then_inc(router_in, 16)
            x_v = x1.rearrange("(i p) d -> p i d", p=P)
            for g in range(BUFS):
                sp.dma_start(xt[:, g, :, :], x_v[:, g * G:(g + 1) * G, :]).then_inc(x_in[g], 16)
            with sp.Fori(1, GROUPS // BUFS) as i:
                for u in range(BUFS):
                    sp.wait_ge(turned, BUFS * i + (u + 1 - BUFS))
                    sp.dma_start(xt[:, u, :, :], x_v[:, bass.ds((BUFS * i + u) * G, G), :]).then_inc(x_in[u], 16)

        @block.gpsimd
        def _(pool):
            nc.gpsimd.memset(ident[:], 0.0).then_inc(zeroed, 1)
            nc.gpsimd.memset(upper[:], 1.0).then_inc(zeroed, 1)
            pool.wait_ge(zeroed, 2)
            nc.gpsimd.affine_select(out=ident[:], in_=ident[:], compare_op=ALU.not_equal, fill=1.0, base=0,
                                    pattern=[[-1, P]], channel_multiplier=1).then_inc(ident_ready, 1)
            nc.gpsimd.affine_select(out=upper[:], in_=upper[:], compare_op=ALU.is_ge, fill=0.0, base=0,
                                    pattern=[[1, P]], channel_multiplier=-1).then_inc(consts, 1)
            nc.gpsimd.memset(ones[:], 1.0).then_inc(consts, 1)
            nc.gpsimd.memset(ones_row[:], 1.0).then_inc(consts, 1)
            nc.gpsimd.memset(overflow[:], float(P * HT)).then_inc(consts, 1)
            nc.gpsimd.iota(column_i[:], pattern=[[1, P]], base=0, channel_multiplier=0).then_inc(zeroed, 1)
            nc.gpsimd.iota(tile_i[:], pattern=[[1, NT]], base=0, channel_multiplier=0).then_inc(zeroed, 1)
            nc.gpsimd.iota(row_i[:], pattern=[[0, NT]], base=0, channel_multiplier=1).then_inc(zeroed, 1)
            nc.gpsimd.iota(iota_i[:, 0:E], pattern=[[-1, E]], base=E, channel_multiplier=0).then_inc(zeroed, 1)
            nc.gpsimd.iota(iota_i[:, E:2 * E], pattern=[[capacity or 0, E]], base=0, channel_multiplier=0).then_inc(zeroed, 1)
            nc.gpsimd.iota(tile_no_i[:], pattern=[[1, SLOT_TILES], [0, E]], base=0, channel_multiplier=0).then_inc(zeroed, 1)
            pool.wait_ge(zeroed, 8)
            nc.gpsimd.tensor_copy(column[:], column_i[:]).then_inc(consts, 1)
            nc.gpsimd.tensor_copy(tile_of[:], tile_i[:]).then_inc(consts, 1)
            nc.gpsimd.tensor_copy(row_of[:], row_i[:]).then_inc(consts, 1)
            nc.gpsimd.tensor_copy(tile_no[:], tile_no_i[:]).then_inc(consts, 1)
            nc.gpsimd.tensor_copy(rev[:], iota_i[:, 0:E]).then_inc(consts, 1)
            nc.gpsimd.tensor_copy(base[:], iota_i[:, E:2 * E]).then_inc(consts, 1)

        @block.scalar
        def _(act):
            with act.Fori(0, GROUPS // 2) as i:
                for u in range(2):
                    act.wait_ge(turned, 2 * i + (u + 1))
                    act.wait_ge(logit_ps, 2 * i + (u + 1))
                    nc.scalar.activation(xT[:, u, :, :], t_ps[:, u, :].rearrange("p (g d) -> p g d", d=D), ACT.Copy).then_inc(xT_ready, 1)
            act.wait_ge(step, 2 if router_b is None else 3)
            nc.scalar.activation(ex[:], ex[:], ACT.Exp).then_inc(ex_ready, 1)

        @block.tensor
        def _(pe):
            pe.wait_ge(router_in, ROUTER_IN)
            pe.wait_ge(ident_ready, 1)
            with pe.Fori(0, GROUPS // BUFS) as i:
                for pair in range(BUFS // 2):
                    for u in range(2):
                        w = 2 * pair + u
                        pe.wait_ge(x_in[w], 16 * i + 16)
                        pe.wait_ge(xT_ready, BUFS * i + (w + 1))
                        for j in range(G):
                            for k in range(KD):
                                ins = nc.tensor.transpose(t_ps[:, u, j * D + k * P:j * D + (k + 1) * P], xt[:, w, j, k * P:(k + 1) * P], ident[:])
                        ins.then_inc(turned, 1)
                    for u in range(2):
                        w = 2 * pair + u
                        pe.wait_ge(xT_ready, BUFS * i + (w + 3))
                        pe.wait_ge(logit_ready, BUFS * i + (w + 1))
                        for j in range(G):
                            for k in range(KD):
                                ins = nc.tensor.matmul(l_ps[:, u, j * E:(j + 1) * E], xT[:, u, j, k * P:(k + 1) * P], router_sb[:, k, :],
                                                       start=(k == 0), stop=(k == KD - 1))
                        ins.then_inc(logit_ps, 1)
            pe.wait_ge(consts, CONSTS)
            pe.wait_ge(hot_ready, 1)
            nc.tensor.matmul(c_ps[:, 0, :, :], upper[:], hot_b[:], start=True, stop=True)
            nc.tensor.matmul(c_ps[:, 1, :, :], ones[:], hot_b[:], start=True, stop=True).then_inc(counted, 1)
            pe.wait_ge(tokens_hot, 1)
            for t in range(NT):
                ins = nc.tensor.matmul(i_ps[:], hot_row[:, t, :], hot_token[:, t, :, :], start=(t == 0), stop=(t == NT - 1))
            ins.then_inc(ids_summed, 1)

        @block.vector
        def _(dve):
            dve.sem_inc(xT_ready, 2)
            dve.sem_inc(logit_ready, 2)
            dve.sem_inc(logit_ps, 2)
            with dve.Fori(0, GROUPS // 2) as i:
                for u in range(2):
                    dve.wait_ge(logit_ps, 2 * i + (u + 3))
                    nc.vector.tensor_copy(logits[:, bass.ds((2 * i + u) * G, G), :],
                                          l_ps[:, u, 0:G * E].rearrange("p (g e) -> p g e", e=E)).then_inc(logit_ready, 1)
            dve.wait_ge(logit_ready, GROUPS + 2)
            dve.wait_ge(consts, CONSTS)
            done = [0]

            def after(ins):
                ins.then_inc(step, 1)
                done[0] += 1
                dve.wait_ge(step, done[0])

            def per_expert(x):
                return x.unsqueeze(1).broadcast_to([P, NT, E])

            def per_token(x):
                return x.unsqueeze(2).broadcast_to([P, NT, E])

            v = nc.vector
            if router_b is not None:
                dve.wait_ge(router_in, ROUTER_IN)
                after(v.tensor_tensor(logits[:], logits[:], per_expert(bias_sb[:]), ALU.add))
            after(v.tensor_reduce(big, logits[:], AX.X, ALU.max))
            after(v.tensor_tensor(ex[:], logits[:], per_token(big), ALU.subtract))
            dve.wait_ge(ex_ready, 1)
            after(v.tensor_reduce(total, ex[:], AX.X, ALU.add))
            after(v.reciprocal(p, total))
            scores = ex if capacity else logits
            after(v.tensor_reduce(big, scores[:], AX.X, ALU.max))
            after(v.tensor_tensor(hot[:], scores[:], per_token(big), ALU.is_ge))
            after(v.tensor_tensor(hot[:], hot[:], per_expert(rev[:]), ALU.mult))
            after(v.tensor_reduce(best, hot[:], AX.X, ALU.max))
            after(v.tensor_tensor(hot[:], per_expert(rev[:]), per_token(best), ALU.is_equal))
            v.tensor_copy(hot_b[:], hot[:]).then_inc(hot_ready, 1)
            dve.wait_ge(counted, 1)
            after(v.tensor_copy(ex[:], c_ps[:, 1, :, :]))
            for e in range(E):
                ins = v.tensor_tensor_scan(before[:, :, e], ones_row[:], ex[:, :, e], 0.0, ALU.mult, ALU.add)
            after(ins)
            if not capacity:
                counts, tiles, ends, starts = (small[:, k, :] for k in range(4))
                after(v.tensor_scalar(counts, before[:, NT - 1, :], P / 2 - 0.5, 1.0 / P, ALU.add, ALU.mult))
                after(v.tensor_copy(small_i[:], counts))
                after(v.tensor_copy(tiles, small_i[:]))
                after(v.tensor_tensor_scan(ends, ones_row[:, 0:E], tiles, 0.0, ALU.mult, ALU.add))
                after(v.tensor_tensor(starts, ends, tiles, ALU.subtract))
                after(v.tensor_scalar(base[:], starts, float(P), None, ALU.mult))
                after(v.tensor_tensor(tile_no[:], tile_no[:], ends.unsqueeze(1).broadcast_to([P, SLOT_TILES, E]), ALU.is_ge))
                after(v.tensor_reduce(tile_f[:], tile_no[:], AX.X, ALU.add))
                after(v.tensor_scalar(tile_f[:], tile_f[:], float(E - 1), None, ALU.min))
                after(v.tensor_copy(tile_expert[:], tile_f[0:1, :]))
            after(v.tensor_tensor(before[:], before[:], ex[:], ALU.subtract))
            after(v.tensor_tensor(before[:], before[:], c_ps[:, 0, :, :], ALU.add))
            after(v.tensor_tensor(ex[:], before[:], hot[:], ALU.mult))
            after(v.tensor_reduce(pos, ex[:], AX.X, ALU.add))
            after(v.tensor_tensor(ex[:], per_expert(base[:]), hot[:], ALU.mult))
            after(v.tensor_reduce(slot, ex[:], AX.X, ALU.add))
            after(v.scalar_tensor_tensor(out=slot, in0=slot, scalar=-1.0, in1=pos, op0=ALU.add, op1=ALU.add))
            if capacity:
                after(v.tensor_scalar(pos, pos, float(capacity), None, ALU.is_le))
                after(v.tensor_tensor(weight[:], p, pos, ALU.mult))
                after(v.tensor_tensor(slot, slot, overflow[:], ALU.subtract))
                after(v.tensor_tensor(slot, slot, pos, ALU.mult))
                after(v.tensor_tensor(slot, slot, overflow[:], ALU.add))
            else:
                after(v.tensor_copy(weight[:], p))
            after(v.tensor_copy(slots[:], slot))
            after(v.tensor_scalar(low[:], slots[:], P - 1, None, ALU.bitwise_and))
            after(v.tensor_scalar(slots[:], slots[:], P.bit_length() - 1, None, ALU.logical_shift_right))
            after(v.tensor_copy(pos, low[:]))
            after(v.tensor_copy(slot, slots[:]))
            after(v.tensor_tensor(hot_tile[:], column[:, 0:HT].unsqueeze(1).broadcast_to([P, NT, HT]),
                                  slot.unsqueeze(2).broadcast_to([P, NT, HT]), ALU.is_equal))
            for k, part in enumerate((row_of, tile_of)):
                after(v.tensor_tensor(hot_token[:, :, k, :], hot_tile[:], part[:].unsqueeze(2).broadcast_to([P, NT, HT]), ALU.mult))
            v.tensor_tensor(hot_row[:], column[:].unsqueeze(1).broadcast_to([P, NT, P]),
                            pos.unsqueeze(2).broadcast_to([P, NT, P]), ALU.is_equal).then_inc(tokens_hot, 1)
            after(v.scalar_tensor_tensor(out=slot, in0=pos, scalar=float(HT), in1=slot, op0=ALU.mult, op1=ALU.add))
            after(v.tensor_copy(slots[:], slot))
            dve.wait_ge(ids_summed, 1)
            after(v.tensor_scalar(ids_f[:], i_ps[:, 1, :], float(P), None, ALU.mult))
            after(v.tensor_tensor(ids_f[:], ids_f[:], i_ps[:, 0, :], ALU.add))
            after(v.tensor_copy(ids[:], ids_f[:]))


class RetentionTables:
    PI = 3.141592653589793
    MAGIC = 12582912.0
    STEPS = 7
    PIECES = 4

    def __init__(self, freqs, gamma, cos_t, decay_t, undo_t):
        self.freqs, self.gamma, self.cos_t, self.decay_t, self.undo_t = freqs, gamma, cos_t, decay_t, undo_t
        self.HEAD = freqs.shape[1]
        self.M = freqs.shape[0] * self.HEAD // P
        self.HB = P // self.HEAD
        self.parts, rest = [], 2 * self.PI
        for bits in (5, 14, 22):
            self.parts.append(int(rest * 2 ** bits) / 2 ** bits)
            rest -= self.parts[-1]
        self.parts.append(rest)

    def allocate(self, s):
        self.time_i = s.sbuf("time_i", [P, T], I32)
        self.time = s.sbuf("time", [P, T])
        self.freq_sb = s.sbuf("freq", [P, self.M])
        self.gam = s.sbuf("gam", [P, self.M])
        self.gam_now = s.sbuf("gam_now", [P, 1])
        self.half_pi = s.sbuf("half_pi", [P, 1])
        self.angle = s.sbuf("angle", [P, T])
        self.turns = s.sbuf("turns", [P, T])
        self.decay = s.sbuf("decay", [P, T])
        self.undo = s.sbuf("undo", [P, T])
        self.consts_in = s.sem("table_in")
        self.filled = s.sem("table_filled")
        self.time_ready = s.sem("table_time_ready")
        self.gam_ready = s.sem("table_gam_ready")
        self.log_ready = s.sem("table_log_ready")
        self.now_ready = s.sem("table_now_ready")
        self.step = s.sem("table_step")
        self.reduced = s.sem("table_reduced")
        self.folded = s.sem("table_folded")
        self.cos_ready = s.sem("table_cos_ready")
        self.decay_ready = s.sem("table_decay_ready")
        self.undo_ready = s.sem("table_undo_ready")
        self.cos_stored = s.sem("table_cos_stored")
        self.decay_stored = s.sem("table_decay_stored")
        self.undo_stored = s.sem("table_undo_stored")

    def load(self, nc, sp):
        sp.dma_start(self.freq_sb[:], self.freqs.rearrange("(m h) d -> (h d) m", m=self.M), allow_slow_non_contiguous=True).then_inc(self.consts_in, 16)
        for h in range(self.HB):
            src = self.gamma.rearrange("(m h) a b -> h (m a b)", m=self.M)[h]
            sp.dma_start(self.gam[h * self.HEAD:(h + 1) * self.HEAD, :], src.partition_broadcast(self.HEAD), allow_slow_non_contiguous=True).then_inc(self.consts_in, 16)

    def store_angles(self, sp, m):
        for table, dst, ready, stored in ((self.decay, self.decay_t, self.decay_ready, self.decay_stored),
                                          (self.angle, self.cos_t, self.cos_ready, self.cos_stored)):
            sp.wait_ge(ready, m + 1)
            sp.dma_start(dst[bass.ds(m, 1), :, :].rearrange("a p t -> p (a t)"), table[:]).then_inc(stored, 16)

    def store_undo(self, sp, m):
        sp.wait_ge(self.undo_ready, m + 2)
        sp.dma_start(self.undo_t[bass.ds(m, 1), :, :].rearrange("a p t -> p (a t)"), self.undo[:]).then_inc(self.undo_stored, 16)

    def stored(self, sp):
        for stored in (self.cos_stored, self.decay_stored, self.undo_stored):
            sp.wait_ge(stored, 16 * self.M + 16)

    def fill(self, nc):
        nc.gpsimd.memset(self.half_pi[:], self.PI / 2).then_inc(self.filled, 1)
        nc.gpsimd.iota(self.time_i[:], pattern=[[1, T]], base=0, channel_multiplier=0).then_inc(self.filled, 1)

    def prepare(self, nc, dve):
        for stored in (self.cos_stored, self.decay_stored, self.undo_stored):
            dve.sem_inc(stored, 16)
        dve.sem_inc(self.undo_ready, 1)
        dve.wait_ge(self.filled, 2)
        nc.vector.tensor_copy(self.time[:], self.time_i[:]).then_inc(self.time_ready, 1)
        dve.wait_ge(self.consts_in, 16 * (1 + self.HB))
        nc.vector.tensor_scalar(self.gam[:], self.gam[:], 2.0 ** -64, None, ALU.max).then_inc(self.gam_ready, 1)
        dve.wait_ge(self.time_ready, 1)

    def take_logs(self, nc, act):
        act.wait_ge(self.gam_ready, 1)
        nc.scalar.activation(self.gam[:], self.gam[:], ACT.Ln).then_inc(self.log_ready, 1)
        act.wait_ge(self.log_ready, 1)

    def angles(self, nc, dve, m):
        v = nc.vector
        first = held(dve, m * self.STEPS)
        before = held(dve, m * 16 + 16)
        dve.wait_ge(self.cos_stored, before)
        v.tensor_scalar(self.angle[:], self.time[:], self.freq_sb[:, bass.ds(m, 1)], None, ALU.mult).then_inc(self.step, 1)
        dve.wait_ge(self.step, first + 1)
        v.tensor_scalar(self.turns[:], self.angle[:], 1.0 / (2 * self.PI), self.MAGIC, ALU.mult, ALU.add).then_inc(self.step, 1)
        dve.wait_ge(self.step, first + 2)
        v.tensor_scalar(self.turns[:], self.turns[:], self.MAGIC, -1.0, ALU.subtract, ALU.mult).then_inc(self.step, 1)
        for k, part in enumerate(self.parts):
            dve.wait_ge(self.step, first + (3 + k))
            ins = v.scalar_tensor_tensor(out=self.angle[:], in0=self.turns[:], scalar=float(part), in1=self.angle[:], op0=ALU.mult, op1=ALU.add)
            ins.then_inc(self.reduced if k == len(self.parts) - 1 else self.step, 1)

    def curves(self, nc, act, m):
        block = held(act, m + 1)
        before = held(act, m * 16 + 16)
        act.wait_ge(self.decay_stored, before)
        act.wait_ge(self.undo_ready, block)
        nc.scalar.activation(self.gam_now[:], self.gam[:, bass.ds(m, 1)], ACT.Copy).then_inc(self.now_ready, 1)
        act.wait_ge(self.now_ready, block)
        nc.scalar.activation(self.decay[:], self.time[:], ACT.Exp, scale=self.gam_now[:]).then_inc(self.decay_ready, 1)
        act.wait_ge(self.reduced, block)
        nc.scalar.activation(self.angle[:], self.angle[:], ACT.Abs).then_inc(self.folded, 1)
        act.wait_ge(self.folded, block)
        nc.scalar.activation(self.angle[:], self.angle[:], ACT.Sin, bias=self.half_pi[:], scale=-1.0).then_inc(self.cos_ready, 1)

    def reciprocals(self, nc, dve, m):
        v = nc.vector
        before = held(dve, m * 16 + 16)
        dve.wait_ge(self.decay_ready, held(dve, m + 1))
        dve.wait_ge(self.undo_stored, before)
        v.tensor_scalar(self.undo[:], self.decay[:], 1e-6, None, ALU.add).then_inc(self.step, 1)
        dve.wait_ge(self.step, held(dve, m * self.STEPS + self.STEPS))
        for k in range(self.PIECES):
            piece = self.undo[:, k * (T // self.PIECES):(k + 1) * (T // self.PIECES)]
            ins = v.reciprocal(piece, piece)
        ins.then_inc(self.undo_ready, 1)


def capacity_experts(nc, x1, ids, w1, b1, w2, b2, eo, capacity, tables):
    E, F = EXPERTS, w1.shape[2]
    FB = F // P
    J = capacity // P
    HALF = capacity // 2
    H_BANKS, O_BANKS = 4, 2
    with ExitStack() as stack:
        s = Scope(nc, stack, "ffn")
        ident = s.sbuf("ident", [P, P])
        w1_sb = s.sbuf("w1", [P, 2, KD, F])
        w2_sb = s.sbuf("w2", [P, 2, FB, D])
        b1_rows = s.sbuf("b1_rows", [E * FB, P])
        b1_sb = s.sbuf("b1", [P, E * FB])
        b2_sb = s.sbuf("b2", [P, E, D])
        ids_now = s.sbuf("ids_now", [P, 2, J], I32)
        b1_now = s.sbuf("b1_now", [P, 2, FB])
        spare = s.sbuf("spare", [P, 1])
        xg = s.sbuf("xg", [P, 2, J, D])
        xT = s.sbuf("xT", [P, 2, KD, capacity])
        hT = s.sbuf("hT", [P, 2, FB, capacity])
        out_sb = s.sbuf("out", [P, 2, J, D])
        t_ps = s.psum("t", [P, 2, BANK])
        h_ps = s.psum("h", [P, H_BANKS, BANK])
        o_ps = s.psum("o", [P, O_BANKS, BANK])

        zeroed = s.sem("zeroed")
        ident_ready = s.sem("ident_ready")
        b1_in = s.sem("b1_in")
        b2_in = s.sem("b2_in")
        b1_turned = s.sem("b1_turned")
        b1_ready = s.sem("b1_ready")
        w1_in = [s.sem(f"w1_in{u}") for u in range(2)]
        w2_in = [s.sem(f"w2_in{u}") for u in range(2)]
        ids_ready = s.sem("ids_ready")
        gathered = [s.sem(f"gathered{u}") for u in range(2)]
        turned = s.sem("turned")
        xT_ready = s.sem("xT_ready")
        h_full = s.sem("h_full")
        h_ready = s.sem("h_ready")
        o_full = s.sem("o_full")
        o_ready = s.sem("o_ready")
        stored = [s.sem(f"stored{u}") for u in range(2)]
        tables.allocate(s)
        assert tables.M == E // 2
        TG = J // 2
        HG = 2 * FB

        block = stack.enter_context(nc.Block())

        @block.sync
        def _(sp):
            sp.dma_start(b1_rows[:], b1.rearrange("e (f p) -> (e f) p", p=P)).then_inc(b1_in, 16)

            def load(e, u):
                sp.dma_start(w1_sb[:, u, :, :], w1[bass.ds(e, 1), :, :].rearrange("a (k p) f -> p (a k) f", p=P)).then_inc(w1_in[u], 16)
                sp.dma_start(w2_sb[:, u, :, :], w2[bass.ds(e, 1), :, :].rearrange("a (f p) d -> p (a f) d", p=P)).then_inc(w2_in[u], 16)

            load(0, 0)
            sp.dma_start(b2_sb[:], b2.partition_broadcast(P)).then_inc(b2_in, 16)
            tables.load(nc, sp)
            sp.wait_ge(ids_ready, 2)
            load(1, 1)

            def store(e, u):
                sp.wait_ge(o_ready, (e + 1) * J + O_BANKS)
                sp.dma_start(eo.rearrange("(p t) d -> p t d", p=P)[:, bass.ds(e * J, J), :], out_sb[:, u, :, :]).then_inc(stored[u], 16)

            with sp.Fori(0, E // 2 - 1) as i:
                for u in range(2):
                    store(2 * i + u, u)
                    (tables.store_undo if u else tables.store_angles)(sp, i)
                    sp.wait_ge(o_full, (2 * i + (u + 3)) * J)
                    load(2 * i + (u + 2), u)
            store(E - 2, 0)
            tables.store_angles(sp, E // 2 - 1)
            tables.store_undo(sp, E // 2 - 1)
            store(E - 1, 1)
            tables.stored(sp)
            for u in range(2):
                sp.wait_ge(stored[u], 8 * E + 16)

        @block.gpsimd
        def _(pool):
            make_identity(nc, s, ident, pool, zeroed, ident_ready)
            tables.fill(nc)
            pool.wait_ge(ident_ready, 1)
            with pool.Fori(0, E // 2) as i:
                for u in range(2):
                    pool.wait_ge(turned, (2 * i + (u + 1)) * TG)
                    nc.gpsimd.tensor_copy(ids_now[:, u, :], ids[:, bass.ds((2 * i + u) * J, J)]).then_inc(ids_ready, 1)
                    pool.wait_ge(ids_ready, 2 * i + (u + 1))
                    nc.gpsimd.tensor_tensor(spare[:], ident[:, 0:1], ident[:, 0:1], ALU.add)
                    for j in range(J):
                        nc.gpsimd.indirect_dma_start(xg[:, u, j, :], None, x1[:],
                                                     bass.IndirectOffsetOnAxis(ap=ids_now[:, u, j:j + 1], axis=0)).then_inc(gathered[u], 16)

        @block.scalar
        def _(act):
            act.wait_ge(b1_turned, 1)
            nc.scalar.activation(b1_sb[:], t_ps[:, 0, 0:E * FB], ACT.Copy).then_inc(b1_ready, 1)
            tables.take_logs(nc, act)
            act.wait_ge(b1_ready, 1)
            with act.Fori(0, E // 2) as i:
                for u in range(2):
                    groups = act.snap((2 * i + u) * HG)
                    act.wait_ge(o_full, (2 * i + (u + 1)) * J)
                    nc.scalar.activation(b1_now[:, u, :], b1_sb[:, bass.ds((2 * i + u) * FB, FB)], ACT.Copy).then_inc(b1_ready, 1)
                    act.wait_ge(b1_ready, 2 * i + (u + 2))
                    for f in range(FB):
                        for half in range(2):
                            k = 2 * f + half
                            act.wait_ge(h_full, groups + (k + 1))
                            nc.scalar.activation(hT[:, u, f, half * HALF:(half + 1) * HALF], h_ps[:, (u * HG + k) % H_BANKS, 0:HALF],
                                                 ACT.Gelu, bias=b1_now[:, u, f:f + 1]).then_inc(h_ready, 1)
                    if u == 0:
                        tables.curves(nc, act, i)

        @block.tensor
        def _(pe):
            pe.wait_ge(ident_ready, 1)
            pe.wait_ge(b1_in, 16)
            nc.tensor.transpose(t_ps[:, 0, 0:E * FB], b1_rows[:], ident[0:E * FB, 0:E * FB]).then_inc(b1_turned, 1)
            pe.wait_ge(b1_ready, 1)

            def turn(e, u):
                tgroups = held(pe, e * TG)
                pe.wait_ge(gathered[u], held(pe, (e - u) * (8 * J) + 16 * J))
                for g in range(TG):
                    b = (u * TG + g) % 2
                    pe.wait_ge(xT_ready, tgroups + (g + 1))
                    for jj in range(2):
                        for k in range(KD):
                            ins = nc.tensor.transpose(t_ps[:, b, (2 * jj + k) * P:(2 * jj + k + 1) * P], xg[:, u, 2 * g + jj, k * P:(k + 1) * P], ident[:])
                    ins.then_inc(turned, 1)

            def hidden(e, u):
                hgroups = held(pe, e * HG)
                pe.wait_ge(xT_ready, held(pe, e * TG + (TG + 2)))
                pe.wait_ge(w1_in[u], held(pe, (e - u) * 8 + 16))
                for f in range(FB):
                    for half in range(2):
                        n = 2 * f + half
                        pe.wait_ge(h_ready, hgroups + (n + 1))
                        for k in range(KD):
                            ins = nc.tensor.matmul(h_ps[:, (u * HG + n) % H_BANKS, 0:HALF], w1_sb[:, u, k, f * P:(f + 1) * P],
                                                   xT[:, u, k, half * HALF:(half + 1) * HALF], start=(k == 0), stop=(k == KD - 1))
                        ins.then_inc(h_full, 1)

            def outputs(e, u):
                ogroups = held(pe, e * J)
                pe.wait_ge(h_ready, held(pe, e * HG + (HG + H_BANKS)))
                pe.wait_ge(w2_in[u], held(pe, (e - u) * 8 + 16))
                for j in range(J):
                    pe.wait_ge(o_ready, ogroups + (j + 1))
                    for f in range(FB):
                        ins = nc.tensor.matmul(o_ps[:, j % O_BANKS, 0:D], hT[:, u, f, j * P:(j + 1) * P], w2_sb[:, u, f, :],
                                               start=(f == 0), stop=(f == FB - 1))
                    ins.then_inc(o_full, 1)

            def expert(e, u, more):
                hidden(e, u)
                if more:
                    turn(e + 1, 1 - u)
                outputs(e, u)

            turn(0, 0)
            with pe.Fori(0, E // 2 - 1) as i:
                for u in range(2):
                    expert(2 * i + u, u, True)
            expert(E - 2, 0, True)
            expert(E - 1, 1, False)

        @block.vector
        def _(dve):
            dve.sem_inc(xT_ready, 2)
            dve.sem_inc(h_ready, H_BANKS)
            dve.sem_inc(o_ready, O_BANKS)
            dve.sem_inc(turned, 2 * TG)
            dve.sem_inc(o_full, 2 * J)
            dve.sem_inc(stored[0], 16)
            dve.sem_inc(stored[1], 16)

            def take_turned(e, u):
                tgroups = held(dve, e * TG)
                for g in range(TG):
                    b = (u * TG + g) % 2
                    dve.wait_ge(turned, tgroups + (2 * TG + g + 1))
                    nc.vector.tensor_copy(xT[:, u, :, 2 * g * P:(2 * g + 2) * P].rearrange("p k (j t) -> p j k t", t=P),
                                          t_ps[:, b, :].rearrange("p (j k t) -> p j k t", k=KD, t=P)).then_inc(xT_ready, 1)

            def expert(i, u, more):
                e = 2 * i + u
                (tables.reciprocals if u else tables.angles)(nc, dve, i)
                if more:
                    take_turned(e + 1, 1 - u)
                ogroups = held(dve, e * J)
                dve.wait_ge(stored[u], held(dve, 16 * i + 16))
                for j in range(J):
                    dve.wait_ge(o_full, ogroups + (2 * J + j + 1))
                    nc.vector.tensor_tensor(out_sb[:, u, j, :], o_ps[:, j % O_BANKS, 0:D], b2_sb[:, bass.ds(e, 1), :].rearrange("p a d -> p (a d)"), ALU.add).then_inc(o_ready, 1)

            take_turned(0, 0)
            tables.prepare(nc, dve)
            dve.wait_ge(b2_in, 16)
            with dve.Fori(0, E // 2 - 1) as i:
                for u in range(2):
                    expert(i, u, True)
            expert(E // 2 - 1, 0, True)
            expert(E // 2 - 1, 1, False)


def combine(nc, prefix, x1, eo, slots, weight, x2, last_slot):
    NT = TOKEN_TILES
    G = 4
    GROUPS = NT // G
    BUFS = 4
    with ExitStack() as stack:
        s = Scope(nc, stack, prefix)
        xt = s.sbuf("xt", [P, BUFS, G, D])
        y = s.sbuf("y", [P, BUFS, G, D])
        inside = s.sbuf("inside", [P, NT], I32)
        inside_now = s.sbuf("inside_now", [P, BUFS, G], I32)
        spare_p = s.sbuf("spare_p", [P, 1])
        stats = s.sbuf("stats", [P, BUFS, G, 6])
        mv = s.sbuf("mv", [P, BUFS, G, 2])
        rstd = s.sbuf("rstd", [P, BUFS, G])
        spare = s.sbuf("spare", [P, 1])
        eps_sb = s.sbuf("eps", [P, 1])

        eps_ready = s.sem("eps_ready")
        inside_ready = s.sem("inside_ready")
        now_ready = s.sem("now_ready")
        gathered = [s.sem(f"gathered{u}") for u in range(BUFS)]
        x_in = [s.sem(f"x_in{u}") for u in range(BUFS)]
        summed = s.sem("summed")
        stat_step = s.sem("stat_step")
        var_ready = s.sem("var_ready")
        std_ready = s.sem("std_ready")
        rstd_ready = s.sem("rstd_ready")
        normed = s.sem("normed")
        stored = [s.sem(f"stored{u}") for u in range(BUFS)]

        block = stack.enter_context(nc.Block())

        @block.sync
        def _(sp):
            x_v = x1.rearrange("(i p) d -> p i d", p=P)
            for g in range(BUFS):
                if g:
                    sp.wait_ge(now_ready, g + 1)
                sp.dma_start(xt[:, g, :, :], x_v[:, g * G:(g + 1) * G, :]).then_inc(x_in[g], 16)
            with sp.Fori(1, GROUPS // BUFS) as i:
                for u in range(BUFS):
                    sp.wait_ge(stored[u], 16 * i)
                    sp.dma_start(xt[:, u, :, :], x_v[:, bass.ds((BUFS * i + u) * G, G), :]).then_inc(x_in[u], 16)

        @block.gpsimd
        def _(pool):
            nc.gpsimd.memset(eps_sb[:], EPS).then_inc(eps_ready, 1)
            nc.gpsimd.tensor_scalar(inside[:], slots[:], float(last_slot), None, ALU.min).then_inc(inside_ready, 1)
            pool.wait_ge(inside_ready, 1)
            pool.wait_ge(eps_ready, 1)
            with pool.Fori(0, GROUPS // BUFS) as i:
                for u in range(BUFS):
                    pool.wait_ge(summed, BUFS * i + (u + 1))
                    nc.gpsimd.tensor_copy(inside_now[:, u, :], inside[:, bass.ds((BUFS * i + u) * G, G)]).then_inc(now_ready, 1)
                    pool.wait_ge(now_ready, BUFS * i + (u + 1))
                    nc.gpsimd.tensor_tensor(spare_p[:], eps_sb[:], eps_sb[:], ALU.add)
                    for j in range(G):
                        nc.gpsimd.indirect_dma_start(y[:, u, j, :], None, eo[:],
                                                     bass.IndirectOffsetOnAxis(ap=inside_now[:, u, j:j + 1], axis=0)).then_inc(gathered[u], 16)

        @block.scalar
        def _(act):
            act.wait_ge(eps_ready, 1)
            with act.Fori(0, GROUPS // BUFS) as i:
                for u in range(BUFS):
                    g = act.snap(BUFS * i + u)
                    act.wait_ge(var_ready, g + 1)
                    nc.scalar.activation(rstd[:, u, :], mv[:, u, :, 1], ACT.Sqrt, bias=eps_sb[:]).then_inc(std_ready, 1)
                    if u % 2:
                        for w in (u - 1, u):
                            act.wait_ge(normed, BUFS * i + (w + 1))
                            act.dma_start(x2.rearrange("(i p) d -> p i d", p=P)[:, bass.ds((BUFS * i + w) * G, G), :], xt[:, w, :, :]).then_inc(stored[w], 16)
            for u in range(BUFS):
                act.wait_ge(stored[u], 16 * (GROUPS // BUFS))

        @block.vector
        def _(dve):
            dve.sem_inc(summed, BUFS)
            with dve.Fori(0, GROUPS // BUFS) as i:
                for u in range(BUFS):
                    g = dve.snap(BUFS * i + u)
                    rows = xt[:, u, :, :]
                    dve.wait_ge(x_in[u], i * 16 + 16)
                    dve.wait_ge(gathered[u], i * (16 * G) + 16 * G)
                    for j in range(G):
                        ins = nc.vector.scalar_tensor_tensor(out=rows[:, j, :], in0=y[:, u, j, :], scalar=weight[:, bass.ds(g * G + j, 1)],
                                                             in1=rows[:, j, :], op0=ALU.mult, op1=ALU.add)
                    ins.then_inc(summed, 1)
                    dve.wait_ge(summed, g + (1 + BUFS))
                    layernorm_stats(nc, dve, rows, stats[:, u, :, :], mv[:, u, :, :], spare, G, g + 1, stat_step, var_ready)
                    if u % 2:
                        for w in (u - 1, u):
                            layernorm_apply(nc, dve, xt[:, w, :, :], xt[:, w, :, :], mv[:, w, :, :], rstd[:, w, :], G,
                                            held(dve, BUFS * i + (w + 1)), std_ready, rstd_ready, normed)


def sorted_experts(nc, x3, ids, tile_expert, w, b, eo):
    E, J = EXPERTS, SLOT_TILES
    R = 4
    XR = 8
    with ExitStack() as stack:
        s = Scope(nc, stack, "top1")
        ident = s.sbuf("ident", [P, P])
        w_sb = s.sbuf("w", [P, KD, E * D])
        b_sb = s.sbuf("b", [1, E * D])
        one_row = s.sbuf("one_row", [1, P])
        ids_now = s.sbuf("ids_now", [P, XR], I32)
        spare = s.sbuf("spare", [P, 1])
        xg = s.sbuf("xg", [P, XR, D])
        xT = s.sbuf("xT", [P, R, D])
        out_sb = s.sbuf("out", [P, J, D])
        t_ps = s.psum("t", [P, R, BANK])
        o_ps = s.psum("o", [P, R, BANK])

        zeroed = s.sem("zeroed")
        ident_ready = s.sem("ident_ready")
        ones_ready = s.sem("ones_ready")
        w_in = s.sem("w_in")
        ids_ready = s.sem("ids_ready")
        gathered = [s.sem(f"gathered{u}") for u in range(XR)]
        turned = s.sem("turned")
        xT_ready = s.sem("xT_ready")
        o_full = s.sem("o_full")
        o_ready = s.sem("o_ready")
        stored = s.sem("stored")
        block = stack.enter_context(nc.Block())

        @block.sync
        def _(sp):
            sp.dma_start(w_sb[:].rearrange("p k (e d) -> p k e d", e=E)[:, 0], w.rearrange("e (k p) d -> k p e d", p=P)[0]).then_inc(w_in, 16)
            sp.dma_start(w_sb[:].rearrange("p k (e d) -> p k e d", e=E)[:, 1], w.rearrange("e (k p) d -> k p e d", p=P)[1]).then_inc(w_in, 16)
            sp.dma_start(b_sb[:], b.rearrange("(a e) d -> a (e d)", a=1)).then_inc(w_in, 16)
            with sp.Fori(0, J // R) as i:
                sp.wait_ge(o_ready, i * R + 2 * R)
                sp.dma_start(eo.rearrange("(p j) d -> p j d", p=P)[:, bass.ds(i * R, R), :], out_sb[:, bass.ds(i * R, R), :]).then_inc(stored, 16)
            sp.wait_ge(stored, 16 * (J // R))

        @block.gpsimd
        def _(pool):
            make_identity(nc, s, ident, pool, zeroed, ident_ready)
            nc.gpsimd.memset(one_row[:], 1.0).then_inc(ones_ready, 1)
            pool.wait_ge(ident_ready, 1)
            with pool.Fori(0, J // XR) as i:
                for u in range(XR):
                    pool.wait_ge(turned, XR * i + (u + 1))
                    nc.gpsimd.tensor_copy(ids_now[:, u:u + 1], ids[:, bass.ds(XR * i + u, 1)]).then_inc(ids_ready, 1)
                    pool.wait_ge(ids_ready, XR * i + (u + 1))
                    nc.gpsimd.tensor_tensor(spare[:], ident[:, 0:1], ident[:, 0:1], ALU.add)
                    nc.gpsimd.indirect_dma_start(xg[:, u, :], None, x3[:],
                                                 bass.IndirectOffsetOnAxis(ap=ids_now[:, u:u + 1], axis=0)).then_inc(gathered[u], 16)

        @block.scalar
        def _(act):
            with act.Fori(0, J // R) as i:
                for u in range(R):
                    act.wait_ge(turned, R * i + (u + 1 + XR))
                    act.wait_ge(o_full, R * i + (u + 1))
                    nc.scalar.activation(xT[:, u, :], t_ps[:, u, 0:D], ACT.Copy).then_inc(xT_ready, 1)

        @block.tensor
        def _(pe):
            pe.wait_ge(ident_ready, 1)
            pe.wait_ge(ones_ready, 1)
            pe.wait_ge(w_in, 48)
            with pe.Fori(0, J // XR) as i:
                for half in range(XR // R):
                    for u in range(R):
                        w = half * R + u
                        pe.wait_ge(gathered[w], 16 * i + 16)
                        pe.wait_ge(xT_ready, XR * i + (w + 1))
                        for k in range(KD):
                            ins = nc.tensor.transpose(t_ps[:, u, k * P:(k + 1) * P], xg[:, w, k * P:(k + 1) * P], ident[:])
                        ins.then_inc(turned, 1)
                    for u in range(R):
                        w = half * R + u
                        first = pe.value_load(tile_expert[0:1, bass.ds(XR * i + w, 1)], min_val=0, max_val=E - 1) * D
                        pe.wait_ge(xT_ready, XR * i + (w + 1 + R))
                        pe.wait_ge(o_ready, XR * i + (w + 1))
                        for k in range(KD):
                            nc.tensor.matmul(o_ps[:, u, 0:D], xT[:, u, k * P:(k + 1) * P], w_sb[:, k, bass.ds(first, D)], start=(k == 0), stop=False)
                        nc.tensor.matmul(o_ps[:, u, 0:D], one_row[:], b_sb[:, bass.ds(first, D)], start=False, stop=True).then_inc(o_full, 1)

        @block.vector
        def _(dve):
            dve.sem_inc(turned, XR)
            for sem in (xT_ready, o_full, o_ready):
                dve.sem_inc(sem, R)
            with dve.Fori(0, J // R) as i:
                for u in range(R):
                    dve.wait_ge(o_full, R * i + (u + 1 + R))
                    nc.vector.tensor_copy(out_sb[:, bass.ds(R * i + u, 1), :].rearrange("p a d -> p (a d)"), o_ps[:, u, 0:D]).then_inc(o_ready, 1)


def retention_layer(nc, x1, eo, slots, weight, last_slot, x2, conv_w, conv_b, qk_w, v_w, g_w, g_b, o_w, ln_g, ln_b, cos_t, decay_t, undo_t, x3):
    E = qk_w.shape[1]
    M = E // P
    HEAD = 32
    HEADS = E // HEAD
    HB = P // HEAD
    TAPS = 4
    CH = BANK
    Q = T // CH
    G = CH // P
    KINDS = 3
    PROJ_RING, R_RING = 2, 2
    assert B == 2
    with ExitStack() as stack:
        s = Scope(nc, stack, "ret")
        ident = s.sbuf("ident", [P, P])
        heads = s.sbuf("heads", [P, HB])
        members = s.sbuf("members", [HEADS, E])
        inv_t = s.sbuf("inv_t", [HEADS, CH])
        qk_sb = s.sbuf("qk_w", [P, KD, E])
        v_sb = s.sbuf("v_w", [P, KD, E])
        g_sb = s.sbuf("g_w", [P, KD, E])
        o_sb = s.sbuf("o_w", [P, M, D])
        gb_sb = s.sbuf("gb", [P, M])
        cw_sb = s.sbuf("cw", [P, KD, TAPS])
        cb_sb = s.sbuf("cb", [P, KD])
        lng_sb = s.sbuf("lng", [P, D])
        lnb_sb = s.sbuf("lnb", [P, D])
        eps_sb = s.sbuf("eps", [P, 1])
        ones = s.sbuf("ones", [P, CH])
        xt = s.sbuf("xt", [P, B, G, D])
        y = s.sbuf("y", [P, B, G, D])
        inside = s.sbuf("inside", [P, TOKEN_TILES], I32)
        inside_now = s.sbuf("inside_now", [P, B, G], I32)
        spare_p = s.sbuf("spare_p", [P, 1])
        mv_x = s.sbuf("mv_x", [P, G, 2])
        rstd_x = s.sbuf("rstd_x", [P, G])
        res = s.sbuf("res", [P, B, G, D])
        xpad = s.sbuf("xpad", [P, B, KD, TAPS - 1 + CH])
        xc = s.sbuf("xc", [P, B, KD, CH])
        qk = s.sbuf("qk", [P, B, M, CH])
        square = s.sbuf("square", [P, M, CH])
        val = s.sbuf("val", [P, B, M, CH])
        gate = s.sbuf("gate", [P, B, M, CH])
        norm = s.sbuf("norm", [P, G * HEADS])
        q = s.sbuf("q", [P, B, M, CH + 1])
        mem = s.sbuf("mem", [P, B, M, CH])
        mem_last = s.sbuf("mem_last", [P, B, M])
        o_in = s.sbuf("o_in", [P, B, M, CH])
        cos_sb = s.sbuf("cos", [P, M, CH])
        decay_sb = s.sbuf("decay", [P, M, CH])
        undo_sb = s.sbuf("undo", [P, M, CH])
        z = s.sbuf("z", [P, G, D])
        stats = s.sbuf("stats", [P, G, 6])
        mv = s.sbuf("mv", [P, 2, G, 2])
        rstd = s.sbuf("rstd", [P, 2, G])
        spare = s.sbuf("spare", [P, 1])

        t_ps = s.psum("t", [P, CH])
        proj = s.psum("proj", [P, PROJ_RING, CH])
        n_ps = s.psum("n_ps", [P, G * HEADS])
        r_ps = s.psum("r_ps", [P, R_RING, CH])
        o_ps = s.psum("o_ps", [P, G, D])

        consts_in = s.sem("consts_in")
        filled = s.sem("filled")
        x_in = [s.sem(f"x_in{b}") for b in range(B)]
        gathered = [s.sem(f"gathered{b}") for b in range(B)]
        inside_ready = s.sem("inside_ready")
        now_ready = s.sem("now_ready")
        joined = s.sem("joined")
        x_stat_step = s.sem("x_stat_step")
        x_var_ready = s.sem("x_var_ready")
        x_std_ready = s.sem("x_std_ready")
        x_rstd_ready = s.sem("x_rstd_ready")
        x_made = s.sem("x_made")
        x2_stored = [s.sem(f"x2_stored{b}") for b in range(B)]
        res_in = [s.sem(f"res_in{b}") for b in range(B)]
        tab_in = s.sem("tab_in")
        turned = s.sem("turned")
        xpad_ready = s.sem("xpad_ready")
        xpad_free = s.sem("xpad_free")
        conv_step = s.sem("conv_step")
        xc_ready = s.sem("xc_ready")
        proj_full = s.sem("proj_full")
        proj_taken = s.sem("proj_taken")
        n_full = s.sem("n_full")
        norm_ready = s.sem("norm_ready")
        inv_step = s.sem("inv_step")
        inv_turned = s.sem("inv_turned")
        inv_ready = s.sem("inv_ready")
        r_full = s.sem("r_full")
        q_ready = s.sem("q_ready")
        q_kept = s.sem("q_kept")
        phase_ready = s.sem("phase_ready")
        gated = s.sem("gated")
        undo_ready = s.sem("undo_ready")
        mem_step = s.sem("mem_step")
        o_in_ready = s.sem("o_in_ready")
        o_full = s.sem("o_full")
        o_taken = s.sem("o_taken")
        z_step = s.sem("z_step")
        stat_step = s.sem("stat_step")
        var_ready = s.sem("var_ready")
        std_ready = s.sem("std_ready")
        rstd_ready = s.sem("rstd_ready")
        normed = s.sem("normed")
        res_biased = s.sem("res_biased")
        stored = [s.sem(f"stored{b}") for b in range(B)]

        loads = [
            (qk_sb[:], qk_w.rearrange("(k p) e -> p k e", p=P)),
            (v_sb[:], v_w.rearrange("(k p) e -> p k e", p=P)),
            (g_sb[:], g_w.rearrange("(k p) e -> p k e", p=P)),
            (o_sb[:], o_w.rearrange("(m p) d -> p m d", p=P)),
            (gb_sb[:], g_b.rearrange("(m p) -> p m", p=P)),
            (cw_sb[:], conv_w.rearrange("(k p) a t -> p k (a t)", p=P)),
            (cb_sb[:], conv_b.rearrange("(k p) -> p k", p=P)),
            (lng_sb[:], ln_g.rearrange("(a d) -> a d", a=1).partition_broadcast(P)),
            (lnb_sb[:], ln_b.rearrange("(a d) -> a d", a=1).partition_broadcast(P)),
        ]
        ALL_IN = 16 * len(loads)
        fills = [(ident[:], 0.0), (heads[:], 0.0), (eps_sb[:], EPS), (ones[:], 1.0), (q[:, :, :, 0:1], 0.0), (mem_last[:], 0.0),
                 (xpad[:, :, :, 0:TAPS - 1], 0.0), (members[:], 1.0)]
        ALL_FILLED = len(fills) + 3 + HB
        SUMS = KINDS * M
        TAP_STEPS = (TAPS - 1) * KD
        MEM_STEPS = 4

        def at(c, b):
            return c * B + b

        def neighbours(c, b):
            ahead = (c, 1) if b == 0 else (c + 1, 0)
            back = (c - 1, 1) if b == 0 else (c, 0)
            return ahead, (c, b), back, (c - 1, b)

        def run_steps(engine, step):
            step(-1, 0, True, False, False, False, False)
            step(-1, 1, True, True, False, False, False)
            step(0, 0, True, True, True, False, False)
            step(0, 1, True, True, True, True, False)
            with engine.Fori(1, Q - 1) as c:
                for b in range(B):
                    step(c, b, True, True, True, True, True)
            step(Q - 1, 0, False, True, True, True, True)
            step(Q - 1, 1, False, False, True, True, True)
            step(Q, 0, False, False, False, True, True)
            step(Q, 1, False, False, False, False, True)

        def later(c):
            return not isinstance(c, int) or c > 0

        block = stack.enter_context(nc.Block())

        @block.sync
        def _(sp):
            def load_tokens(src, dst, tile, sem):
                sp.dma_start(dst, src.rearrange("(i p) d -> p i d", p=P)[:, bass.ds(tile, G), :]).then_inc(sem, 16)

            def load_table(k, first):
                dst, src = ((cos_sb, cos_t), (decay_sb, decay_t), (undo_sb, undo_t))[k]
                sp.dma_start(dst[:], src.rearrange("m p t -> p m t")[:, :, bass.ds(first, CH)]).then_inc(tab_in, 16)

            def step(c, b, join, ahead, here, back, last):
                if not here:
                    if join:
                        load_tokens(x1, xt[:, b, :, :], b * (T // P), x_in[b])
                    if join and not ahead:
                        sp.wait_ge(now_ready, 1)
                        for dst, src in loads:
                            sp.dma_start(dst, src, allow_slow_non_contiguous=True).then_inc(consts_in, 16)
                    if join and ahead:
                        for k in range(3):
                            load_table(k, 0)
                    return
                n = held(sp, at(c, b))
                time = held(sp, c * CH)
                tile = held(sp, c * G + b * (T // P))
                gone = held(sp, c * 16)
                kept = held(sp, c * 16 + 16)
                if join:
                    after = held(sp, (c + 1) * G + b * (T // P))
                    done = held(sp, at(c, b) * KD + KD)
                    sp.wait_ge(turned, done)
                    sp.wait_ge(x2_stored[b], kept)
                    load_tokens(x1, xt[:, b, :, :], after, x_in[b])
                if b == 0 and later(c):
                    for k, used in enumerate((phase_ready, gated, undo_ready)):
                        sp.wait_ge(used, n)
                        load_table(k, time)
                if later(c):
                    sp.wait_ge(stored[b], gone)
                sp.wait_ge(x2_stored[b], kept)
                load_tokens(x2, res[:, b, :, :], tile, res_in[b])

            run_steps(sp, step)

        @block.gpsimd
        def _(pool):
            for k, (dst, value) in enumerate(fills):
                nc.gpsimd.memset(dst, value).then_inc(filled, 1)
                pool.wait_ge(filled, k + 1)
            nc.gpsimd.affine_select(out=ident[:], in_=ident[:], compare_op=ALU.not_equal, fill=1.0, base=0,
                                    pattern=[[-1, P]], channel_multiplier=1).then_inc(filled, 1)
            nc.gpsimd.affine_select(out=members[:], in_=members[:], compare_op=ALU.is_ge, fill=0.0, base=0,
                                    pattern=[[1, E]], channel_multiplier=-HEAD).then_inc(filled, 1)
            pool.wait_ge(filled, len(fills) + 2)
            nc.gpsimd.affine_select(out=members[:], in_=members[:], compare_op=ALU.is_ge, fill=0.0, base=HEAD - 1,
                                    pattern=[[-1, E]], channel_multiplier=HEAD).then_inc(filled, 1)
            for h in range(HB):
                nc.gpsimd.memset(heads[h * HEAD:(h + 1) * HEAD, h:h + 1], 1.0).then_inc(filled, 1)
                pool.wait_ge(filled, len(fills) + 4 + h)
            nc.gpsimd.tensor_scalar(inside[:], slots[:], float(last_slot), None, ALU.min).then_inc(inside_ready, 1)
            pool.wait_ge(inside_ready, 1)

            def step(c, b, join, ahead, here, back, last):
                if back:
                    sum_up(c, b, here)
                if join:
                    gather(c + 1, b)

            def gather(c, b):
                n = at(c, b)
                if later(c):
                    pool.wait_ge(joined, n - 1)
                nc.gpsimd.tensor_copy(inside_now[:, b, :], inside[:, bass.ds(b * (T // P) + c * G, G)]).then_inc(now_ready, 1)
                pool.wait_ge(now_ready, n + 1)
                nc.gpsimd.tensor_tensor(spare_p[:], eps_sb[:], eps_sb[:], ALU.add)
                for j in range(G):
                    nc.gpsimd.indirect_dma_start(y[:, b, j, :], None, eo[:],
                                                 bass.IndirectOffsetOnAxis(ap=inside_now[:, b, j:j + 1], axis=0)).then_inc(gathered[b], 16)

            def sum_up(c, b, here):
                c1, b1 = neighbours(c, b)[2]
                n = at(c1, b1)
                pool.wait_ge(q_ready, M * (n + 1))
                pool.wait_ge(tab_in, c1 * 48 + 48)
                if later(c1):
                    pool.wait_ge(o_in_ready, n - 1)
                nc.gpsimd.tensor_tensor(mem[:, b1, :, :], cos_sb[:], q[:, b1, :, 0:CH], ALU.add).then_inc(phase_ready, 1)
                if here:
                    pool.wait_ge(proj_taken, SUMS * (n + 1))
                    nc.gpsimd.tensor_tensor(gate[:, b1, :, :], gate[:, b1, :, :], decay_sb[:], ALU.mult).then_inc(gated, 1)
                if later(c1):
                    pool.wait_ge(o_full, n - 1)
                nc.gpsimd.tensor_tensor(o_in[:, b1, :, :], undo_sb[:], q[:, b1, :, 1:CH + 1], ALU.mult).then_inc(undo_ready, 1)
                pool.wait_ge(consts_in, ALL_IN)
                pool.wait_ge(res_in[b1], c1 * 16 + 16)
                nc.gpsimd.tensor_tensor(res[:, b1, :, :], res[:, b1, :, :], lnb_sb[:].unsqueeze(1).broadcast_to([P, G, D]), ALU.add).then_inc(res_biased, 1)

            run_steps(pool, step)

        @block.scalar
        def _(act):
            act.wait_ge(filled, ALL_FILLED)

            def step(c, b, join, ahead, here, back, last):
                (c0, b0), _, _, (c2, b2) = neighbours(c, b)

                def take_turned(k):
                    n = at(c0, b0)
                    act.wait_ge(turned, KD * n + (k + 1))
                    if later(c0):
                        act.wait_ge(xpad_free, n - 1)
                    nc.scalar.activation(xpad[:, b0, k, TAPS - 1:], t_ps[:], ACT.Copy).then_inc(xpad_ready, 1)

                def take(kind, m):
                    n = at(c, b)
                    i = kind * M + m
                    bank = proj[:, i % PROJ_RING, :]
                    act.wait_ge(proj_full, SUMS * n + (i + 1))
                    if kind == 0:
                        nc.scalar.activation(qk[:, b, m, :], bank, ACT.Copy)
                        ins = nc.scalar.activation(square[:, m, :], bank, ACT.Square)
                    elif kind == 1:
                        ins = nc.scalar.activation(val[:, b, m, :], bank, ACT.Copy)
                    else:
                        ins = nc.scalar.activation(gate[:, b, m, :], bank, ACT.Sigmoid, bias=gb_sb[:, m:m + 1])
                    ins.then_inc(proj_taken, 1)

                def root(r):
                    n = at(c2, b2)
                    act.wait_ge(var_ready, 2 * n + (r + 1))
                    nc.scalar.activation(rstd[:, r, :], mv[:, r, :, 1], ACT.Sqrt, bias=eps_sb[:]).then_inc(std_ready, 1)

                if ahead:
                    take_turned(0)
                if here:
                    n = at(c, b)
                    if later(c):
                        act.wait_ge(o_in_ready, n - 1)
                    if not isinstance(n, int) or n > 0:
                        act.wait_ge(n_full, n)
                    if isinstance(n, int) and n == 0:
                        act.wait_ge(consts_in, ALL_IN)
                    take(0, 0)
                    take(0, 1)
                if last:
                    root(0)
                if here:
                    take(0, 2)
                if ahead:
                    take_turned(1)
                if here:
                    take(0, 3)
                    take(1, 0)
                if last:
                    root(1)
                if here:
                    take(1, 1)
                    take(1, 2)
                    take(1, 3)
                    n = at(c, b)
                    act.wait_ge(n_full, n + 1)
                    if not isinstance(n, int) or n > 0:
                        act.wait_ge(inv_turned, n)
                    nc.scalar.activation(norm[:], n_ps[:], ACT.Sqrt).then_inc(norm_ready, 1)
                    for m in range(M):
                        take(2, m)
                if join:
                    nj = at(c + 1, b)
                    act.wait_ge(x_var_ready, nj + 1)
                    nc.scalar.activation(rstd_x[:], mv_x[:, :, 1], ACT.Sqrt, bias=eps_sb[:]).then_inc(x_std_ready, 1)
                if here:
                    act.wait_ge(inv_turned, n + 1)
                    if not isinstance(n, int) or n > 0:
                        act.wait_ge(r_full, M * n)
                    nc.scalar.activation(inv_t[:], t_ps[0:HEADS, :], ACT.Copy).then_inc(inv_ready, 1)
                if join:
                    act.wait_ge(x_made, nj + 1)
                    act.dma_start(x2.rearrange("(i p) d -> p i d", p=P)[:, bass.ds(b * (T // P) + (c + 1) * G, G), :], xt[:, b, :, :]).then_inc(x2_stored[b], 16)
                if last:
                    act.wait_ge(normed, at(c2, b2) + 1)
                    act.dma_start(x3.rearrange("(i p) d -> p i d", p=P)[:, bass.ds(b2 * (T // P) + c2 * G, G), :], res[:, b2, :, :]).then_inc(stored[b2], 16)

            run_steps(act, step)
            for b in range(B):
                act.wait_ge(stored[b], 16 * Q)

        @block.tensor
        def _(pe):
            pe.wait_ge(filled, ALL_FILLED)

            def step(c, b, join, ahead, here, back, last):
                (c0, b0), _, (c1, b1), _ = neighbours(c, b)

                def turn(k):
                    n = at(c0, b0)
                    pe.wait_ge(x_made, n + 1)
                    if k:
                        pe.wait_ge(xpad_ready, KD * n + k)
                    elif not isinstance(n, int) or n > 0:
                        if here and (not isinstance(at(c, b), int) or at(c, b) > 0):
                            pe.wait_ge(inv_ready, at(c, b))
                        else:
                            pe.wait_ge(xpad_ready, KD * n)
                    for j in range(G):
                        ins = nc.tensor.transpose(t_ps[:, j * P:(j + 1) * P], xt[:, b0, j, k * P:(k + 1) * P], ident[:])
                    ins.then_inc(turned, 1)

                def project(kind, m):
                    n = at(c, b)
                    i = kind * M + m
                    if i >= PROJ_RING or not isinstance(n, int) or n > 0:
                        pe.wait_ge(proj_taken, SUMS * n + (i + 1 - PROJ_RING))
                    w = (qk_sb, v_sb, g_sb)[kind]
                    for k in range(KD):
                        ins = nc.tensor.matmul(proj[:, i % PROJ_RING, :], w[:, k, m * P:(m + 1) * P], xc[:, b, k, :], start=(k == 0), stop=(k == KD - 1))
                    ins.then_inc(proj_full, 1)

                def turn_inverse():
                    n = at(c, b)
                    pe.wait_ge(inv_step, 2 * n + 2)
                    if ahead:
                        pe.wait_ge(xpad_ready, KD * (at(c0, b0) + 1))
                    for j in range(G):
                        ins = nc.tensor.transpose(t_ps[0:HEADS, j * P:(j + 1) * P], norm[:, j * HEADS:(j + 1) * HEADS], ident[:])
                    ins.then_inc(inv_turned, 1)

                def spread(m):
                    n = at(c, b)
                    pe.wait_ge(inv_ready, n + 1)
                    if m >= R_RING or not isinstance(n, int) or n > 0:
                        pe.wait_ge(q_ready, M * n + (m + 1 - R_RING))
                    nc.tensor.matmul(r_ps[:, m % R_RING, :], members[:, m * P:(m + 1) * P], inv_t[:], start=True, stop=True).then_inc(r_full, 1)

                if ahead:
                    turn(0)
                if here:
                    pe.wait_ge(consts_in, ALL_IN)
                    pe.wait_ge(xc_ready, KD * (at(c, b) + 1))
                    for m in range(M - 1):
                        project(0, m)
                if ahead:
                    turn(1)
                if here:
                    project(0, M - 1)
                    for m in range(M):
                        project(1, m)
                    n = at(c, b)
                    pe.wait_ge(proj_taken, SUMS * n + M)
                    if not isinstance(n, int) or n > 0:
                        pe.wait_ge(norm_ready, n)
                    for j in range(G):
                        for m in range(M):
                            first = j * HEADS + m * HB
                            ins = nc.tensor.matmul(n_ps[:, first:first + HB], square[:, m, j * P:(j + 1) * P], heads[:], start=True, stop=True)
                    ins.then_inc(n_full, 1)
                    for m in range(M):
                        project(2, m)
                    turn_inverse()
                if back:
                    n = at(c1, b1)
                    pe.wait_ge(o_in_ready, n + 1)
                    if not isinstance(n, int) or n > 0:
                        pe.wait_ge(o_taken, n)
                    for j in range(G):
                        for m in range(M):
                            ins = nc.tensor.matmul(o_ps[:, j, :], o_in[:, b1, m, j * P:(j + 1) * P], o_sb[:, m, :], start=(m == 0), stop=(m == M - 1))
                    ins.then_inc(o_full, 1)
                if here:
                    for m in range(M):
                        spread(m)

            run_steps(pe, step)

        @block.vector
        def _(dve):
            dve.wait_ge(filled, ALL_FILLED)
            v = nc.vector

            def step(c, b, join, ahead, here, back, last):
                (c0, b0), _, (c1, b1), (c2, b2) = neighbours(c, b)

                def tap(t):
                    n = at(c0, b0)
                    for k in range(KD):
                        src = xpad[:, b0, k, t:t + CH]
                        dst = xc[:, b0, k, :]
                        if t == 0:
                            dve.wait_ge(consts_in, ALL_IN)
                            dve.wait_ge(xpad_ready, KD * n + (k + 1))
                            if later(c0):
                                dve.wait_ge(proj_full, SUMS * (n - 1))
                            ins = v.tensor_scalar(dst, src, cw_sb[:, k, 0:1], cb_sb[:, k:k + 1], ALU.mult, ALU.add)
                        else:
                            dve.wait_ge(conv_step, TAP_STEPS * n + ((t - 1) * KD + k + 1))
                            ins = v.scalar_tensor_tensor(out=dst, in0=src, scalar=cw_sb[:, k, t:t + 1], in1=dst, op0=ALU.mult, op1=ALU.add)
                        ins.then_inc(xc_ready if t == TAPS - 1 else conv_step, 1)

                def keep_history():
                    dve.wait_ge(xc_ready, KD * (at(c0, b0) + 1))
                    v.tensor_copy(xpad[:, b0, :, 0:TAPS - 1], xpad[:, b0, :, CH:CH + TAPS - 1]).then_inc(xpad_free, 1)

                def statistics(rows, r):
                    n = at(c2, b2)
                    for j in range(G):
                        ins = v.bn_stats(stats[:, j, :], rows[:, j, :])
                    ins.then_inc(stat_step, 1)
                    dve.wait_ge(stat_step, 2 * n + (r + 1))
                    v.memset(spare[:], 0.0)
                    for j in range(G):
                        ins = v.bn_aggr(mv[:, r, j, :], stats[:, j, :])
                    ins.then_inc(var_ready, 1)

                def invert_root(r):
                    n = at(c2, b2)
                    dve.wait_ge(std_ready, 2 * n + (r + 1))
                    v.reciprocal(rstd[:, r, :], rstd[:, r, :]).then_inc(rstd_ready, 1)
                    dve.wait_ge(rstd_ready, 2 * n + (r + 1))

                if last:
                    n = at(c2, b2)
                    rows = res[:, b2, :, :]
                    dve.wait_ge(o_full, n + 1)
                    statistics(o_ps, 0)
                    dve.wait_ge(var_ready, 2 * n + 1)
                    for j in range(G):
                        ins = v.scalar_tensor_tensor(out=z[:, j, :], in0=o_ps[:, j, :], scalar=mv[:, 0, j, 0:1], in1=lng_sb[:], op0=ALU.subtract, op1=ALU.mult)
                    ins.then_inc(o_taken, 1)
                if ahead:
                    tap(0)
                    tap(1)
                if last:
                    invert_root(0)
                    dve.wait_ge(o_taken, n + 1)
                    dve.wait_ge(res_biased, n + 1)
                    for j in range(G):
                        ins = v.scalar_tensor_tensor(out=rows[:, j, :], in0=z[:, j, :], scalar=rstd[:, 0, j:j + 1], in1=rows[:, j, :], op0=ALU.mult, op1=ALU.add)
                    ins.then_inc(z_step, 1)
                    dve.wait_ge(z_step, n + 1)
                    statistics(rows, 1)
                if ahead:
                    tap(2)
                    tap(3)
                    keep_history()
                if back:
                    n1 = at(c1, b1)
                    rows1 = mem[:, b1, :, :]
                    if not here:
                        dve.wait_ge(tab_in, c1 * 48 + 48)
                        dve.wait_ge(proj_taken, SUMS * (n1 + 1))
                        v.tensor_tensor(gate[:, b1, :, :], gate[:, b1, :, :], decay_sb[:], ALU.mult).then_inc(gated, 1)
                    dve.wait_ge(phase_ready, n1 + 1)
                    v.tensor_tensor(rows1, rows1, val[:, b1, :, :], ALU.mult).then_inc(mem_step, 1)
                    dve.wait_ge(mem_step, MEM_STEPS * n1 + 1)
                    dve.wait_ge(gated, n1 + 1)
                    v.tensor_tensor(rows1, rows1, gate[:, b1, :, :], ALU.mult).then_inc(mem_step, 1)
                if last:
                    invert_root(1)
                    for j in range(G):
                        ins = v.tensor_scalar(rows[:, j, :], rows[:, j, :], mv[:, 1, j, 0:1], rstd[:, 1, j:j + 1], ALU.subtract, ALU.mult)
                    ins.then_inc(normed, 1)
                if here:
                    n3 = at(c, b)
                    dve.wait_ge(norm_ready, n3 + 1)
                    v.tensor_scalar(norm[:], norm[:], 1e-12, None, ALU.max).then_inc(inv_step, 1)
                    dve.wait_ge(inv_step, 2 * n3 + 1)
                    v.reciprocal(norm[:], norm[:]).then_inc(inv_step, 1)
                if back:
                    dve.wait_ge(mem_step, MEM_STEPS * n1 + 2)
                    for m in range(M):
                        ins = v.tensor_tensor_scan(mem[:, b1, m, :], ones[:], mem[:, b1, m, :], mem_last[:, b1, m:m + 1], ALU.mult, ALU.add)
                    ins.then_inc(mem_step, 1)
                    dve.wait_ge(mem_step, MEM_STEPS * n1 + 3)
                    v.tensor_copy(mem_last[:, b1, :], mem[:, b1, :, CH - 1]).then_inc(mem_step, 1)
                    dve.wait_ge(undo_ready, n1 + 1)
                    v.tensor_tensor(o_in[:, b1, :, :], rows1, o_in[:, b1, :, :], ALU.mult).then_inc(o_in_ready, 1)
                if join:
                    nj = at(c + 1, b)
                    xrows = xt[:, b, :, :]
                    dve.wait_ge(x_in[b], c * 16 + 32)
                    dve.wait_ge(gathered[b], c * (16 * G) + 32 * G)
                    for j in range(G):
                        ins = v.scalar_tensor_tensor(out=xrows[:, j, :], in0=y[:, b, j, :], scalar=weight[:, bass.ds(b * (T // P) + (c + 1) * G + j, 1)],
                                                     in1=xrows[:, j, :], op0=ALU.mult, op1=ALU.add)
                    ins.then_inc(joined, 1)
                    dve.wait_ge(joined, nj + 1)
                    layernorm_stats(nc, dve, xrows, stats, mv_x, spare, G, nj + 1, x_stat_step, x_var_ready)
                    layernorm_apply(nc, dve, xrows, xrows, mv_x, rstd_x, G, nj + 1, x_std_ready, x_rstd_ready, x_made)
                if here:
                    if later(c):
                        dve.wait_ge(undo_ready, n3 - 1)
                        v.tensor_copy(q[:, b, :, 0:1], q[:, b, :, CH:CH + 1]).then_inc(q_kept, 1)
                        dve.wait_ge(q_kept, n3 - 1)
                    for m in range(M):
                        dve.wait_ge(r_full, M * n3 + (m + 1))
                        v.tensor_tensor(q[:, b, m, 1:CH + 1], qk[:, b, m, :], r_ps[:, m % R_RING, :], ALU.mult).then_inc(q_ready, 1)

            run_steps(dve, step)


def program(nc, a, out):
    x1, x2, x3 = (nc.dram_tensor(name, [N, D], F32) for name in ("x1", "x2", "x3"))
    state_space_layer(nc, a["x_tok"], a["x_feat"], a["L0_attn_Win"], a["L0_attn_b_in"], a["L0_attn_A_log"],
                      a["L0_attn_B_param"], a["L0_attn_C_param"], a["L0_attn_Wdt"], a["L0_attn_b_dt"],
                      a["L0_attn_Wconv"], a["L0_attn_Wout"], a["L0_attn_b_out"], x1)
    capacity = max(-(-3 * N // (2 * EXPERTS)), 1)
    H, HD = a["L1_attn_freqs"].shape
    cos_t, decay_t, undo_t = (nc.dram_tensor(name, [H * HD // P, P, T], F32) for name in ("cos_t", "decay_t", "undo_t"))
    tables = RetentionTables(a["L1_attn_freqs"], a["L1_attn_gamma"], cos_t, decay_t, undo_t)
    eo = nc.dram_tensor("eo", [EXPERTS * capacity, D], F32)
    with ExitStack() as stack:
        s = Scope(nc, stack, "moe")
        slots = s.sbuf("slots", [P, TOKEN_TILES], I32)
        weight = s.sbuf("weight", [P, TOKEN_TILES])
        ids = s.sbuf("ids", [P, EXPERTS * capacity // P], I32)
        route(nc, "route", x1, a["L0_ffn_router_w"], None, ids, slots, weight, capacity)
        capacity_experts(nc, x1, ids, a["L0_ffn_w1"], a["L0_ffn_b1"], a["L0_ffn_w2"], a["L0_ffn_b2"], eo, capacity,
                         tables)
        retention_layer(nc, x1, eo, slots, weight, EXPERTS * capacity - 1, x2, a["L1_attn_conv_w"], a["L1_attn_conv_b"],
                        a["L1_attn_qk_w"], a["L1_attn_v_w"], a["L1_attn_g_w"], a["L1_attn_g_b"], a["L1_attn_o_w"],
                        a["L1_attn_ln_g"], a["L1_attn_ln_b"], cos_t, decay_t, undo_t, x3)
    eo2 = nc.dram_tensor("eo2", [P * SLOT_TILES, D], F32)
    with ExitStack() as stack:
        s = Scope(nc, stack, "moe2")
        slots = s.sbuf("slots", [P, TOKEN_TILES], I32)
        weight = s.sbuf("weight", [P, TOKEN_TILES])
        ids = s.sbuf("ids", [P, SLOT_TILES], I32)
        tile_expert = s.sbuf("tile_expert", [1, SLOT_TILES], I32)
        route(nc, "route2", x3, a["L1_ffn_router_w"], a["L1_ffn_router_b"], ids, slots, weight, None, tile_expert)
        sorted_experts(nc, x3, ids, tile_expert, a["L1_ffn_expert_w"], a["L1_ffn_expert_b"], eo2)
        combine(nc, "comb2", x3, eo2, slots, weight, out, P * SLOT_TILES - 1)


TRANSPOSED = ["L0_attn_Win", "L0_attn_Wdt", "L0_attn_Wout", "L0_ffn_router_w", "L1_attn_qk_w", "L1_attn_v_w",
              "L1_attn_g_w", "L1_attn_o_w", "L1_ffn_router_w"]


def kernel(**inputs):
    import numpy as np
    import concourse.bacc as bacc
    from concourse.bass_utils import run_bass_kernel_spmd

    arrays = {}
    for name, value in inputs.items():
        value = np.asarray(value)
        if name == "L0_attn_input":
            tokens = value.reshape(N, D)
            arrays["x_tok"] = np.ascontiguousarray(tokens)
            arrays["x_feat"] = np.ascontiguousarray(tokens.T)
        elif name in TRANSPOSED:
            arrays[name] = np.ascontiguousarray(value.T)
        elif name == "L1_ffn_expert_w":
            arrays[name] = np.ascontiguousarray(value.transpose(0, 2, 1))
        else:
            arrays[name] = np.ascontiguousarray(value)
    nc = bacc.Bacc("TRN2", target_bir_lowering=False, num_devices=1)
    a = {n: nc.dram_tensor(f"in_{n}", v.shape, mybir.dt.from_np(v.dtype), kind="ExternalInput").ap() for n, v in arrays.items()}
    out = nc.dram_tensor("out", (N, D), F32, kind="ExternalOutput").ap()
    program(nc, a, out)
    r = run_bass_kernel_spmd(nc, [{f"in_{n}": v for n, v in arrays.items()}], core_ids=[0])
    return r.results[0]["out"].reshape(B, T, D)
```
